# Optimizing a Trainium2 kernel written in Bass

```python
import numpy as np
import jax
import jax.numpy as jnp

def _softmax(x, axis=-1):
    return jax.nn.softmax(x, axis=axis)

def _gelu(x):
    return jax.nn.gelu(x, approximate=True)

def _silu(x):
    return jax.nn.silu(x)

def _sigmoid(x):
    return jax.nn.sigmoid(x)

def _layernorm(x, axis=-1, eps=1e-05):
    m = jnp.mean(x, axis=axis, keepdims=True)
    v = jnp.var(x, axis=axis, keepdims=True)
    return (x - m) / jnp.sqrt(v + eps)

def _scatter_add(tgt, idx, src, axis=0):
    return tgt.at[idx].add(src)

def _segment_sum(src, seg, n):
    return jax.ops.segment_sum(src, seg, n)
kernel_name = 'mk_seq_preln_d2_jaxref_r8_0619c0'

def setup_inputs(seed: int=0):
    np.random.seed(seed)
    _w = jnp.asarray

    def _L0_attn_setup():
        import jax, jax.numpy as jnp
        import numpy as np
        EPS = 1e-06

        def _phi(x):
            return jax.nn.elu(x) + 1.0

        def chunked_causal_linear_attention(q, k, v, chunk=128):
            B, H, N, D = q.shape
            qp, kp = (_phi(q), _phi(k))
            NC = N // chunk

            def to_chunks(t):
                return t.reshape(B, H, NC, chunk, D).transpose(2, 0, 1, 3, 4)
            qs, ks, vs = (to_chunks(qp), to_chunks(kp), to_chunks(v))

            def step(carry, inp):
                s_kv, s_k = carry
                qc, kc, vc = inp
                kv_c = jnp.einsum('bhcd,bhce->bhcde', kc, vc)
                kv_scan = jnp.cumsum(kv_c, axis=2)
                out = jnp.einsum('bhcd,bhde->bhce', qc, s_kv) + jnp.einsum('bhcd,bhcde->bhce', qc, kv_scan)
                norm = jnp.sum(qc * s_k[:, :, None, :], axis=-1, keepdims=True) + jnp.sum(qc * jnp.cumsum(kc, axis=2), axis=-1, keepdims=True)
                out = out / jnp.maximum(norm, EPS)
                return ((s_kv + kv_c.sum(axis=2), s_k + kc.sum(axis=2)), out)
            init = (jnp.zeros((B, H, D, D), q.dtype), jnp.zeros((B, H, D), q.dtype))
            _, outs = jax.lax.scan(step, init, (qs, ks, vs))
            return outs.transpose(1, 2, 0, 3, 4).reshape(B, H, N, D)

        def causal_block_mean(x, block):
            B, H, N, D = x.shape
            prefix = jnp.cumsum(x, axis=2)
            idx = jnp.arange(N)
            start = idx // block * block
            prev_idx = jnp.clip(start - 1, 0, None)
            prev = prefix[:, :, prev_idx, :]
            prev = jnp.where((start > 0)[None, None, :, None], prev, 0.0)
            sums = prefix - prev
            lengths = (idx - start + 1).astype(x.dtype)[None, None, :, None]
            return sums / lengths

        def local_attention(q, k, v, window):
            B, H, N, D = q.shape
            scale = 1.0 / np.sqrt(D)
            scores = jnp.einsum('bhqd,bhkd->bhqk', q, k) * scale
            rows = jnp.arange(N)[:, None]
            cols = jnp.arange(N)[None, :]
            mask = (cols <= rows) & (cols > rows - window)
            scores = jnp.where(mask[None, None], scores, -1e+30)
            probs = jax.nn.softmax(scores, axis=-1)
            return jnp.einsum('bhqk,bhkd->bhqd', probs, v)

        def hale_forward(x, Wq, Wk, Wv, Wkl, Wvl, haar_Wk, haar_Wv, haar_scale, Wg, bg, Wgo, bgo, Wo, bo, num_heads=16, local_window=64, chunk_size=128):
            B, N, Dm = x.shape
            Dh = Dm // num_heads

            def heads(t):
                return t.reshape(B, N, num_heads, Dh).transpose(0, 2, 1, 3)

            def merge(t):
                return t.transpose(0, 2, 1, 3).reshape(B, N, Dm)
            q = heads(x @ Wq.T)
            k = heads(x @ Wk.T)
            v = heads(x @ Wv.T)
            k_loc = heads(x @ Wkl.T)
            v_loc = heads(x @ Wvl.T)
            local_out = local_attention(q, k_loc, v_loc, min(local_window, N))
            glob = chunked_causal_linear_attention(q, k, v, chunk=chunk_size)
            scale_w = jax.nn.softmax(haar_scale)
            num_levels = haar_scale.shape[0]
            for lvl in range(num_levels):
                block = 2 ** (lvl + 1)
                k_lvl = causal_block_mean(k, block) @ haar_Wk[lvl].T
                v_lvl = causal_block_mean(v, block) @ haar_Wv[lvl].T
                glob = glob + scale_w[lvl] * chunked_causal_linear_attention(q, k_lvl, v_lvl, chunk=chunk_size)
            local_m = merge(local_out)
            glob_m = merge(glob)
            diff = local_m - glob_m
            gate_h = jax.nn.silu(jnp.concatenate([x, diff], axis=-1) @ Wg.T + bg)
            alpha = jax.nn.sigmoid(gate_h @ Wgo.T + bgo)
            mixed = alpha * local_m + (1.0 - alpha) * glob_m
            return mixed @ Wo.T + bo
        key = jax.random.key(seed)
        B, N, Dm, H, L = (1, 256, 128, 16, 4)
        Dh = Dm // H
        ks = jax.random.split(key, 16)
        s_dm = 1.0 / np.sqrt(Dm)
        s_dh = 1.0 / np.sqrt(Dh)
        return {'x': jax.random.normal(ks[0], (B, N, Dm), jnp.float32), 'Wq': jax.random.normal(ks[1], (Dm, Dm), jnp.float32) * s_dm, 'Wk': jax.random.normal(ks[2], (Dm, Dm), jnp.float32) * s_dm, 'Wv': jax.random.normal(ks[3], (Dm, Dm), jnp.float32) * s_dm, 'Wkl': jax.random.normal(ks[4], (Dm, Dm), jnp.float32) * s_dm, 'Wvl': jax.random.normal(ks[5], (Dm, Dm), jnp.float32) * s_dm, 'haar_Wk': jax.random.normal(ks[6], (L, Dh, Dh), jnp.float32) * s_dh, 'haar_Wv': jax.random.normal(ks[7], (L, Dh, Dh), jnp.float32) * s_dh, 'haar_scale': jax.random.normal(ks[8], (L,), jnp.float32) * 0.1, 'Wg': jax.random.normal(ks[9], (Dm, 2 * Dm), jnp.float32) * (1.0 / np.sqrt(2 * Dm)), 'bg': jnp.zeros((Dm,), jnp.float32), 'Wgo': jax.random.normal(ks[10], (1, Dm), jnp.float32) * s_dm, 'bgo': jnp.zeros((1,), jnp.float32), 'Wo': jax.random.normal(ks[11], (Dm, Dm), jnp.float32) * s_dm, 'bo': jnp.zeros((Dm,), jnp.float32)}
    _L0_attn_in = _L0_attn_setup()

    def _L0_ffn_setup():
        import jax, jax.numpy as jnp
        import numpy as np
        E, H, I = (8, 128, 64)
        NG, TKG, TOPK = (4, 2, 4)
        SCALE = 2.5

        def _mlp(x, wg, wu, wd):
            return jax.nn.silu(x @ wg) * (x @ wu) @ wd
        key = jax.random.key(seed)
        ks = jax.random.split(key, 8)
        s = 0.02
        return {'hidden_states': jax.random.normal(ks[0], (32, 32, H), jnp.float32), 'gate_w': jax.random.normal(ks[1], (E, H), jnp.float32) * np.float32(np.sqrt(2.0 / H)), 'correction_bias': jnp.zeros((E,), jnp.float32), 'Wg': jax.random.normal(ks[2], (E, H, I), jnp.float32) * s, 'Wu': jax.random.normal(ks[3], (E, H, I), jnp.float32) * s, 'Wd': jax.random.normal(ks[4], (E, I, H), jnp.float32) * s, 'Wg_s': jax.random.normal(ks[5], (H, I), jnp.float32) * s, 'Wu_s': jax.random.normal(ks[6], (H, I), jnp.float32) * s, 'Wd_s': jax.random.normal(ks[7], (I, H), jnp.float32) * s}
    _L0_ffn_in = _L0_ffn_setup()

    def _L1_attn_setup():
        import jax, jax.numpy as jnp
        import numpy as np
        D_MODEL = 128
        NUM_HEADS = 16
        HEAD_DIM = D_MODEL // NUM_HEADS
        CHUNK = 64
        B, T = (4, 512)

        def l2norm(x, eps=1e-06):
            return x * jax.lax.rsqrt(jnp.sum(x * x, axis=-1, keepdims=True) + eps)

        def _forward(x, Wq, Wk, Wv, Wg, Wo, Wb, Wa, dt_bias, A_log, norm_w):
            Bb, Tt, D = x.shape
            H, K, C = (NUM_HEADS, HEAD_DIM, CHUNK)
            n = Tt // C
            q = l2norm((x @ Wq).reshape(Bb, Tt, H, K)) / np.sqrt(K)
            k = l2norm((x @ Wk).reshape(Bb, Tt, H, K))
            v = (x @ Wv).reshape(Bb, Tt, H, K)
            gate = (x @ Wg).reshape(Bb, Tt, H, K)
            beta = jax.nn.sigmoid(x @ Wb)
            decay = -jnp.exp(A_log)[None, None, :] * jax.nn.softplus(x @ Wa + dt_bias)
            q = jnp.transpose(q, (0, 2, 1, 3)).astype(jnp.float32)
            k = jnp.transpose(k, (0, 2, 1, 3)).astype(jnp.float32)
            v = jnp.transpose(v, (0, 2, 1, 3)).astype(jnp.float32)
            beta_h = jnp.transpose(beta, (0, 2, 1))[..., None]
            v = v * beta_h
            k_beta = k * beta_h
            q = q.reshape(Bb, H, n, C, K)
            k = k.reshape(Bb, H, n, C, K)
            v = v.reshape(Bb, H, n, C, K)
            k_beta = k_beta.reshape(Bb, H, n, C, K)
            g = jnp.cumsum(jnp.transpose(decay, (0, 2, 1)).reshape(Bb, H, n, C), axis=-1)
            tril = jnp.tril(jnp.ones((C, C), bool))
            strict = jnp.tril(jnp.ones((C, C), bool), -1)
            diff = g[..., :, None] - g[..., None, :]
            L = jnp.where(tril, jnp.exp(jnp.where(tril, diff, 0.0)), 0.0)
            P = jnp.where(strict, jnp.einsum('bhncd,bhnmd->bhncm', k_beta, k) * L, 0.0)
            Ainv = jnp.eye(C, dtype=P.dtype) + P
            Pk = P
            for _ in range(int(np.ceil(np.log2(C))) - 1):
                Pk = Pk @ Pk
                Ainv = Ainv + Pk @ Ainv
            v = Ainv @ v
            k_cumdecay = Ainv @ (k_beta * jnp.exp(g)[..., None])

            def step(S, inp):
                q_i, k_i, v_i, kcd_i, g_i, L_i = inp
                attn = jnp.where(tril, jnp.einsum('bhck,bhmk->bhcm', q_i, k_i) * L_i, 0.0)
                v_new = v_i - kcd_i @ S
                o_i = q_i * jnp.exp(g_i)[..., None] @ S + attn @ v_new
                g_last = g_i[..., -1:]
                S_new = S * jnp.exp(g_last)[..., None] + jnp.einsum('bhck,bhcd->bhkd', k_i * jnp.exp(g_last - g_i)[..., None], v_new)
                return (S_new, o_i)
            to_scan = lambda a: jnp.moveaxis(a, 2, 0)
            S0 = jnp.zeros((Bb, H, K, K), jnp.float32)
            _, o = jax.lax.scan(step, S0, (to_scan(q), to_scan(k), to_scan(v), to_scan(k_cumdecay), to_scan(g), to_scan(L)))
            o = jnp.transpose(o, (1, 0, 3, 2, 4)).reshape(Bb, Tt, H, K)
            o = o * jax.lax.rsqrt(jnp.mean(o * o, axis=-1, keepdims=True) + 1e-05) * norm_w
            o = o * jax.nn.silu(gate)
            return o.reshape(Bb, Tt, D) @ Wo
        key = jax.random.key(seed)
        ks = jax.random.split(key, 10)
        s = 1.0 / np.sqrt(D_MODEL)
        inp = {'x': jax.random.normal(ks[0], (B, T, D_MODEL), jnp.float32), 'Wq': jax.random.normal(ks[1], (D_MODEL, D_MODEL), jnp.float32) * s, 'Wk': jax.random.normal(ks[2], (D_MODEL, D_MODEL), jnp.float32) * s, 'Wv': jax.random.normal(ks[3], (D_MODEL, D_MODEL), jnp.float32) * s, 'Wg': jax.random.normal(ks[4], (D_MODEL, D_MODEL), jnp.float32) * s, 'Wo': jax.random.normal(ks[5], (D_MODEL, D_MODEL), jnp.float32) * s, 'Wb': jax.random.normal(ks[6], (D_MODEL, NUM_HEADS), jnp.float32) * s, 'Wa': jax.random.normal(ks[7], (D_MODEL, NUM_HEADS), jnp.float32) * s, 'dt_bias': jnp.ones((NUM_HEADS,), jnp.float32), 'A_log': jnp.log(jax.random.uniform(ks[8], (NUM_HEADS,), jnp.float32, 0.001, 16.0)), 'norm_w': jnp.ones((HEAD_DIM,), jnp.float32)}
        return inp
    _L1_attn_in = _L1_attn_setup()

    def _L1_ffn_setup():
        import jax, jax.numpy as jnp
        import numpy as np
        DIM = 128

        def _reference_tuple_inner(x, W_r, W_k, W_v, mu_r, mu_k):
            B, T, C = x.shape
            x_prev = jnp.concatenate([jnp.zeros((B, 1, C), x.dtype), x[:, :-1, :]], axis=1)
            xr = mu_r * x + (1.0 - mu_r) * x_prev
            xk = mu_k * x + (1.0 - mu_k) * x_prev
            r = jax.nn.sigmoid(jnp.einsum('btc,dc->btd', xr, W_r))
            k = jnp.einsum('btc,dc->btd', xk, W_k)
            k_act = jnp.square(jax.nn.relu(k))
            out = r * jnp.einsum('btc,dc->btd', k_act, W_v)
            new_state = x[:, -1, :]
            return (out, new_state)
        key = jax.random.key(seed)
        ks = jax.random.split(key, 6)
        B, T, C = (8, 256, DIM)
        x = jax.random.normal(ks[0], (B, T, C), dtype=jnp.float32)
        s = 1.0 / np.sqrt(C)
        W_r = jax.random.uniform(ks[1], (C, C), jnp.float32, -s, s)
        W_k = jax.random.uniform(ks[2], (C, C), jnp.float32, -s, s)
        W_v = jax.random.uniform(ks[3], (C, C), jnp.float32, -s, s)
        mu_r = jax.random.uniform(ks[4], (C,), jnp.float32)
        mu_k = jax.random.uniform(ks[5], (C,), jnp.float32)
        return {'x': x, 'W_r': W_r, 'W_k': W_k, 'W_v': W_v, 'mu_r': mu_r, 'mu_k': mu_k}
    _L1_ffn_in = _L1_ffn_setup()
    _d = {'L0_attn_x': _L0_attn_in['x'], 'L0_attn_Wq': _L0_attn_in['Wq'], 'L0_attn_Wk': _L0_attn_in['Wk'], 'L0_attn_Wv': _L0_attn_in['Wv'], 'L0_attn_Wkl': _L0_attn_in['Wkl'], 'L0_attn_Wvl': _L0_attn_in['Wvl'], 'L0_attn_haar_Wk': _L0_attn_in['haar_Wk'], 'L0_attn_haar_Wv': _L0_attn_in['haar_Wv'], 'L0_attn_haar_scale': _L0_attn_in['haar_scale'], 'L0_attn_Wg': _L0_attn_in['Wg'], 'L0_attn_bg': _L0_attn_in['bg'], 'L0_attn_Wgo': _L0_attn_in['Wgo'], 'L0_attn_bgo': _L0_attn_in['bgo'], 'L0_attn_Wo': _L0_attn_in['Wo'], 'L0_attn_bo': _L0_attn_in['bo'], 'L0_ffn_gate_w': _L0_ffn_in['gate_w'], 'L0_ffn_correction_bias': _L0_ffn_in['correction_bias'], 'L0_ffn_Wg': _L0_ffn_in['Wg'], 'L0_ffn_Wu': _L0_ffn_in['Wu'], 'L0_ffn_Wd': _L0_ffn_in['Wd'], 'L0_ffn_Wg_s': _L0_ffn_in['Wg_s'], 'L0_ffn_Wu_s': _L0_ffn_in['Wu_s'], 'L0_ffn_Wd_s': _L0_ffn_in['Wd_s'], 'L1_attn_Wq': _L1_attn_in['Wq'], 'L1_attn_Wk': _L1_attn_in['Wk'], 'L1_attn_Wv': _L1_attn_in['Wv'], 'L1_attn_Wg': _L1_attn_in['Wg'], 'L1_attn_Wo': _L1_attn_in['Wo'], 'L1_attn_Wb': _L1_attn_in['Wb'], 'L1_attn_Wa': _L1_attn_in['Wa'], 'L1_attn_dt_bias': _L1_attn_in['dt_bias'], 'L1_attn_A_log': _L1_attn_in['A_log'], 'L1_attn_norm_w': _L1_attn_in['norm_w'], 'L1_ffn_W_r': _L1_ffn_in['W_r'], 'L1_ffn_W_k': _L1_ffn_in['W_k'], 'L1_ffn_W_v': _L1_ffn_in['W_v'], 'L1_ffn_mu_r': _L1_ffn_in['mu_r'], 'L1_ffn_mu_k': _L1_ffn_in['mu_k']}
    _x0 = _d['L0_attn_x']
    _d['L0_attn_x'] = jax.random.normal(jax.random.fold_in(jax.random.key(seed), 1), (2, 1024, 128), dtype=_x0.dtype)
    del _x0
    return _d

def reference(L0_attn_x, L0_attn_Wq, L0_attn_Wk, L0_attn_Wv, L0_attn_Wkl, L0_attn_Wvl, L0_attn_haar_Wk, L0_attn_haar_Wv, L0_attn_haar_scale, L0_attn_Wg, L0_attn_bg, L0_attn_Wgo, L0_attn_bgo, L0_attn_Wo, L0_attn_bo, L0_ffn_gate_w, L0_ffn_correction_bias, L0_ffn_Wg, L0_ffn_Wu, L0_ffn_Wd, L0_ffn_Wg_s, L0_ffn_Wu_s, L0_ffn_Wd_s, L1_attn_Wq, L1_attn_Wk, L1_attn_Wv, L1_attn_Wg, L1_attn_Wo, L1_attn_Wb, L1_attn_Wa, L1_attn_dt_bias, L1_attn_A_log, L1_attn_norm_w, L1_ffn_W_r, L1_ffn_W_k, L1_ffn_W_v, L1_ffn_mu_r, L1_ffn_mu_k):

    def _L0_attn_ref(x, Wq, Wk, Wv, Wkl, Wvl, haar_Wk, haar_Wv, haar_scale, Wg, bg, Wgo, bgo, Wo, bo):
        import jax, jax.numpy as jnp
        import numpy as np
        EPS = 1e-06

        def _phi(x):
            return jax.nn.elu(x) + 1.0

        def chunked_causal_linear_attention(q, k, v, chunk=128):
            B, H, N, D = q.shape
            qp, kp = (_phi(q), _phi(k))
            NC = N // chunk

            def to_chunks(t):
                return t.reshape(B, H, NC, chunk, D).transpose(2, 0, 1, 3, 4)
            qs, ks, vs = (to_chunks(qp), to_chunks(kp), to_chunks(v))

            def step(carry, inp):
                s_kv, s_k = carry
                qc, kc, vc = inp
                kv_c = jnp.einsum('bhcd,bhce->bhcde', kc, vc)
                kv_scan = jnp.cumsum(kv_c, axis=2)
                out = jnp.einsum('bhcd,bhde->bhce', qc, s_kv) + jnp.einsum('bhcd,bhcde->bhce', qc, kv_scan)
                norm = jnp.sum(qc * s_k[:, :, None, :], axis=-1, keepdims=True) + jnp.sum(qc * jnp.cumsum(kc, axis=2), axis=-1, keepdims=True)
                out = out / jnp.maximum(norm, EPS)
                return ((s_kv + kv_c.sum(axis=2), s_k + kc.sum(axis=2)), out)
            init = (jnp.zeros((B, H, D, D), q.dtype), jnp.zeros((B, H, D), q.dtype))
            _, outs = jax.lax.scan(step, init, (qs, ks, vs))
            return outs.transpose(1, 2, 0, 3, 4).reshape(B, H, N, D)

        def causal_block_mean(x, block):
            B, H, N, D = x.shape
            prefix = jnp.cumsum(x, axis=2)
            idx = jnp.arange(N)
            start = idx // block * block
            prev_idx = jnp.clip(start - 1, 0, None)
            prev = prefix[:, :, prev_idx, :]
            prev = jnp.where((start > 0)[None, None, :, None], prev, 0.0)
            sums = prefix - prev
            lengths = (idx - start + 1).astype(x.dtype)[None, None, :, None]
            return sums / lengths

        def local_attention(q, k, v, window):
            B, H, N, D = q.shape
            scale = 1.0 / np.sqrt(D)
            scores = jnp.einsum('bhqd,bhkd->bhqk', q, k) * scale
            rows = jnp.arange(N)[:, None]
            cols = jnp.arange(N)[None, :]
            mask = (cols <= rows) & (cols > rows - window)
            scores = jnp.where(mask[None, None], scores, -1e+30)
            probs = jax.nn.softmax(scores, axis=-1)
            return jnp.einsum('bhqk,bhkd->bhqd', probs, v)

        def hale_forward(x, Wq, Wk, Wv, Wkl, Wvl, haar_Wk, haar_Wv, haar_scale, Wg, bg, Wgo, bgo, Wo, bo, num_heads=16, local_window=64, chunk_size=128):
            B, N, Dm = x.shape
            Dh = Dm // num_heads

            def heads(t):
                return t.reshape(B, N, num_heads, Dh).transpose(0, 2, 1, 3)

            def merge(t):
                return t.transpose(0, 2, 1, 3).reshape(B, N, Dm)
            q = heads(x @ Wq.T)
            k = heads(x @ Wk.T)
            v = heads(x @ Wv.T)
            k_loc = heads(x @ Wkl.T)
            v_loc = heads(x @ Wvl.T)
            local_out = local_attention(q, k_loc, v_loc, min(local_window, N))
            glob = chunked_causal_linear_attention(q, k, v, chunk=chunk_size)
            scale_w = jax.nn.softmax(haar_scale)
            num_levels = haar_scale.shape[0]
            for lvl in range(num_levels):
                block = 2 ** (lvl + 1)
                k_lvl = causal_block_mean(k, block) @ haar_Wk[lvl].T
                v_lvl = causal_block_mean(v, block) @ haar_Wv[lvl].T
                glob = glob + scale_w[lvl] * chunked_causal_linear_attention(q, k_lvl, v_lvl, chunk=chunk_size)
            local_m = merge(local_out)
            glob_m = merge(glob)
            diff = local_m - glob_m
            gate_h = jax.nn.silu(jnp.concatenate([x, diff], axis=-1) @ Wg.T + bg)
            alpha = jax.nn.sigmoid(gate_h @ Wgo.T + bgo)
            mixed = alpha * local_m + (1.0 - alpha) * glob_m
            return mixed @ Wo.T + bo
        return hale_forward(x, Wq, Wk, Wv, Wkl, Wvl, haar_Wk, haar_Wv, haar_scale, Wg, bg, Wgo, bgo, Wo, bo)

    def _L0_ffn_ref(hidden_states, gate_w, correction_bias, Wg, Wu, Wd, Wg_s, Wu_s, Wd_s):
        import jax, jax.numpy as jnp
        import numpy as np
        E, H, I = (8, 128, 64)
        NG, TKG, TOPK = (4, 2, 4)
        SCALE = 2.5

        def _mlp(x, wg, wu, wd):
            return jax.nn.silu(x @ wg) * (x @ wu) @ wd
        B, T, _ = hidden_states.shape
        x = hidden_states.reshape(-1, H)
        N = x.shape[0]
        logits = x @ gate_w.T
        scores = jax.nn.sigmoid(logits)
        scores_c = scores + correction_bias
        grp = scores_c.reshape(N, NG, E // NG)
        group_scores = jnp.sum(jax.lax.top_k(grp, 2)[0], axis=-1)
        grp_idx = jax.lax.top_k(group_scores, TKG)[1]
        group_mask = jnp.zeros_like(group_scores).at[jnp.arange(N)[:, None], grp_idx].set(1.0)
        score_mask = jnp.repeat(group_mask, E // NG, axis=-1) > 0.5
        scores_for_choice = jnp.where(score_mask, scores_c, 0.0)
        topk_idx = jax.lax.top_k(scores_for_choice, TOPK)[1]
        topk_w = jnp.take_along_axis(scores, topk_idx, axis=-1)
        topk_w = topk_w / (jnp.sum(topk_w, axis=-1, keepdims=True) + 1e-20)
        topk_w = topk_w * SCALE
        cw = jnp.sum(jax.nn.one_hot(topk_idx, E, dtype=topk_w.dtype) * topk_w[..., None], axis=1)
        g = jnp.einsum('nh,ehi->eni', x, Wg)
        u = jnp.einsum('nh,ehi->eni', x, Wu)
        y = jnp.einsum('eni,eih->enh', jax.nn.silu(g) * u, Wd)
        routed = jnp.einsum('enh,ne->nh', y, cw)
        out = routed + _mlp(x, Wg_s, Wu_s, Wd_s)
        return out.reshape(B, T, H)

    def _L1_attn_ref(x, Wq, Wk, Wv, Wg, Wo, Wb, Wa, dt_bias, A_log, norm_w):
        import jax, jax.numpy as jnp
        import numpy as np
        D_MODEL = 128
        NUM_HEADS = 16
        HEAD_DIM = D_MODEL // NUM_HEADS
        CHUNK = 64
        B, T = (4, 512)

        def l2norm(x, eps=1e-06):
            return x * jax.lax.rsqrt(jnp.sum(x * x, axis=-1, keepdims=True) + eps)

        def _forward(x, Wq, Wk, Wv, Wg, Wo, Wb, Wa, dt_bias, A_log, norm_w):
            Bb, Tt, D = x.shape
            H, K, C = (NUM_HEADS, HEAD_DIM, CHUNK)
            n = Tt // C
            q = l2norm((x @ Wq).reshape(Bb, Tt, H, K)) / np.sqrt(K)
            k = l2norm((x @ Wk).reshape(Bb, Tt, H, K))
            v = (x @ Wv).reshape(Bb, Tt, H, K)
            gate = (x @ Wg).reshape(Bb, Tt, H, K)
            beta = jax.nn.sigmoid(x @ Wb)
            decay = -jnp.exp(A_log)[None, None, :] * jax.nn.softplus(x @ Wa + dt_bias)
            q = jnp.transpose(q, (0, 2, 1, 3)).astype(jnp.float32)
            k = jnp.transpose(k, (0, 2, 1, 3)).astype(jnp.float32)
            v = jnp.transpose(v, (0, 2, 1, 3)).astype(jnp.float32)
            beta_h = jnp.transpose(beta, (0, 2, 1))[..., None]
            v = v * beta_h
            k_beta = k * beta_h
            q = q.reshape(Bb, H, n, C, K)
            k = k.reshape(Bb, H, n, C, K)
            v = v.reshape(Bb, H, n, C, K)
            k_beta = k_beta.reshape(Bb, H, n, C, K)
            g = jnp.cumsum(jnp.transpose(decay, (0, 2, 1)).reshape(Bb, H, n, C), axis=-1)
            tril = jnp.tril(jnp.ones((C, C), bool))
            strict = jnp.tril(jnp.ones((C, C), bool), -1)
            diff = g[..., :, None] - g[..., None, :]
            L = jnp.where(tril, jnp.exp(jnp.where(tril, diff, 0.0)), 0.0)
            P = jnp.where(strict, jnp.einsum('bhncd,bhnmd->bhncm', k_beta, k) * L, 0.0)
            Ainv = jnp.eye(C, dtype=P.dtype) + P
            Pk = P
            for _ in range(int(np.ceil(np.log2(C))) - 1):
                Pk = Pk @ Pk
                Ainv = Ainv + Pk @ Ainv
            v = Ainv @ v
            k_cumdecay = Ainv @ (k_beta * jnp.exp(g)[..., None])

            def step(S, inp):
                q_i, k_i, v_i, kcd_i, g_i, L_i = inp
                attn = jnp.where(tril, jnp.einsum('bhck,bhmk->bhcm', q_i, k_i) * L_i, 0.0)
                v_new = v_i - kcd_i @ S
                o_i = q_i * jnp.exp(g_i)[..., None] @ S + attn @ v_new
                g_last = g_i[..., -1:]
                S_new = S * jnp.exp(g_last)[..., None] + jnp.einsum('bhck,bhcd->bhkd', k_i * jnp.exp(g_last - g_i)[..., None], v_new)
                return (S_new, o_i)
            to_scan = lambda a: jnp.moveaxis(a, 2, 0)
            S0 = jnp.zeros((Bb, H, K, K), jnp.float32)
            _, o = jax.lax.scan(step, S0, (to_scan(q), to_scan(k), to_scan(v), to_scan(k_cumdecay), to_scan(g), to_scan(L)))
            o = jnp.transpose(o, (1, 0, 3, 2, 4)).reshape(Bb, Tt, H, K)
            o = o * jax.lax.rsqrt(jnp.mean(o * o, axis=-1, keepdims=True) + 1e-05) * norm_w
            o = o * jax.nn.silu(gate)
            return o.reshape(Bb, Tt, D) @ Wo
        return _forward(x, Wq, Wk, Wv, Wg, Wo, Wb, Wa, dt_bias, A_log, norm_w)

    def _L1_ffn_ref(x, W_r, W_k, W_v, mu_r, mu_k):
        import jax, jax.numpy as jnp
        import numpy as np
        DIM = 128

        def _reference_tuple_inner(x, W_r, W_k, W_v, mu_r, mu_k):
            B, T, C = x.shape
            x_prev = jnp.concatenate([jnp.zeros((B, 1, C), x.dtype), x[:, :-1, :]], axis=1)
            xr = mu_r * x + (1.0 - mu_r) * x_prev
            xk = mu_k * x + (1.0 - mu_k) * x_prev
            r = jax.nn.sigmoid(jnp.einsum('btc,dc->btd', xr, W_r))
            k = jnp.einsum('btc,dc->btd', xk, W_k)
            k_act = jnp.square(jax.nn.relu(k))
            out = r * jnp.einsum('btc,dc->btd', k_act, W_v)
            new_state = x[:, -1, :]
            return (out, new_state)
        return _reference_tuple_inner(x, W_r, W_k, W_v, mu_r, mu_k)[0]
    x = L0_attn_x
    x = x + _L0_attn_ref(_layernorm(x, axis=-1), L0_attn_Wq, L0_attn_Wk, L0_attn_Wv, L0_attn_Wkl, L0_attn_Wvl, L0_attn_haar_Wk, L0_attn_haar_Wv, L0_attn_haar_scale, L0_attn_Wg, L0_attn_bg, L0_attn_Wgo, L0_attn_bgo, L0_attn_Wo, L0_attn_bo)
    x = x + _L0_ffn_ref(_layernorm(x, axis=-1), L0_ffn_gate_w, L0_ffn_correction_bias, L0_ffn_Wg, L0_ffn_Wu, L0_ffn_Wd, L0_ffn_Wg_s, L0_ffn_Wu_s, L0_ffn_Wd_s)
    x = x + _L1_attn_ref(_layernorm(x, axis=-1), L1_attn_Wq, L1_attn_Wk, L1_attn_Wv, L1_attn_Wg, L1_attn_Wo, L1_attn_Wb, L1_attn_Wa, L1_attn_dt_bias, L1_attn_A_log, L1_attn_norm_w)
    x = x + _L1_ffn_ref(_layernorm(x, axis=-1), L1_ffn_W_r, L1_ffn_W_k, L1_ffn_W_v, L1_ffn_mu_r, L1_ffn_mu_k)
    return x

_drawn_inputs = setup_inputs


def setup_inputs(seed=0):
    import zlib

    import numpy as np

    out = dict(_drawn_inputs(seed))
    spreads = {'L0_attn_bg': (0.0, 0.8),
     'L0_attn_bo': (0.0, 0.1),
     'L0_ffn_correction_bias': (0.0, 0.8),
     'L1_attn_dt_bias': (1.0, 0.6),
     'L1_attn_norm_w': (1.0, 0.2)}
    factors = {'L0_attn_haar_Wk': 2.912,
     'L0_attn_haar_scale': 5.562,
     'L0_ffn_gate_w': 4.495,
     'L0_ffn_Wu': 3.505,
     'L0_ffn_Wd': 3.561,
     'L0_ffn_Wg_s': 3.761,
     'L0_ffn_Wu_s': 4.144,
     'L0_ffn_Wd_s': 3.448,
     'L1_ffn_W_r': 3.723,
     'L1_ffn_mu_r': 7.42}
    for name, (base, spread) in spreads.items():
        noise = np.random.default_rng([zlib.crc32(name.encode()), seed]).standard_normal(out[name].shape)
        drawn = base * np.exp(spread * noise) if base else spread * noise
        out[name] = jnp.asarray(drawn.astype(out[name].dtype))
    for name, factor in factors.items():
        out[name] = (out[name] * factor).astype(out[name].dtype)
    return out
```

```python
from contextlib import ExitStack

import concourse.bass as bass
from concourse import mybir

F32 = mybir.dt.float32
BF16 = mybir.dt.bfloat16
ALU = mybir.AluOpType
ACT = mybir.ActivationFunctionType
AX = mybir.AxisListType.X

P = 128
NB, T = 2, 1024
NT = NB * T // P
NH, DH = 16, 8
CH = 64
PAD = 64
LV = 5
SEG = 512
NQ = NB * T // SEG
DE = DH + 1
NE = 8
EPS_LN, EPS_LIN, EPS_NORM, EPS_RMS = 1e-5, 1e-6, 1e-6, 1e-5
NC1 = T // CH
LH = 4
PW = 4 * LH * DH + 2 * LH

W_PARTS = [("WqT", 128), ("WklT", 128), ("WvlT", 128), ("Wk", 128), ("Wv", 128),
           ("HBk", 512), ("HBv", 512), ("hscale", 4), ("bo", 128),
           ("WgTa", 128), ("WgTb", 128), ("WgoT", 1), ("bg", 1), ("bgo", 1), ("WoT", 128),
           ("gateT", NE), ("cbias", NE), ("Eg", 576), ("Eu", 576), ("Ed", 512), ("Eds", 128),
           ("L1W", 4 * PW), ("dtb", LH), ("Alog", LH), ("normw", DH), ("L1Wo", 512),
           ("WrT", 128), ("WkT2", 128), ("WvT2", 128), ("mur", 1), ("muk", 1)]
W_OFF, _o = {}, 0
for _n, _w in W_PARTS:
    W_OFF[_n] = (_o, _o + _w)
    _o += _w
W_COLS = _o
C_PARTS = [("ident", 128), ("mean", LV * 128), ("tri", CH), ("hmask", NH), ("nmask", 128), ("nmask0", 128), ("half", 2), ("low4", 16), ("low8", 64)]
C_OFF, _o = {}, 0
for _n, _w in C_PARTS:
    C_OFF[_n] = (_o, _o + _w)
    _o += _w
C_COLS = _o


def program(nc, x_dram, w_dram, wk_dram, wv_dram, c_dram, out_dram, u_dram, s_dram, upto=9):
    with ExitStack() as ctx:
        def sb(name, shape, dt=F32):
            return ctx.enter_context(nc.sbuf_tensor(name, shape, dt))

        def sem(name):
            return ctx.enter_context(nc.semaphore(name))

        PS = ctx.enter_context(nc.psum_tensor("PS", [P, 8, 512], F32))
        W = sb("W", [P, W_COLS])
        C = sb("C", [P, C_COLS])
        X = sb("X", [P, NT, P])
        H = sb("H", [P, NT, P])
        hT = sb("hT", [P, NB, PAD + T])
        identb = sb("identb", [P, P], BF16)
        nmaskb = sb("nmaskb", [P, 2, P], BF16)
        st = sb("st", [P, NT, 6])
        mv = sb("mv", [P, NT, 2])
        sd = sb("sd", [P, 3, NT])
        arena = sb("arena", [P, 36864])
        pos = [0]

        def take(cols):
            a = arena[:, pos[0]:pos[0] + cols]
            pos[0] += cols
            assert pos[0] <= 36864, pos[0]
            return a

        def w(name, rows=P):
            a, b = W_OFF[name]
            return W[0:rows, a:b]

        def cst(name):
            a, b = C_OFF[name]
            return C[:, a:b]

        ident = cst("ident")
        mean = cst("mean").rearrange("p (l t) -> p l t", l=LV)

        qbd = [take(NH * SEG).rearrange("p (h t) -> p h t", h=NH) for _ in range(2)]
        qT = take(NB * T)
        qf = take(NB * T)
        loc_ = take(NT * P)
        loc = loc_.rearrange("p (j d) -> p j d", j=NT)
        glob_ = qT
        glob = glob_.rearrange("p (j d) -> p j d", j=NT)
        mark = pos[0]
        klT = take(NB * (PAD + T)).rearrange("p (b t) -> p b t", b=NB)
        v9l = take(NB * NC1 * NH * DE).rearrange("p (w h e) -> p w h e", w=NB * NC1, h=NH)
        prob = [take(512) for _ in range(3)]
        probT = [take(512) for _ in range(2)]
        rowmax = take(2 * 4).rearrange("p (u h) -> p u h", u=2)
        lrec = take(2 * NH).rearrange("p (u h) -> p u h", u=2)
        pos[0] = mark
        wk5 = sb("wk5", [P, LV * P])
        wv5 = sb("wv5", [P, LV * P])
        kvw = take(2 * LV * P)
        ephi = take(3 * 512).rearrange("p (u n) -> p u n", u=3)
        KF = [take(2 * LV * P).rearrange("p (a l n) -> p a l n", a=2, l=LV) for _ in range(2)]
        V9 = [take(2 * LV * NH * DE).rearrange("p (c l n) -> p c l n", c=2, l=LV) for _ in range(2)]
        AT = [take(512) for _ in range(4)]
        SB = take(4 * LV * NH * DE).rearrange("p (s l n) -> p s l n", s=4, l=LV)
        den = take(3 * LV * NH).rearrange("p (s l h) -> p s l h", s=3, l=LV)
        quo = take(LV * P).rearrange("p (l n) -> p l n", l=LV)
        hsw = sb("hsw", [P, 4 * LV])
        pos[0] = 0
        dT = [take(512) for _ in range(2)]
        gh = [take(512) for _ in range(2)]
        mix = take(NT * P).rearrange("p (j d) -> p j d", j=NT)
        mixT = [take(512) for _ in range(2)]
        diff = take(NT * P).rearrange("p (j d) -> p j d", j=NT)
        alpha = take(2 * NT)
        pos[0] = 0
        sgu = [take(512) for _ in range(3)]
        act = [take(5 * 512).rearrange("p (q n) -> p q n", q=5) for _ in range(2)]
        pos[0] = 12000
        rt_s, rt_c, rt_ch, rt_sel, rt_w, cw = (take(NT * NE).rearrange("p (j e) -> p j e", j=NT) for _ in range(6))
        rt_g, rt_gr, rt_gm = (take(NT * 4).rearrange("p (j e) -> p j e", j=NT) for _ in range(3))
        rt_p4, rt_q4 = (take(NT * 16).rearrange("p (j a b) -> p j a b", j=NT, a=4) for _ in range(2))
        rt_p8, rt_q8 = (take(NT * 64).rearrange("p (j a b) -> p j a b", j=NT, a=NE) for _ in range(2))
        rt_r8 = take(NT * NE).rearrange("p (j e) -> p j e", j=NT)
        rt_n = take(3 * NT).rearrange("p (k j) -> p k j", k=3)
        pos[0] = 0
        LD = LH * DH
        RC = LH * 2 * DH * DH
        pr = take(CH * PW).rearrange("p (t c) -> p t c", t=CH)
        ovl = take(CH * (3 * LD + LH * 2 * DH))
        kn, qn, kba = (ovl[:, i * CH * LD:(i + 1) * CH * LD].rearrange("p (t c) -> p t c", t=CH) for i in range(3))
        bb = ovl[:, 3 * CH * LD:].rearrange("p (t h c) -> p t h c", t=CH, h=LH)
        oS = [ovl[:, 0:4096], ovl[:, 3 * CH * LD:3 * CH * LD + 4096]]
        oT = ovl[0:LD, 0:P * CH]
        qeg = take(CH * LD).rearrange("p (t c) -> p t c", t=CH)
        og = take(CH * LD).rearrange("p (t c) -> p t c", t=CH)
        Z_ = take(CH * LH * 2 * DH)
        Z = Z_.rearrange("p (t h c) -> p t h c", t=CH, h=LH)
        Rs = [take(RC) for _ in range(2)]
        UW = 2 * 64 + 1
        late = take(4 * RC + 16)
        Ra, rk, ro = (late[:, i * RC:(i + 1) * RC] for i in range(3))
        rq = late[:, 3 * RC:4 * RC]
        rq4 = take(RC // 2).rearrange("p (n d) -> p n d", d=4)
        rq2 = take(RC // 4).rearrange("p (n d) -> p n d", d=2)
        Ui = late[:, 0:NC1 * UW].rearrange("p (n w) -> p n w", n=NC1)
        ry, rx = take(2 * LD), take(2 * LD)
        ss = take(CH * 8).rearrange("p (t h) -> p t h", t=CH)
        rs = take(CH * 8).rearrange("p (t h) -> p t h", t=CH)
        beta, dz, da, dsp, dec, alp, gc, eg, ba, be = (take(CH * LH).rearrange("p (t h) -> p t h", t=CH) for _ in range(10))
        ones = take(CH)
        eA = take(LH)
        Uo = take(LH * (2 * 64 + 1)).rearrange("p (h w) -> p h w", h=LH)
        Hf = H[:, :, :].rearrange("p j d -> p (j d)")
        SH = Hf[:, 0:NC1 * 64].rearrange("p (n w) -> p n w", n=NC1)
        sm, sr_, sv_ = Hf[:, 1024:1536], Hf[:, 1536:1600], Hf[:, 1600:1664]
        SL = Hf[:, 1664:1664 + LH * 64].rearrange("p (h w) -> p h w", h=LH)
        pos[0] = 0
        xr, xk = take(NB * T), take(NB * T)
        rl, ka, sgr, rv = ([take(512) for _ in range(2)] for _ in range(4))
        omu = take(2)

        x_in, w_in, c_in, cb_ready = sem("x_in"), sem("w_in"), sem("c_in"), sem("cb_ready")
        zeroed = sem("zeroed")
        ln_stats, ln_mv, ln_var, ln_sd, ln_rstd = (sem(n) for n in ("ln_stats", "ln_mv", "ln_var", "ln_sd", "ln_rstd"))
        ln_h, ln_T, ln_hT = sem("ln_h"), sem("ln_T"), sem("ln_hT")
        x_upd = sem("x_upd")
        xbo = sem("xbo")
        b_comb, b_w5, b_q, b_qe, b_qT, b_qm, b_qf, b_kl, b_klT, b_vl, b_v9 = (
            sem("b_" + n) for n in ("comb", "w5", "q", "qe", "qT", "qm", "qf", "kl", "klT", "vl", "v9"))
        b_sw, b_klT_pad, v9_zero, v9_ones = sem("b_sw"), sem("b_pads"), sem("v9_zero"), sem("v9_ones")
        c_qbd = [sem(f"c_qbd{i}") for i in range(NQ)]
        d_qbd = [sem(f"d_qbd{i}") for i in range(NQ)]
        c_S, c_max, c_sub, c_P, c_T, c_PT, c_O, c_rec, c_loc = (
            sem("c_" + n) for n in ("S", "max", "sub", "P", "T", "PT", "O", "rec", "loc"))
        d_u, d_kvw, d_e, d_em, d_phi, d_v9 = (sem("d_" + n) for n in ("u", "kvw", "e", "em", "phi", "v9"))
        d_st, d_Sb, d_S, d_A, d_av, d_den, d_rden, d_rw, d_quo, d_glob = (
            sem("d_" + n) for n in ("st", "Sb", "S", "A", "av", "den", "rden", "rw", "quo", "glob"))
        e_diff, e_dT, e_dTs, e_g, e_gh, e_al, e_alpha, e_mix, e_mT, e_mTs, e_out = (
            sem("e_" + n) for n in ("diff", "dT", "dTs", "g", "gh", "al", "alpha", "mix", "mT", "mTs", "out"))
        y_out = sem("y_out")
        f_lg, f_sc, f_rt, f_gu, f_cw, f_sg, f_a1, f_a2, f_out = (
            sem("f_" + n) for n in ("lg", "sc", "rt", "gu", "cw", "sg", "a1", "a2", "out"))
        g_p, g_pr, g_sq, g_act, g_dve, g_pool, g_ready = (
            sem("g_" + n) for n in ("p", "pr", "sq", "act", "dve", "pool", "ready"))
        l_R, l_Ra, l_rk, l_y, l_x, l_o, l_rq, l_r4, l_r2, l_z = (
            sem("l_" + n) for n in ("R", "Ra", "rk", "y", "x", "o", "rq", "r4", "r2", "z"))
        g_Uo, g_Ud, g_Ui, g_chain, g_Sd, g_SL = (sem("g_" + n) for n in ("Uo", "Ud", "Ui", "chain", "Sd", "SL"))
        g_w, g_om, g_os, g_o, g_norm, g_gate, g_T, g_oT, g_out = (
            sem("g_" + n) for n in ("w", "om", "os", "o", "norm", "gate", "T", "oT", "out"))
        g_norm0, h_pad = sem("g_norm0"), sem("h_pad")
        h_omu, h_mix, h_k, h_r, h_rl, h_ka, h_sr, h_v, h_rv, h_x = (
            sem("h_" + n) for n in ("omu", "mix", "k", "r", "rl", "ka", "sr", "v", "rv", "x"))

        block = ctx.enter_context(nc.Block())

        def hslice(q):
            b, o = divmod(q * SEG, T)
            return hT[:, b, PAD + o:PAD + o + SEG]

        hpack = hT[:, :, :].rearrange("p b t -> p (b t)")[:, 0:NB * T]

        def htile(j):
            b, o = divmod(j * P, T)
            return hT[:, b, PAD + o:PAD + o + P]

        def ln_dve(e, k):
            for j in range(NT):
                if k == 0:
                    e.wait_ge(x_in, 64)
                else:
                    e.wait_ge(x_upd, 4 * (k - 1) + j // 4 + 1)
                e.bn_stats(st[:, j, :], X[:, j, :]).then_inc(ln_stats, 1)
            for j in range(NT):
                e.wait_ge(ln_stats, NT * k + j + 1)
                e.bn_aggr(mv[:, j, :], st[:, j, :]).then_inc(ln_mv, 1)
            e.wait_ge(ln_mv, NT * (k + 1))
            e.tensor_scalar(sd[:, 0, :], mv[:, :, 1], EPS_LN, None, ALU.add).then_inc(ln_var, 1)
            e.wait_ge(ln_sd, k + 1)
            e.reciprocal(sd[:, 2, :], sd[:, 1, :]).then_inc(ln_rstd, 1)
            e.wait_ge(ln_rstd, k + 1)
            for j in range(NT):
                e.tensor_scalar(H[:, j, :], X[:, j, :], mv[:, j, 0:1], sd[:, 2, j:j + 1],
                                ALU.subtract, ALU.mult).then_inc(ln_h, 1)

        def ln_pe(e, k):
            for j in range(NT):
                q = j // 4
                e.wait_ge(ln_h, NT * k + j + 1)
                if k == 0 and j == 0:
                    e.wait_ge(c_in, 16)
                if q >= 2 and j % 4 == 0:
                    e.wait_ge(ln_hT, 4 * k + q - 1)
                m = e.transpose(PS[:, 6 + q % 2, (j % 4) * P:(j % 4 + 1) * P], H[:, j, :], ident)
                if j % 4 == 3:
                    m.then_inc(ln_T, 1)

        def ln_act(e, k):
            e.wait_ge(ln_var, k + 1)
            e.activation(sd[:, 1, :], sd[:, 0, :], ACT.Sqrt).then_inc(ln_sd, 1)
            for q in range(NQ):
                e.wait_ge(ln_T, 4 * k + q + 1)
                dst = hpack[:, q * SEG:(q + 1) * SEG] if k == 2 else hslice(q)
                e.activation(dst, PS[:, 6 + q % 2, :], ACT.Copy).then_inc(ln_hT, 1)

        NU = NT * 4

        def local_pe(e):
            def scores(u):
                j, g = divmod(u, 4)
                b, c0 = divmod(2 * j, NC1)
                if u >= 3:
                    e.wait_ge(c_sub, u - 2)
                if u % 16 == 0:
                    e.wait_ge(c_qbd[u // 16], 16 * NH)
                bank = PS[:, u % 3, :]
                e.matmul(bank, identb[:, :], nmaskb[:, 0 if c0 == 0 else 1, :].rearrange("p (o k) -> p o k", o=1)
                         .to_broadcast([P, 4, P]), start=True, stop=False, skip_group_check=True)
                for hh in range(4):
                    for c in range(2):
                        t0 = (j % 4) * P + CH * c
                        m = e.matmul(PS[CH * c:CH * c + CH, u % 3, hh * P:(hh + 1) * P],
                                     qbd[(j // 4) % 2][:, 4 * g + hh, t0:t0 + CH],
                                     klT[:, b, CH * (c0 + c):CH * (c0 + c) + P],
                                     start=False, stop=True, skip_group_check=True)
                m.then_inc(c_S, 1)

            def turn(u):
                e.wait_ge(c_P, u + 1)
                if u >= 2:
                    e.wait_ge(c_PT, u - 1)
                for hh in range(4):
                    m = e.transpose(PS[:, 3 + u % 2, hh * P:(hh + 1) * P], prob[u % 3][:, hh * P:(hh + 1) * P], ident)
                m.then_inc(c_T, 1)

            def values(u):
                j, g = divmod(u, 4)
                e.wait_ge(c_PT, u + 1)
                if g == 0 and j >= 2:
                    e.wait_ge(c_loc, j - 1)
                for hh in range(4):
                    h = 4 * g + hh
                    for c in range(2):
                        o = (8 * c + h // 2) * DE
                        m = e.matmul(PS[CH * (h % 2):CH * (h % 2) + CH, 5 + j % 2, o:o + DE],
                                     probT[u % 2][:, hh * P + CH * c:hh * P + CH * c + CH],
                                     v9l[:, 2 * j + c, h, :], start=True, stop=True, skip_group_check=True)
                m.then_inc(c_O, 1)

            e.wait_ge(cb_ready, 3)
            e.wait_ge(b_klT, NQ)
            e.wait_ge(b_v9, 8)
            scores(0)
            scores(1)
            for u in range(NU):
                if u + 2 < NU:
                    scores(u + 2)
                turn(u)
                if u >= 1:
                    values(u - 1)
            values(NU - 1)

        def local_dve(e):
            def normalise(j):
                e.wait_ge(c_O, 4 * j + 4)
                o = PS[:, 5 + j % 2, 0:NH * DE].rearrange("p (h e) -> p h e", e=DE)
                e.reciprocal(lrec[:, j % 2, :], o[:, :, DH]).then_inc(c_rec, 1)
                e.wait_ge(c_rec, j + 1)
                e.tensor_tensor(loc[:, j, :].rearrange("p (h e) -> p h e", e=DH), o[:, :, 0:DH],
                                lrec[:, j % 2, :].rearrange("p (h o) -> p h o", o=1).to_broadcast([P, NH, DH]),
                                ALU.mult).then_inc(c_loc, 1)

            for u in range(NU):
                e.wait_ge(c_S, u + 1)
                s = PS[:, u % 3, :].rearrange("p (h k) -> p h k", h=4)
                e.tensor_reduce(rowmax[:, u % 2, :], s, AX, ALU.max).then_inc(c_max, 1)
                e.wait_ge(c_max, u + 1)
                if u >= 3:
                    e.wait_ge(c_T, u - 2)
                e.tensor_tensor(prob[u % 3].rearrange("p (h k) -> p h k", h=4), s,
                                rowmax[:, u % 2, :].rearrange("p (h o) -> p h o", o=1).to_broadcast([P, 4, P]),
                                ALU.subtract).then_inc(c_sub, 1)
                if u % 4 == 2 and u >= 4:
                    normalise(u // 4 - 1)
            normalise(NT - 1)

        def local_act(e):
            def copy_back(u):
                e.wait_ge(c_T, u + 1)
                if u >= 2:
                    e.wait_ge(c_O, u - 1)
                e.activation(probT[u % 2], PS[:, 3 + u % 2, :], ACT.Copy).then_inc(c_PT, 1)

            for u in range(NU):
                e.wait_ge(c_sub, u + 1)
                e.activation(prob[u % 3], prob[u % 3], ACT.Exp, scale=float(DH) ** -0.5).then_inc(c_P, 1)
                if u >= 1:
                    copy_back(u - 1)
            copy_back(NU - 1)

        def prep_pe(e, j, i):
            p = 7 * j + i
            bank = PS[:, 6 + p % 2, :]
            h = htile(j)
            if j == 0 and i == 0:
                e.wait_ge(b_w5, 4)
            if i == 0 and j > 0:
                e.wait_ge(d_phi, 3 * j)
            elif i == 1 and j > 0:
                e.wait_ge(d_v9, 4 * j)
            elif i == 2:
                e.wait_ge(d_kvw, 3 * j + 1)
            elif i == 3:
                e.wait_ge(d_kvw, 3 * j + 2)
            elif i == 4:
                e.wait_ge(d_kvw, 3 * j + 3)
            elif i == 5:
                e.wait_ge(d_phi, 3 * j + 1)
            elif i == 6:
                e.wait_ge(d_phi, 3 * j + 2)
                e.wait_ge(d_v9, 4 * j + 2)
            kw = lambda l: kvw[:, l * P:(l + 1) * P] if l < 4 else kvw[:, 512:640]
            vw = lambda l: kvw[:, 768 + l * P:768 + (l + 1) * P] if l < 4 else kvw[:, 640:768]
            mm = lambda c, a, b: e.matmul(bank[:, c * P:(c + 1) * P], a, b, start=True, stop=True, skip_group_check=True)
            if i == 0:
                m = e.matmul(bank, h, wk5[:, 0:512], start=True, stop=True)
            elif i == 1:
                mm(0, h, wk5[:, 512:640])
                m = mm(1, h, wv5[:, 512:640])
            elif i == 2:
                m = e.matmul(bank, h, wv5[:, 0:512], start=True, stop=True)
            elif i == 3:
                for l in range(4):
                    m = mm(l, kw(l), mean[:, l, :])
            elif i == 4:
                mm(0, kw(4), mean[:, 4, :])
                mm(1, mean[:, 4, :], kw(4))
                m = mm(2, mean[:, 4, :], vw(4))
            elif i == 5:
                for l in range(4):
                    m = mm(l, mean[:, l, :], kw(l))
            else:
                for l in range(4):
                    m = mm(l, mean[:, l, :], vw(l))
            m.then_inc(d_u, 1)

        def prep_act(e, j):
            for i in range(7):
                p = 7 * j + i
                bank = PS[:, 6 + p % 2, :]
                e.wait_ge(d_u, p + 1)
                if i in (0, 1, 2):
                    a, n = ((0, 512), (512, 256), (768, 512))[i]
                    e.activation(kvw[:, a:a + n], bank[:, 0:n], ACT.Copy).then_inc(d_kvw, 1)
                if i in (3, 4, 5):
                    n = 256 if i == 4 else 512
                    if j > 0:
                        e.wait_ge(d_phi, 3 * (j - 1) + i - 2)
                    e.activation(ephi[:, i - 3, 0:n], bank[:, 0:n], ACT.Exp).then_inc(d_e, 1)
                if i in (4, 6):
                    if j >= 2:
                        e.wait_ge(d_av, 10 * (j - 1))
                    ls, a = ((4, 5), 256) if i == 4 else ((0, 4), 0)
                    n = (ls[1] - ls[0]) * P
                    for c in range(2):
                        r = slice(CH * c, CH * c + CH)
                        e.activation(V9[j % 2][r, c, ls[0]:ls[1], :].rearrange("p l (h e) -> p (l h) e", e=DE)[:, :, 0:DH],
                                     bank[r, a:a + n].rearrange("p (h e) -> p h e", e=DH), ACT.Copy).then_inc(d_v9, 1)

        def prep_pool(e, j):
            for i in range(3):
                n = 256 if i == 1 else 512
                e.wait_ge(d_e, 3 * j + i + 1)
                e.tensor_scalar(ephi[:, i, 0:n], ephi[:, i, 0:n], 1.0, None, ALU.min).then_inc(d_em, 1)

        def prep_dve(e, j, i):
            p = 7 * j + 3 + i
            bank = PS[:, 6 + p % 2, :]
            e.wait_ge(d_em, 3 * j + i + 1)
            if j >= 2:
                e.wait_ge(d_av, 10 * (j - 1))
            if i == 1:
                e.wait_ge(d_v9, 4 * j + 2)
                out, n, v = KF[j % 2][:, :, 4, :], 256, "p (a n) -> p a n"
                kw_ = dict(a=2)
            else:
                out, n, v = KF[j % 2][:, i // 2, 0:4, :], 512, "p (a n) -> p a n"
                kw_ = dict(a=4)
            e.scalar_tensor_tensor(out, bank[:, 0:n].rearrange(v, **kw_), 1.0, ephi[:, i, 0:n].rearrange(v, **kw_),
                                   ALU.add, ALU.max).then_inc(d_phi, 1)

        STATE = [(4, 0, 3), (5, 3, 5)]
        OUT = [(2, 0, 3), (3, 3, 5)]
        HE = NH * DE

        def bank_of(table, l, rows=slice(0, P)):
            for bk, a, b in table:
                if a <= l < b:
                    return PS[rows, bk, (l - a) * HE:(l - a + 1) * HE]

        def linear_pe(e):
            def state(j, c):
                k = 2 * j + c
                if k > 0:
                    e.wait_ge(d_Sb, 2 * k)
                for l in range(LV):
                    first = j % (NT // NB) == 0 and c == 0 and l in (0, 3)
                    m = e.matmul(bank_of(STATE, l), KF[j % 2][:, 1, l, :], V9[j % 2][:, c, l, :],
                                 start=first, stop=True, skip_group_check=True)
                m.then_inc(d_st, 1)

            def scores(j, s):
                l, hh = divmod(s, 2)
                n = 10 * j + s
                if n >= 2:
                    e.wait_ge(d_A, n - 1)
                if j % 4 == 0 and s == 0:
                    e.wait_ge(d_qbd[j // 4], 16 * NH)
                for c in range(2):
                    t0 = (j % 4) * P + CH * c
                    m = e.matmul(PS[CH * c:CH * c + CH, n % 2, :], KF[j % 2][:, 0, l, CH * c:CH * c + CH],
                                 qbd[(j // 4) % 2][:, 8 * hh:8 * hh + 8, t0:t0 + CH],
                                 start=True, stop=True, skip_group_check=True)
                m.then_inc(d_S, 1)

            def values(j, s):
                l, hh = divmod(s, 2)
                n = 10 * j + s
                if s == 0 and j > 0:
                    e.wait_ge(d_quo, 2 * j)
                if hh == 0:
                    for c in range(2):
                        k = 2 * j + c
                        e.wait_ge(d_Sb, 2 * k)
                        t0 = j * P + CH * c
                        for p in range(2):
                            e.matmul(bank_of(OUT, l, slice(CH * p, CH * p + CH))[:, c * HE // 2:(c + 1) * HE // 2],
                                     qf[:, t0:t0 + CH],
                                     SB[:, k % 4, l, :].rearrange("q (a p e) -> q p a e", p=2, e=DE)[:, p, :, :],
                                     start=(c == 0), stop=False, skip_group_check=True)
                e.wait_ge(d_A, n + 1)
                for h in range(8):
                    hd = 8 * hh + h
                    r = slice(CH * (hd % 2), CH * (hd % 2) + CH)
                    m = e.matmul(bank_of(OUT, l, r).rearrange("p (c a e) -> p c a e", c=2, e=DE)[:, :, hd // 2, :],
                                 AT[n % 4][:, h * CH:(h + 1) * CH], V9[j % 2][:, :, l, hd * DE:(hd + 1) * DE],
                                 start=False, stop=True, skip_group_check=True)
                m.then_inc(d_av, 1)

            e.wait_ge(c_loc, NT)
            e.wait_ge(zeroed, 4)
            e.wait_ge(v9_ones, 2)
            for i in range(7):
                prep_pe(e, 0, i)
            e.wait_ge(d_phi, 3)
            e.wait_ge(d_v9, 4)
            for j in range(NT):
                state(j, 0)
                scores(j, 0)
                scores(j, 1)
                for s in range(10):
                    if s < 7 and j + 1 < NT:
                        prep_pe(e, j + 1, s)
                    if s + 2 < 10:
                        scores(j, s + 2)
                    values(j, s)
                    if s == 4:
                        state(j, 1)
                if j + 1 < NT:
                    e.wait_ge(d_phi, 3 * (j + 2))
                    e.wait_ge(d_v9, 4 * (j + 2))

        tri = cst("tri").rearrange("p (o t) -> p o t", o=1)
        smask = cst("hmask").rearrange("p (h o) -> p h o", o=1)

        def linear_dve(e):
            def state(j, c):
                k = 2 * j + c
                e.wait_ge(d_st, k + 1)
                if k >= 4:
                    e.wait_ge(d_av, 5 * (k - 3) + 5)
                for bk, a, b in STATE:
                    o = SB[:, (k + 1) % 4, a:b, :]
                    if c == 1 and (j + 1) % (NT // NB) == 0:
                        e.memset(o, 0.0).then_inc(d_Sb, 1)
                    else:
                        e.tensor_tensor(o.rearrange("p l (h e) -> p l h e", e=DE),
                                        PS[:, bk, 0:(b - a) * HE].rearrange("p (l h e) -> p l h e", l=b - a, e=DE),
                                        smask.rearrange("p (l h) o -> p l h o", l=1).to_broadcast([P, b - a, NH, DE]),
                                        ALU.mult).then_inc(d_Sb, 1)

            def mask(j, s):
                n = 10 * j + s
                e.wait_ge(d_S, n + 1)
                if n >= 4:
                    e.wait_ge(d_av, n - 3)
                e.tensor_tensor(AT[n % 4].rearrange("p (h t) -> p h t", h=8),
                                PS[:, n % 2, :].rearrange("p (h t) -> p h t", h=8),
                                tri.to_broadcast([P, 8, CH]), ALU.mult).then_inc(d_A, 1)

            def finish(j):
                e.wait_ge(d_av, 10 * (j + 1))
                for bk, a, b in OUT:
                    o = PS[:, bk, 0:(b - a) * HE].rearrange("p (l h e) -> p l h e", l=b - a, e=DE)
                    e.tensor_scalar(den[:, 0, a:b, :], o[:, :, :, DH], EPS_LIN, None, ALU.max).then_inc(d_den, 1)
                e.wait_ge(d_den, 2 * j + 2)
                e.reciprocal(den[:, 1, :, :], den[:, 0, :, :]).then_inc(d_rden, 1)
                e.wait_ge(d_rden, j + 1)
                e.tensor_tensor(den[:, 2, :, :], den[:, 1, :, :],
                                hsw[:, 0:LV].rearrange("p (l o) -> p l o", o=1).to_broadcast([P, LV, NH]),
                                ALU.mult).then_inc(d_rw, 1)
                e.wait_ge(d_rw, j + 1)
                for bk, a, b in OUT:
                    o = PS[:, bk, 0:(b - a) * HE].rearrange("p (l h e) -> p (l h) e", l=b - a, e=DE)
                    e.tensor_tensor(quo[:, a:b, :].rearrange("p l (h e) -> p (l h) e", e=DH), o[:, :, 0:DH],
                                    den[:, 2, a:b, :].rearrange("p l (h o) -> p (l h) o", o=1)
                                    .to_broadcast([P, (b - a) * NH, DH]), ALU.mult).then_inc(d_quo, 1)
                e.wait_ge(d_quo, 2 * j + 2)
                e.tensor_reduce(glob[:, j, :], quo.rearrange("p l n -> p n l"), AX, ALU.add).then_inc(d_glob, 1)

            e.wait_ge(zeroed, 4)
            e.wait_ge(v9_ones, 2)
            for i in range(3):
                prep_dve(e, 0, i)
            for j in range(NT):
                state(j, 0)
                mask(j, 0)
                for s in range(10):
                    if s + 1 < 10:
                        mask(j, s + 1)
                    if s in (5, 6, 7) and j + 1 < NT:
                        prep_dve(e, j + 1, s - 5)
                    if s == 5:
                        state(j, 1)
                finish(j)

        def bc(ap, shape):
            return ap.to_broadcast(shape)

        def moe_pe(e):
            for j in range(NT):
                e.wait_ge(ln_hT, 4 + j // 4 + 1)
                m = e.matmul(PS[:, 0, j * NE:(j + 1) * NE], htile(j), w("gateT"), start=True, stop=True,
                             skip_group_check=True)
            m.then_inc(f_lg, 1)

            def down(tb):
                e.wait_ge(f_a2, 5 * (tb + 1))
                if tb >= 2:
                    e.wait_ge(x_upd, 4 + tb - 1)
                for i in range(4):
                    for q in range(5):
                        k = P if q < 4 else 64
                        wd = w("Ed")[:, q * P:(q + 1) * P] if q < 4 else w("Eds")[0:64, :]
                        m = e.matmul(PS[:, 6 + tb % 2, i * P:(i + 1) * P], act[tb % 2][0:k, q, i * P:(i + 1) * P], wd,
                                     start=(q == 0), stop=(q == 4), skip_group_check=True)
                m.then_inc(f_out, 1)

            for n in range(5 * NQ):
                tb, q = divmod(n, 5)
                rows_ = P if q < 4 else 64
                if n == 0:
                    e.wait_ge(f_sc, 1)
                if n >= 2:
                    e.wait_ge(f_sg, n - 1)
                    e.wait_ge(f_a2, n - 1)
                cols = slice(q * P, q * P + rows_)
                e.matmul(PS[0:rows_, n % 2, :], w("Eg")[:, cols], hslice(tb), start=True, stop=True)
                e.matmul(PS[0:rows_, 2 + n % 2, :], w("Eu")[:, cols], hslice(tb), start=True, stop=True).then_inc(f_gu, 1)
                if q < 4:
                    if n == 0:
                        e.wait_ge(f_rt, RT_STEPS)
                    for i in range(4):
                        for x in range(2):
                            m = e.matmul(PS[64 * x:64 * x + 64, 4 + n % 2, i * P:(i + 1) * P],
                                         bc(cw[:, 4 * tb + i, 2 * q + x:2 * q + x + 1], [P, 64]),
                                         ident, start=True, stop=True, skip_group_check=True)
                    m.then_inc(f_cw, 1)
                if q == 1 and tb > 0:
                    down(tb - 1)
            down(NQ - 1)

        RT_STEPS = 17

        def router(e):
            n = [0]

            def step(ins):
                n[0] += 1
                ins.then_inc(f_rt, 1)
                e.wait_ge(f_rt, n[0])

            e.wait_ge(f_sc, 1)
            step(e.tensor_tensor(rt_c, rt_s, bc(w("cbias").rearrange("p (o e) -> p o e", o=1), [P, NT, NE]), ALU.add))
            pair = rt_c.rearrange("p j (g two) -> p j g two", two=2)
            step(e.tensor_tensor(rt_g, pair[:, :, :, 0], pair[:, :, :, 1], ALU.add))

            def rank(v, m, p4, q4, low, r):
                vi = bc(v.rearrange("p j (g o) -> p j g o", o=1), [P, NT, m, m])
                vj = bc(v.rearrange("p j (o g) -> p j o g", o=1), [P, NT, m, m])
                step(e.tensor_tensor(p4, vj, vi, ALU.is_gt))
                step(e.tensor_tensor(q4, vj, vi, ALU.is_equal))
                lw = bc(low.rearrange("p (o n) -> p o n", o=1), [P, NT, m * m])
                step(e.tensor_tensor(q4.rearrange("p j a b -> p j (a b)"), q4.rearrange("p j a b -> p j (a b)"), lw, ALU.mult))
                step(e.tensor_tensor(p4, p4, q4, ALU.add))
                step(e.tensor_reduce(r, p4, AX, ALU.add))

            rank(rt_g, 4, rt_p4, rt_q4, cst("low4"), rt_gr)
            step(e.tensor_scalar(rt_gm, rt_gr, 2.0, None, ALU.is_lt))
            step(e.tensor_tensor(rt_ch.rearrange("p j (g two) -> p j g two", two=2), pair,
                                 bc(rt_gm.rearrange("p j (g o) -> p j g o", o=1), [P, NT, 4, 2]), ALU.mult))
            rank(rt_ch, NE, rt_p8, rt_q8, cst("low8"), rt_r8)
            step(e.scalar_tensor_tensor(rt_w, rt_r8, 4.0, rt_s, ALU.is_lt, ALU.mult))
            step(e.tensor_reduce(rt_n[:, 0, :], rt_w, AX, ALU.add))
            e.tensor_scalar(rt_n[:, 1, :], rt_n[:, 0, :], 1e-20, None, ALU.add).then_inc(g_w, 1)
            e.wait_ge(g_w, 1)
            e.reciprocal(rt_n[:, 2, :], rt_n[:, 1, :]).then_inc(g_w, 1)
            e.wait_ge(g_w, 2)
            e.tensor_tensor(rt_ch, rt_w, bc(rt_n[:, 2, :].rearrange("p (j o) -> p j o", o=1), [P, NT, NE]), ALU.mult)\
                .then_inc(g_w, 1)
            e.wait_ge(g_w, 3)
            step(e.tensor_scalar(cw, rt_ch, 2.5, None, ALU.mult))
            assert n[0] == RT_STEPS, n[0]

        def moe_dve(e):
            router(e)

            def residual(tb):
                e.wait_ge(f_out, tb + 1)
                xs = X[:, 4 * tb:4 * tb + 4, :]
                e.tensor_tensor(xs, PS[:, 6 + tb % 2, :].rearrange("p (j d) -> p j d", j=4), xs, ALU.add).then_inc(x_upd, 1)

            for n in range(5 * NQ):
                tb, q = divmod(n, 5)
                if q == 0 and tb >= 2:
                    e.wait_ge(f_out, tb - 1)
                e.wait_ge(f_sg, n + 1)
                if q < 4:
                    e.tensor_tensor(sgu[n % 3], sgu[n % 3], PS[:, 2 + n % 2, :], ALU.mult).then_inc(f_a1, 1)
                    e.wait_ge(f_a1, 4 * tb + q + 1)
                    e.wait_ge(f_cw, 4 * tb + q + 1)
                    e.tensor_tensor(act[tb % 2][:, q, :], sgu[n % 3], PS[:, 4 + n % 2, :], ALU.mult).then_inc(f_a2, 1)
                else:
                    e.tensor_tensor(act[tb % 2][0:64, q, :], sgu[n % 3][0:64], PS[0:64, 2 + n % 2, :], ALU.mult).then_inc(f_a2, 1)
                if q == 2 and tb > 0:
                    residual(tb - 1)
            residual(NQ - 1)

        def moe_act(e):
            e.wait_ge(f_lg, 1)
            e.activation(rt_s.rearrange("p j e -> p (j e)"), PS[:, 0, 0:NT * NE], ACT.Sigmoid).then_inc(f_sc, 1)
            for n in range(5 * NQ):
                rows_ = P if n % 5 < 4 else 64
                e.wait_ge(f_gu, n + 1)
                if n >= 3:
                    e.wait_ge(f_a2, n - 2)
                e.activation(sgu[n % 3][0:rows_], PS[0:rows_, n % 2, :], ACT.Silu).then_inc(f_sg, 1)

        tok = hpack.rearrange("p (n c) -> p n c", c=CH)
        NG = (CH + 2) // 3

        def col(ap, o):
            return ap[:, :, o:o + LD].rearrange("p t (h d) -> p t h d", h=LH)

        def per_head(ap, n=DH):
            return bc(ap.rearrange("p t (h o) -> p t h o", o=1), [P, CH, LH, n])

        h4 = lambda ap: ap.rearrange("p t (h d) -> p t h d", h=LH)

        def delta_pe(e):
            e.wait_ge(ln_hT, 12)
            for i in range(NG):
                if i >= 4:
                    e.wait_ge(g_pr, i - 3)
                for s in range(min(3, CH - 3 * i)):
                    t = 3 * i + s
                    for j in range(4):
                        m = e.matmul(PS[32 * j:32 * j + 32, i % 4, s * PW:(s + 1) * PW], tok[:, :, t],
                                     w("L1W")[:, j * PW:(j + 1) * PW], start=True, stop=True, skip_group_check=True)
                m.then_inc(g_p, 1)
            e.wait_ge(g_norm, 4)
            for i in range(CH // 4):
                if i >= 2:
                    e.wait_ge(g_oT, i - 1)
                for s in range(4):
                    m = e.transpose(PS[0:LD, 4 + i % 2, s * P:(s + 1) * P], og[:, 4 * i + s, :], ident)
                m.then_inc(g_T, 1)
            e.wait_ge(g_oT, CH // 4)
            for q in range(NQ):
                if q >= 2:
                    e.wait_ge(x_upd, 8 + q - 1)
                for i in range(4):
                    for j in range(4):
                        a = j * NB * T + (4 * q + i) * P
                        m = e.matmul(PS[:, 6 + q % 2, i * P:(i + 1) * P], oT[:, a:a + P],
                                     w("L1Wo", LD)[:, j * P:(j + 1) * P], start=(j == 0), stop=(j == 3),
                                     skip_group_check=True)
                m.then_inc(g_out, 1)

        def delta_act(e):
            for i in range(NG):
                n = min(3, CH - 3 * i)
                e.wait_ge(g_p, i + 1)
                e.activation(pr[:, 3 * i:3 * i + n, :].rearrange("p t c -> p (t c)"), PS[:, i % 4, 0:n * PW], ACT.Copy)\
                 .then_inc(g_pr, 1)
            e.wait_ge(g_pr, NG)
            e.activation(Z_.rearrange("p (t c) -> p t c", t=CH), pr[:, :, 0:2 * LD], ACT.Square).then_inc(g_sq, 1)
            e.activation(beta, pr[:, :, 4 * LD:4 * LD + LH], ACT.Sigmoid).then_inc(g_act, 1)
            e.wait_ge(g_dve, 1)
            e.activation(ss, ss, ACT.Sqrt).then_inc(g_act, 1)
            e.wait_ge(g_dve, 2)
            e.activation(da, dz, ACT.Abs).then_inc(g_act, 1)
            e.wait_ge(g_act, 3)
            e.activation(da, da, ACT.Exp, scale=-1.0).then_inc(g_act, 1)
            e.activation(eA, w("Alog"), ACT.Exp).then_inc(g_act, 1)
            e.wait_ge(g_dve, 3)
            e.activation(da, da, ACT.Ln).then_inc(g_act, 1)
            e.wait_ge(g_dve, 6)
            e.activation(alp, dec, ACT.Exp).then_inc(g_act, 1)
            e.activation(eg, gc, ACT.Exp).then_inc(g_act, 1)
            e.activation(pr[:, :, 3 * LD:4 * LD], pr[:, :, 3 * LD:4 * LD], ACT.Silu).then_inc(g_gate, 1)
            e.wait_ge(g_act, 8)
            e.activation(Uo[:, :, 128], eg[:, CH - 1, :], ACT.Copy).then_inc(g_Uo, 1)
            def decay(t, par):
                e.wait_ge(l_R, t + 1)
                for h in range(LH):
                    cols = slice(h * RC // LH, (h + 1) * RC // LH)
                    e.activation(Ra[:, cols], Rs[1 - par][:, cols], ACT.Copy, scale=alp[:, t, h:h + 1]).then_inc(l_Ra, 1)

            e.wait_ge(g_ready, 1)
            with e.Fori(0, CH // 2) as pair:
                decay(2 * pair, 0)
                decay(2 * pair + 1, 1)
            e.wait_ge(l_R, CH + 1)
            e.activation(Uo[:, :, 0:128], Rs[(CH - 1) % 2].rearrange("p (h w) -> p h w", h=LH), ACT.Copy).then_inc(g_Uo, 1)
            e.wait_ge(g_o, 1)
            e.activation(qeg, og, ACT.Square).then_inc(g_norm, 1)
            e.wait_ge(g_norm, 2)
            e.activation(ss[:, :, 0:LH], ss[:, :, 0:LH], ACT.Sqrt).then_inc(g_norm, 1)
            for i in range(CH // 4):
                e.wait_ge(g_T, i + 1)
                e.activation(oT.rearrange("p (l t) -> p l t", t=CH)[:, :, 4 * i:4 * i + 4],
                             PS[0:LD, 4 + i % 2, :].rearrange("p (t l) -> p l t", t=4), ACT.Copy).then_inc(g_oT, 1)

        def delta_pool(e):
            e.memset(ones, 1.0).then_inc(g_pool, 1)
            e.wait_ge(g_p, NG)
            e.memset(hT[:, :, 0:PAD], 0.0).then_inc(h_pad, 1)
            e.wait_ge(g_dve, 5)
            e.tensor_tensor(h4(kn), col(pr, LD), per_head(rs[:, :, 4:8]), ALU.mult).then_inc(g_pool, 1)
            e.wait_ge(g_act, 8)
            e.tensor_tensor(ba, beta, alp, ALU.mult).then_inc(g_pool, 1)
            e.tensor_tensor(be, beta, eg, ALU.mult).then_inc(g_pool, 1)
            e.wait_ge(g_pool, 4)
            e.tensor_tensor(h4(kba), h4(kn), per_head(ba), ALU.mult).then_inc(g_pool, 1)
            e.wait_ge(g_pool, 5)

            def query(t, par):
                e.wait_ge(l_R, t + 2)
                e.tensor_tensor(rq.rearrange("p (h c d) -> p h c d", h=LH, d=DH),
                                Rs[par].rearrange("p (h c d) -> p h c d", h=LH, d=DH),
                                bc(qn[:, t, :].rearrange("p (h o d) -> p h o d", h=LH, o=1), [P, LH, 2 * DH, DH]),
                                ALU.mult).then_inc(l_rq, 1)
                e.wait_ge(l_rq, t + 1)
                v = rq.rearrange("p (n d) -> p n d", d=8)
                e.tensor_tensor(rq4, v[:, :, 0:4], v[:, :, 4:8], ALU.add).then_inc(l_r4, 1)
                e.wait_ge(l_r4, t + 1)
                e.tensor_tensor(rq2, rq4[:, :, 0:2], rq4[:, :, 2:4], ALU.add).then_inc(l_r2, 1)
                e.wait_ge(l_r2, t + 1)
                e.tensor_tensor(Z[:, t, :, :].rearrange("p h c -> p (h c)"), rq2[:, :, 0], rq2[:, :, 1], ALU.add)\
                 .then_inc(l_z, 1)

            e.wait_ge(g_ready, 1)
            with e.Fori(0, CH // 2) as pair:
                query(2 * pair, 0)
                query(2 * pair + 1, 1)
            e.wait_ge(l_z, CH)
            e.wait_ge(g_SL, 128)
            e.wait_ge(g_w, 4)
            e.tensor_tensor(oS[1].rearrange("p (t e d) -> p t e d", t=CH, e=DH),
                            bc(qeg[:, :, 3 * DH:4 * DH].rearrange("p t (o d) -> p t o d", o=1), [P, CH, DH, DH]),
                            bc(SL[:, 3, :].rearrange("p (o e d) -> p o e d", o=1, e=DH), [P, CH, DH, DH]),
                            ALU.mult).then_inc(g_os, 1)
            e.wait_ge(g_gate, 1)
            e.tensor_tensor(col(pr, 3 * LD), col(pr, 3 * LD),
                            bc(w("normw").rearrange("p (o q d) -> p o q d", o=1, q=1), [P, CH, LH, DH]), ALU.mult)\
             .then_inc(g_gate, 1)

        def delta_dve(e):
            e.wait_ge(g_sq, 1)
            e.tensor_reduce(ss.rearrange("p t h -> p (t h)"), Z_.rearrange("p (n d) -> p n d", d=DH), AX, ALU.add).then_inc(g_norm0, 1)
            e.wait_ge(g_norm0, 1)
            e.tensor_scalar(ss, ss, EPS_NORM, None, ALU.add).then_inc(g_dve, 1)
            e.tensor_tensor(dz, pr[:, :, 4 * LD + LH:PW], bc(w("dtb").rearrange("p (o h) -> p o h", o=1), [P, CH, LH]),
                            ALU.add).then_inc(g_dve, 1)
            e.wait_ge(g_act, 4)
            e.tensor_scalar(da, da, 1.0, None, ALU.add).then_inc(g_dve, 1)
            e.wait_ge(g_act, 2)
            e.reciprocal(rs, ss).then_inc(g_dve, 1)
            e.wait_ge(g_dve, 4)
            e.tensor_scalar(rs[:, :, 0:LH], rs[:, :, 0:LH], float(DH) ** -0.5, None, ALU.mult).then_inc(g_dve, 1)
            e.wait_ge(g_act, 6)
            e.scalar_tensor_tensor(dsp, dz, 0.0, da, ALU.max, ALU.add).then_inc(g_norm0, 1)
            e.wait_ge(g_norm0, 2)
            e.scalar_tensor_tensor(dec, dsp, -1.0, bc(eA.rearrange("p (o h) -> p o h", o=1), [P, CH, LH]),
                                   ALU.mult, ALU.mult).then_inc(g_norm0, 1)
            e.wait_ge(g_norm0, 3)
            e.wait_ge(g_pool, 1)
            for h in range(LH):
                m = e.tensor_tensor_scan(gc[:, :, h], ones, dec[:, :, h], 0.0, ALU.mult, ALU.add)
            m.then_inc(g_dve, 1)
            e.wait_ge(g_dve, 5)
            e.tensor_tensor(h4(qn), col(pr, 0), per_head(rs[:, :, 0:4]), ALU.mult).then_inc(g_dve, 1)
            e.wait_ge(g_act, 8)
            e.tensor_tensor(bb[:, :, :, 0:DH], col(pr, 2 * LD), per_head(beta), ALU.mult).then_inc(g_dve, 1)
            e.wait_ge(g_pool, 4)
            e.tensor_tensor(bb[:, :, :, DH:2 * DH], h4(kn), per_head(be), ALU.mult).then_inc(g_dve, 1)
            e.wait_ge(g_dve, 7)
            e.tensor_tensor(h4(qeg), h4(qn), per_head(eg), ALU.mult).then_inc(g_dve, 1)
            e.memset(Rs[1], 0.0).then_inc(l_R, 1)
            e.wait_ge(g_pool, 5)
            e.wait_ge(g_dve, 10)
            e.memset(ry, 0.0).then_inc(g_ready, 1)

            hcd = lambda ap: ap.rearrange("p (h c d) -> p h c d", h=LH, d=DH)

            def step(t, par, first=False):
                e.wait_ge(l_R, t + 1)
                e.tensor_tensor(hcd(rk), hcd(Rs[1 - par]),
                                bc(kba[:, t, :].rearrange("p (h o d) -> p h o d", h=LH, o=1), [P, LH, 2 * DH, DH]),
                                ALU.mult).then_inc(l_rk, 1)
                e.wait_ge(l_rk, t + 1)
                e.tensor_reduce(ry, rk.rearrange("p (n d) -> p n d", d=DH), AX, ALU.add).then_inc(l_y, 1)
                e.wait_ge(l_y, t + 1)
                e.tensor_tensor(rx, ry, bb[:, t, :, :].rearrange("p h c -> p (h c)"), ALU.add).then_inc(l_x, 1)
                e.wait_ge(l_x, t + 1)
                e.tensor_tensor(hcd(ro), bc(rx.rearrange("p (h c o) -> p h c o", h=LH, o=1), [P, LH, 2 * DH, DH]),
                                bc(kn[:, t, :].rearrange("p (h o d) -> p h o d", h=LH, o=1), [P, LH, 2 * DH, DH]),
                                ALU.mult).then_inc(l_o, 1)
                e.wait_ge(l_o, t + 1)
                e.wait_ge(l_Ra, LH * (t + 1))
                if not first:
                    e.wait_ge(l_rq, t - 1)
                e.tensor_tensor(Rs[par], Ra, ro, ALU.add).then_inc(l_R, 1)

            e.wait_ge(g_ready, 1)
            step(0, 0, True)
            step(1, 1, True)
            with e.Fori(1, CH // 2) as pair:
                t = 2 * pair
                step(t, 0)
                step(t + 1, 1)

            e.memset(SH[0:32, 0, :], 0.0).then_inc(g_chain, 1)
            e.wait_ge(l_z, CH)
            e.tensor_tensor(h4(qeg), h4(qeg), Z[:, :, :, DH:2 * DH], ALU.subtract).then_inc(g_w, 1)
            e.wait_ge(g_Ui, 128)
            k = 1
            for n in range(NC1 - 1):
                S = SH[0:32, n, :]
                e.wait_ge(g_chain, k)
                e.tensor_tensor(sm[0:32].rearrange("p (e d i) -> p e d i", e=DH, d=DH),
                                bc(Ui[0:32, n, 64:128].rearrange("p (o i d) -> p o d i", o=1, i=DH), [32, DH, DH, DH]),
                                bc(S.rearrange("p (e o i) -> p e o i", e=DH, o=1), [32, DH, DH, DH]), ALU.mult)\
                 .then_inc(g_chain, 1)
                e.wait_ge(g_chain, k + 1)
                e.tensor_reduce(sr_[0:32], sm[0:32].rearrange("p (n i) -> p n i", i=DH), AX, ALU.add).then_inc(g_chain, 1)
                e.wait_ge(g_chain, k + 2)
                e.scalar_tensor_tensor(sv_[0:32], S, Ui[0:32, n, 128:129], sr_[0:32], ALU.mult, ALU.subtract)\
                 .then_inc(g_chain, 1)
                e.wait_ge(g_chain, k + 3)
                e.tensor_tensor(SH[0:32, n + 1, :], sv_[0:32], Ui[0:32, n, 0:64], ALU.add).then_inc(g_chain, 1)
                k += 4

            e.wait_ge(g_SL, 128)
            e.wait_ge(g_w, 4)
            for h in range(LH):
                buf = oS[0] if h < 3 else oS[1]
                if h < 3:
                    e.tensor_tensor(buf.rearrange("p (t e d) -> p t e d", t=CH, e=DH),
                                    bc(qeg[:, :, h * DH:(h + 1) * DH].rearrange("p t (o d) -> p t o d", o=1), [P, CH, DH, DH]),
                                    bc(SL[:, h, :].rearrange("p (o e d) -> p o e d", o=1, e=DH), [P, CH, DH, DH]),
                                    ALU.mult).then_inc(g_om, 1)
                    e.wait_ge(g_om, 2 * h + 1)
                else:
                    e.wait_ge(g_os, 1)
                e.tensor_reduce(og[:, :, h * DH:(h + 1) * DH], buf.rearrange("p (t e d) -> p t e d", t=CH, e=DH), AX,
                                ALU.add).then_inc(g_om, 1)
                e.wait_ge(g_om, min(2 * h + 2, 7))
            e.tensor_tensor(h4(og), h4(og), Z[:, :, :, 0:DH], ALU.add).then_inc(g_o, 1)
            e.wait_ge(g_norm, 1)
            e.tensor_reduce(rs[:, :, 0:LH], h4(qeg), AX, ALU.add).then_inc(g_om, 1)
            e.wait_ge(g_om, 8)
            e.tensor_scalar(ss[:, :, 0:LH], rs[:, :, 0:LH], 1.0 / DH, EPS_RMS, ALU.mult, ALU.add).then_inc(g_norm, 1)
            e.wait_ge(g_norm, 3)
            e.reciprocal(rs[:, :, 4:8], ss[:, :, 0:LH]).then_inc(g_om, 1)
            e.wait_ge(g_om, 9)
            e.tensor_tensor(h4(og), h4(og), per_head(rs[:, :, 4:8]), ALU.mult).then_inc(g_om, 1)
            e.wait_ge(g_om, 10)
            e.wait_ge(g_gate, 2)
            e.tensor_tensor(og, og, pr[:, :, 3 * LD:4 * LD], ALU.mult).then_inc(g_norm, 1)
            for q in range(NQ):
                e.wait_ge(g_out, q + 1)
                xs = X[:, 4 * q:4 * q + 4, :]
                e.tensor_tensor(xs, PS[:, 6 + q % 2, :].rearrange("p (j d) -> p j d", j=4), xs, ALU.add).then_inc(x_upd, 1)

        def mix_dve(e):
            for i, mu in enumerate(("mur", "muk")):
                e.tensor_scalar(omu[:, i:i + 1], w(mu), -1.0, 1.0, ALU.mult, ALU.add).then_inc(h_omu, 1)
            e.wait_ge(h_omu, 2)
            e.wait_ge(h_pad, 1)
            for q in range(NQ):
                e.wait_ge(ln_hT, 12 + q + 1)
                b, o = divmod(q * SEG, T)
                cols = slice(q * SEG, (q + 1) * SEG)
                for i, (mu, dst) in enumerate((("mur", xr), ("muk", xk))):
                    e.tensor_scalar(dst[:, cols], hslice(q), w(mu), None, ALU.mult).then_inc(h_mix, 1)
                for i, (mu, dst) in enumerate((("mur", xr), ("muk", xk))):
                    e.wait_ge(h_mix, 4 * q + i + 1)
                    e.scalar_tensor_tensor(dst[:, cols], hT[:, b, PAD + o - 1:PAD + o - 1 + SEG], omu[:, i:i + 1],
                                           dst[:, cols], ALU.mult, ALU.add).then_inc(h_mix, 1)
            for q in range(NQ + 1):
                if q < NQ:
                    e.wait_ge(h_rl, q + 1)
                    if q >= 2:
                        e.wait_ge(h_v, q - 1)
                    e.tensor_tensor(ka[q % 2], PS[:, q % 2, :], rl[q % 2], ALU.mult).then_inc(h_ka, 1)
                if q >= 1:
                    p_ = q - 1
                    e.wait_ge(h_v, p_ + 1)
                    e.wait_ge(h_sr, p_ + 1)
                    e.tensor_tensor(rv[p_ % 2], PS[:, 4 + p_ % 2, :], sgr[p_ % 2], ALU.mult).then_inc(h_rv, 1)
                    e.wait_ge(h_rv, p_ + 1)
                    xs = X[:, 4 * p_:4 * p_ + 4, :]
                    e.tensor_tensor(xs, rv[p_ % 2].rearrange("p (j d) -> p j d", j=4), xs, ALU.add).then_inc(h_x, 1)

        def mix_pe(e):
            for q in range(NQ + 1):
                if q < NQ:
                    e.wait_ge(h_mix, 4 * q + 4)
                    if q >= 2:
                        e.wait_ge(h_ka, q - 1)
                        e.wait_ge(h_sr, q - 1)
                    e.matmul(PS[:, q % 2, :], w("WkT2"), xk[:, q * SEG:(q + 1) * SEG], start=True, stop=True).then_inc(h_k, 1)
                    for i in range(4):
                        a = q * SEG + i * P
                        m = e.matmul(PS[:, 2 + q % 2, i * P:(i + 1) * P], xr[:, a:a + P], w("WrT"), start=True, stop=True,
                                     skip_group_check=True)
                    m.then_inc(h_r, 1)
                if q >= 1:
                    p_ = q - 1
                    e.wait_ge(h_ka, p_ + 1)
                    if p_ >= 2:
                        e.wait_ge(h_rv, p_ - 1)
                    for i in range(4):
                        m = e.matmul(PS[:, 4 + p_ % 2, i * P:(i + 1) * P], ka[p_ % 2][:, i * P:(i + 1) * P], w("WvT2"),
                                     start=True, stop=True, skip_group_check=True)
                    m.then_inc(h_v, 1)

        def mix_act(e):
            for q in range(NQ):
                e.wait_ge(h_k, q + 1)
                if q >= 2:
                    e.wait_ge(h_ka, q - 1)
                e.activation(rl[q % 2], PS[:, q % 2, :], ACT.Relu).then_inc(h_rl, 1)
                e.wait_ge(h_r, q + 1)
                if q >= 2:
                    e.wait_ge(h_rv, q - 1)
                e.activation(sgr[q % 2], PS[:, 2 + q % 2, :], ACT.Sigmoid).then_inc(h_sr, 1)

        def turn64(e, bank, src, q):
            for i in range(4):
                for c in range(2):
                    for p in range(2):
                        r = slice(CH * p, CH * p + CH)
                        m = e.matmul(PS[r, bank, i * P + CH * c:i * P + CH * c + CH],
                                     src[r, 4 * q + i, CH * c:CH * c + CH], ident[r, CH * p:CH * p + CH],
                                     start=True, stop=True, skip_group_check=True)
            return m

        @block.sync
        def _(e):
            xv = x_dram.rearrange("b (t p) d -> p (b t) d", p=P)
            for q in range(NQ):
                e.dma_start(X[:, 4 * q:4 * q + 4, :], xv[:, 4 * q:4 * q + 4, :]).then_inc(x_in, 16)
            e.dma_start(C[:, :], c_dram).then_inc(c_in, 16)
            e.dma_start(W[:, :], w_dram).then_inc(w_in, 16)
            e.dma_start(wk5[:, 0:P], wk_dram).then_inc(w_in, 16)
            e.dma_start(wv5[:, 0:P], wv_dram).then_inc(w_in, 16)
            e.wait_ge(zeroed, 2)
            for s in range(NQ):
                e.wait_ge(b_qT, s + 1)
                if s >= 2:
                    e.wait_ge(c_S, 16 * (s - 1))
                for h in range(NH):
                    r = slice(DH * h, DH * h + DH)
                    e.dma_start(qbd[s % 2][r, h, :], qT[r, s * SEG:(s + 1) * SEG]).then_inc(c_qbd[s], 16)
            for s in range(NQ):
                e.wait_ge(b_qf, s + 1)
                if s < 2:
                    e.wait_ge(c_S, 16 * (s + 3))
                else:
                    e.wait_ge(d_S, 40 * (s - 1))
                for h in range(NH):
                    r = slice(DH * h, DH * h + DH)
                    e.dma_start(qbd[s % 2][r, h, :], qf[r, s * SEG:(s + 1) * SEG]).then_inc(d_qbd[s], 16)
            ov = out_dram.rearrange("b (t p) d -> p (b t) d", p=P)
            e.wait_ge(g_Uo, 2)
            e.dma_start(u_dram, Uo).then_inc(g_Ud, 16)
            e.wait_ge(g_Ud, 16)
            e.wait_ge(l_z, CH)
            for jb in range(8):
                e.dma_start(Ui[4 * jb:4 * jb + 4, :, :], u_dram[16 * jb:16 * jb + 16, :, :].rearrange("n h w -> h n w"))\
                 .then_inc(g_Ui, 16)
            e.wait_ge(g_chain, 4 * (NC1 - 1) + 1)
            e.dma_start(s_dram, SH[0:32, :, :]).then_inc(g_Sd, 16)
            e.wait_ge(g_Sd, 16)
            for jb in range(8):
                e.dma_start(SL[16 * jb:16 * jb + 16, :, :], s_dram[4 * jb:4 * jb + 4, :, :].rearrange("h n w -> n h w"))\
                 .then_inc(g_SL, 16)
            for q in range(NQ):
                e.wait_ge(h_x, q + 1)
                e.dma_start(ov[:, 4 * q:4 * q + 4, :], X[:, 4 * q:4 * q + 4, :]).then_inc(y_out, 16)
            e.wait_ge(y_out, 16 * NQ)

        @block.gpsimd
        def _(e):
            e.memset(qbd[0], 0.0).then_inc(zeroed, 1)
            e.memset(qbd[1], 0.0).then_inc(zeroed, 1)
            e.memset(hT[:, :, 0:PAD], 0.0).then_inc(zeroed, 1)
            e.memset(klT[:, :, 0:PAD], 0.0).then_inc(b_klT_pad, 1)
            e.memset(v9l[:, :, :, DH:DE], 1.0).then_inc(b_klT_pad, 1)
            e.wait_ge(c_in, 16)
            e.wait_ge(w_in, 48)
            e.wait_ge(ln_h, NT)
            e.tensor_tensor(X[:, :, :], X[:, :, :], w("bo").rearrange("p (o d) -> p o d", o=1).to_broadcast([P, NT, P]),
                            ALU.add).then_inc(xbo, 1)
            for q in range(NQ):
                e.wait_ge(b_qe, q + 1)
                e.tensor_scalar(qf[:, q * SEG:(q + 1) * SEG], qf[:, q * SEG:(q + 1) * SEG], 1.0, None,
                                ALU.min).then_inc(b_qm, 1)
            e.wait_ge(c_loc, NT)
            for par in range(2):
                e.memset(V9[par], 0.0).then_inc(v9_zero, 1)
            e.memset(SB[:, 0, :, :], 0.0).then_inc(zeroed, 1)
            e.wait_ge(v9_zero, 2)
            for par in range(2):
                e.tensor_copy(V9[par].rearrange("p c l (h e) -> p c (l h) e", e=DE)[:, :, :, DH],
                              cst("half").rearrange("p (c o) -> p c o", o=1).to_broadcast([P, 2, LV * NH]))\
                 .then_inc(v9_ones, 1)
            for j in range(NT):
                prep_pool(e, j)
            for q in range(NQ):
                e.wait_ge(d_glob, 4 * q + 4)
                e.wait_ge(d_av, 10 * NT)
                e.tensor_tensor(diff[:, 4 * q:4 * q + 4, :], loc[:, 4 * q:4 * q + 4, :], glob[:, 4 * q:4 * q + 4, :],
                                ALU.subtract).then_inc(e_diff, 1)
            e.wait_ge(x_upd, 8)
            delta_pool(e)

        @block.scalar
        def _(e):
            e.wait_ge(c_in, 16)
            e.activation(identb[:, :], ident, ACT.Copy).then_inc(cb_ready, 1)
            e.activation(nmaskb[:, 0, :], cst("nmask0"), ACT.Copy).then_inc(cb_ready, 1)
            e.activation(nmaskb[:, 1, :], cst("nmask"), ACT.Copy).then_inc(cb_ready, 1)
            ln_act(e, 0)
            for i, t in enumerate((wk5, wv5)):
                e.wait_ge(b_comb, i + 1)
                e.activation(t[:, P:LV * P], PS[:, i, :], ACT.Copy).then_inc(b_w5, 2)
            for q in range(NQ):
                e.wait_ge(b_q, q + 1)
                cols = slice(q * SEG, (q + 1) * SEG)
                e.activation(qT[:, cols], PS[:, 2 + q, :], ACT.Copy).then_inc(b_qT, 1)
                e.activation(qf[:, cols], PS[:, 2 + q, :], ACT.Exp).then_inc(b_qe, 1)
            for q in range(NQ):
                e.wait_ge(b_kl, q + 1)
                b, o = divmod(q * SEG, T)
                e.activation(klT[:, b, PAD + o:PAD + o + SEG], PS[:, 6 + q % 2, :], ACT.Copy).then_inc(b_klT, 1)
            for i in range(8):
                e.wait_ge(b_vl, i + 1)
                if i == 0:
                    e.wait_ge(b_klT_pad, 2)
                e.activation(v9l[:, 4 * i:4 * i + 4, :, 0:DH].rearrange("p w h e -> p (w h) e"),
                             PS[:, i % 2, :].rearrange("p (h e) -> p h e", e=DH), ACT.Copy).then_inc(b_v9, 1)
            e.wait_ge(b_sw, 2)
            e.activation(hsw[:, 8:12], hsw[:, 4:8], ACT.Exp).then_inc(b_sw, 1)
            local_act(e)
            e.wait_ge(zeroed, 4)
            e.wait_ge(v9_ones, 2)
            for j in range(NT):
                prep_act(e, j)
            e.wait_ge(d_glob, NT)
            for q in range(NQ):
                e.wait_ge(e_dT, q + 1)
                e.activation(dT[q % 2], PS[:, q % 2, :], ACT.Copy).then_inc(e_dTs, 1)
                e.wait_ge(e_g, q + 1)
                e.activation(gh[q % 2], PS[:, 2 + q % 2, :], ACT.Silu, bias=w("bg")).then_inc(e_gh, 1)
                e.wait_ge(e_al, q + 1)
                e.activation(alpha[:, 8 * q:8 * q + 8], PS[:, 4 + q % 2, 0:8], ACT.Sigmoid, bias=w("bgo")).then_inc(e_alpha, 1)
            for q in range(NQ):
                e.wait_ge(e_mT, q + 1)
                e.activation(mixT[q % 2], PS[:, 6, :], ACT.Copy).then_inc(e_mTs, 1)
            ln_act(e, 1)
            moe_act(e)
            ln_act(e, 2)
            delta_act(e)
            ln_act(e, 3)
            mix_act(e)

        @block.tensor
        def _(e):
            ln_pe(e, 0)
            e.wait_ge(w_in, 48)
            e.wait_ge(zeroed, 3)
            for i, (a, b) in enumerate((("Wk", "HBk"), ("Wv", "HBv"))):
                e.matmul(PS[:, i, :], w(a), w(b), start=True, stop=True).then_inc(b_comb, 1)
            e.wait_ge(ln_hT, 4)
            for q in range(NQ):
                e.matmul(PS[:, 2 + q, :], w("WqT"), hslice(q), start=True, stop=True).then_inc(b_q, 1)
            for q in range(NQ):
                if q >= 2:
                    e.wait_ge(b_klT, q - 1)
                e.matmul(PS[:, 6 + q % 2, :], w("WklT"), hslice(q), start=True, stop=True).then_inc(b_kl, 1)
            e.wait_ge(b_w5, 4)
            for i in range(8):
                if i >= 2:
                    e.wait_ge(b_v9, i - 1)
                for k in range(4):
                    b, c = divmod(4 * i + k, NC1)
                    m = e.matmul(PS[:, i % 2, k * P:(k + 1) * P], hT[:, b, CH * c:CH * c + P], w("WvlT"),
                                 start=True, stop=True, skip_group_check=True)
                m.then_inc(b_vl, 1)
            e.wait_ge(b_qf, NQ)
            local_pe(e)
            linear_pe(e)
            e.wait_ge(d_glob, NT)
            for q in range(NQ):
                e.wait_ge(e_diff, q + 1)
                if q >= 2:
                    e.wait_ge(e_dTs, q - 1)
                m = turn64(e, q % 2, diff, q)
                m.then_inc(e_dT, 1)
                e.wait_ge(e_dTs, q + 1)
                if q >= 2:
                    e.wait_ge(e_gh, q - 1)
                e.matmul(PS[:, 2 + q % 2, :], w("WgTa"), hslice(q), start=True, stop=False)
                e.matmul(PS[:, 2 + q % 2, :], w("WgTb"), dT[q % 2], start=False, stop=True).then_inc(e_g, 1)
                e.wait_ge(e_gh, q + 1)
                if q >= 2:
                    e.wait_ge(e_alpha, q - 1)
                for i in range(8):
                    for p in range(2):
                        m = e.matmul(PS[CH * p:CH * p + CH, 4 + q % 2, i:i + 1], gh[q % 2][:, i * CH:(i + 1) * CH], w("WgoT"),
                                     start=True, stop=True, skip_group_check=True)
                m.then_inc(e_al, 1)
            for q in range(NQ):
                e.wait_ge(e_mix, 8 * q + 8)
                if q >= 1:
                    e.wait_ge(e_mTs, q)
                m = turn64(e, 6, mix, q)
                m.then_inc(e_mT, 1)
                e.wait_ge(e_mTs, q + 1)
                if q >= 1:
                    e.wait_ge(x_upd, q)
                for i in range(4):
                    m = e.matmul(PS[:, 7, i * P:(i + 1) * P], mixT[q % 2][:, i * P:(i + 1) * P], w("WoT"),
                                 start=True, stop=True, skip_group_check=True)
                m.then_inc(e_out, 1)
            ln_pe(e, 1)
            moe_pe(e)
            ln_pe(e, 2)
            delta_pe(e)
            ln_pe(e, 3)
            mix_pe(e)

        @block.vector
        def _(e):
            ln_dve(e, 0)
            e.wait_ge(w_in, 48)
            hs = w("hscale")
            e.tensor_reduce(hsw[:, 16:17], hs, AX, ALU.max).then_inc(b_sw, 1)
            e.wait_ge(b_sw, 1)
            e.tensor_scalar(hsw[:, 4:8], hs, hsw[:, 16:17], None, ALU.subtract).then_inc(b_sw, 1)
            for q in range(NQ):
                e.wait_ge(b_qm, q + 1)
                cols = slice(q * SEG, (q + 1) * SEG)
                e.scalar_tensor_tensor(qf[:, cols], PS[:, 2 + q, :], 1.0, qf[:, cols], ALU.add, ALU.max).then_inc(b_qf, 1)
            e.wait_ge(b_sw, 3)
            e.tensor_reduce(hsw[:, 17:18], hsw[:, 8:12], AX, ALU.add).then_inc(b_sw, 1)
            e.wait_ge(b_sw, 4)
            e.reciprocal(hsw[:, 18:19], hsw[:, 17:18]).then_inc(b_sw, 1)
            e.memset(hsw[:, 0:1], 1.0).then_inc(b_sw, 1)
            e.wait_ge(b_sw, 6)
            e.tensor_scalar(hsw[:, 1:5], hsw[:, 8:12], hsw[:, 18:19], None, ALU.mult).then_inc(b_sw, 1)
            e.wait_ge(b_sw, 7)
            local_dve(e)
            linear_dve(e)
            for q in range(NQ):
                e.wait_ge(e_alpha, q + 1)
                for i in range(8):
                    j, cols = 4 * q + i // 2, slice(CH * (i % 2), CH * (i % 2) + CH)
                    e.scalar_tensor_tensor(mix[:, j, cols], diff[:, j, cols], alpha[:, 8 * q + i:8 * q + i + 1],
                                           glob[:, j, cols], ALU.mult, ALU.add).then_inc(e_mix, 1)
            e.wait_ge(xbo, 1)
            for q in range(NQ):
                e.wait_ge(e_out, q + 1)
                xs = X[:, 4 * q:4 * q + 4, :]
                e.tensor_tensor(xs, PS[:, 7, :].rearrange("p (j d) -> p j d", j=4), xs, ALU.add).then_inc(x_upd, 1)
            ln_dve(e, 1)
            moe_dve(e)
            ln_dve(e, 2)
            delta_dve(e)
            ln_dve(e, 3)
            mix_dve(e)


def kernel(**inputs):
    import numpy as np
    import concourse.bacc as _bacc
    from concourse.bass_utils import run_bass_kernel_spmd as _run

    g = {k: np.ascontiguousarray(v) for k, v in inputs.items()}
    f4 = np.float32

    def bd(wl):
        out = np.zeros((NH, DH, 4, NH, DH), f4)
        for h in range(NH):
            out[h, :, :, h, :] = wl.transpose(2, 0, 1)
        return out.reshape(P, 512)

    def rows(v):
        return np.broadcast_to(v.reshape(1, -1), (P, v.size))

    def lanes(v):
        return np.repeat(v.reshape(4, LH), 32, axis=0)

    def split(wt):
        return wt.reshape(NH // 2, 2, DH, P).transpose(1, 0, 2, 3).reshape(P, P)

    a, f = "L0_attn_", "L0_ffn_"
    parts = {
        "WqT": g[a + "Wq"].T, "WklT": g[a + "Wkl"].T, "WvlT": g[a + "Wvl"].T, "Wk": g[a + "Wk"], "Wv": g[a + "Wv"],
        "HBk": bd(g[a + "haar_Wk"]), "HBv": bd(g[a + "haar_Wv"]), "hscale": rows(g[a + "haar_scale"]),
        "bo": rows(g[a + "bo"]), "WgTa": g[a + "Wg"].T[:P], "WgTb": split(g[a + "Wg"].T[P:]), "WgoT": g[a + "Wgo"].T,
        "bg": g[a + "bg"].reshape(P, 1), "bgo": rows(g[a + "bgo"]), "WoT": split(g[a + "Wo"].T),
        "gateT": g[f + "gate_w"].T, "cbias": rows(g[f + "correction_bias"]),
        "Eg": np.concatenate([g[f + "Wg"].transpose(1, 0, 2).reshape(P, 512), g[f + "Wg_s"]], 1),
        "Eu": np.concatenate([g[f + "Wu"].transpose(1, 0, 2).reshape(P, 512), g[f + "Wu_s"]], 1),
        "Ed": g[f + "Wd"].reshape(4, P, P).transpose(1, 0, 2).reshape(P, 512),
        "Eds": np.concatenate([g[f + "Wd_s"], np.zeros((64, P), f4)], 0),
        "dtb": lanes(g["L1_attn_dt_bias"]), "Alog": lanes(g["L1_attn_A_log"]), "normw": rows(g["L1_attn_norm_w"]),
        "L1Wo": np.concatenate([g["L1_attn_Wo"].reshape(4, 32, P).transpose(1, 0, 2).reshape(32, 512),
                                np.zeros((96, 512), f4)], 0),
        "WrT": g["L1_ffn_W_r"].T, "WkT2": g["L1_ffn_W_k"].T, "WvT2": g["L1_ffn_W_v"].T,
        "mur": g["L1_ffn_mu_r"].reshape(P, 1), "muk": g["L1_ffn_mu_k"].reshape(P, 1),
    }
    b = "L1_attn_"
    parts["L1W"] = np.concatenate(
        [np.concatenate([g[b + n][:, 32 * j:32 * j + 32] for n in ("Wq", "Wk", "Wv", "Wg")]
                        + [g[b + n][:, 4 * j:4 * j + 4] for n in ("Wb", "Wa")], 1) for j in range(4)], 1)
    wpack = np.concatenate([parts[n] for n, _ in W_PARTS], 1)

    s, t = np.arange(P)[:, None], np.arange(P)[None, :]
    mean = np.zeros((P, LV, P), f4)
    for i, blk in enumerate((1, 2, 4, 8, 16)):
        mean[:, i, :] = np.where((s // blk == t // blk) & (s <= t), 1.0 / (t % blk + 1), 0.0)
    qq = s % CH
    ok = (t <= qq + CH) & (t > qq)
    consts = {
        "ident": np.eye(P, dtype=f4), "mean": mean.reshape(P, -1),
        "tri": (qq <= np.arange(CH)[None, :]).astype(f4),
        "hmask": (s // DH == np.arange(NH)[None, :]).astype(f4),
        "nmask": np.where(ok, 0.0, -1e30).astype(f4),
        "low4": rows(np.tril(np.ones((4, 4), f4), -1)), "low8": rows(np.tril(np.ones((NE, NE), f4), -1)),
        "half": (s // CH == np.arange(2)[None, :]).astype(f4),
        "nmask0": np.where(ok & ((s >= CH) | (t >= CH)), 0.0, -1e30).astype(f4),
    }
    cpack = np.concatenate([consts[n] for n, _ in C_PARTS], 1).astype(f4)

    nc = _bacc.Bacc("TRN2", target_bir_lowering=False, num_devices=1)
    arrays = {"x": g["L0_attn_x"], "wpack": np.ascontiguousarray(wpack), "wkT": np.ascontiguousarray(g[a + "Wk"].T),
              "wvT": np.ascontiguousarray(g[a + "Wv"].T), "cpack": np.ascontiguousarray(cpack)}
    dram = {n: nc.dram_tensor(n, v.shape, F32, kind="ExternalInput").ap() for n, v in arrays.items()}
    out = nc.dram_tensor("out", (NB, T, P), F32, kind="ExternalOutput").ap()
    u = nc.dram_tensor("carry_out", (P, LH, 2 * DH * DH + 1), F32).ap()
    sd = nc.dram_tensor("carry_in", (32, NC1, DH * DH), F32).ap()
    program(nc, dram["x"], dram["wpack"], dram["wkT"], dram["wvT"], dram["cpack"], out, u, sd)
    return _run(nc, [arrays], core_ids=[0]).results[0]["out"]
```

```python
from contextlib import ExitStack

import concourse.bass as bass
from concourse import mybir

F32 = mybir.dt.float32
BF16 = mybir.dt.bfloat16
ALU = mybir.AluOpType
ACT = mybir.ActivationFunctionType
AX = mybir.AxisListType.X

P = 128
NB, T = 2, 1024
NT = NB * T // P
NH, DH = 16, 8
CH = 64
PAD = 64
LV = 5
SEG = 512
NQ = NB * T // SEG
DE = DH + 1
NE = 8
EPS_LN, EPS_LIN, EPS_NORM, EPS_RMS = 1e-5, 1e-6, 1e-6, 1e-5
NC1 = T // CH
LH = 4
PW = 4 * LH * DH + 2 * LH

W_PARTS = [("WqT", 128), ("WklT", 128), ("WvlT", 128), ("Wk", 128), ("Wv", 128),
           ("HBk", 512), ("HBv", 512), ("hscale", 4), ("bo", 128),
           ("WgTa", 128), ("WgTb", 128), ("WgoT", 1), ("bg", 1), ("bgo", 1), ("WoT", 128),
           ("gateT", NE), ("cbias", NE), ("Eg", 576), ("Eu", 576), ("Ed", 512), ("Eds", 128),
           ("L1W", 4 * PW), ("dtb", LH), ("Alog", LH), ("normw", DH), ("L1Wo", 128),
           ("WrT", 128), ("WkT2", 128), ("WvT2", 128), ("mur", 1), ("muk", 1)]
W_OFF, _o = {}, 0
for _n, _w in W_PARTS:
    W_OFF[_n] = (_o, _o + _w)
    _o += _w
W_COLS = _o
C_PARTS = [("ident", 128), ("mean", LV * 128), ("tri", CH), ("hmask", NH), ("nmask", 128), ("nmask0", 128), ("half", 2), ("low4", 16), ("low8", 64)]
C_OFF, _o = {}, 0
for _n, _w in C_PARTS:
    C_OFF[_n] = (_o, _o + _w)
    _o += _w
C_COLS = _o


def program(nc, x_dram, w_dram, wk_dram, wv_dram, c_dram, out_dram, u_dram, s_dram, upto=9):
    with ExitStack() as ctx:
        def sb(name, shape, dt=F32):
            return ctx.enter_context(nc.sbuf_tensor(name, shape, dt))

        def sem(name):
            return ctx.enter_context(nc.semaphore(name))

        PS = ctx.enter_context(nc.psum_tensor("PS", [P, 8, 512], F32))
        W = sb("W", [P, W_COLS])
        C = sb("C", [P, C_COLS])
        X = sb("X", [P, NT, P])
        H = sb("H", [P, NT, P])
        hT = sb("hT", [P, NB, PAD + T])
        identb = sb("identb", [P, P], BF16)
        nmaskb = sb("nmaskb", [P, 2, P], BF16)
        st = sb("st", [P, NT, 6])
        mv = sb("mv", [P, NT, 2])
        sd = sb("sd", [P, 3, NT])
        arena = sb("arena", [P, 36864])
        pos = [0]

        def take(cols):
            a = arena[:, pos[0]:pos[0] + cols]
            pos[0] += cols
            assert pos[0] <= 36864, pos[0]
            return a

        def w(name, rows=P):
            a, b = W_OFF[name]
            return W[0:rows, a:b]

        def cst(name):
            a, b = C_OFF[name]
            return C[:, a:b]

        ident = cst("ident")
        mean = cst("mean").rearrange("p (l t) -> p l t", l=LV)

        qbd = [take(NH * SEG).rearrange("p (h t) -> p h t", h=NH) for _ in range(2)]
        qT = take(NB * T)
        qf = take(NB * T)
        loc_ = take(NT * P)
        loc = loc_.rearrange("p (j d) -> p j d", j=NT)
        glob_ = qT
        glob = glob_.rearrange("p (j d) -> p j d", j=NT)
        mark = pos[0]
        klT = take(NB * (PAD + T)).rearrange("p (b t) -> p b t", b=NB)
        v9l = take(NB * NC1 * NH * DE).rearrange("p (w h e) -> p w h e", w=NB * NC1, h=NH)
        prob = [take(512) for _ in range(3)]
        probT = [take(512) for _ in range(2)]
        rowmax = take(2 * 4).rearrange("p (u h) -> p u h", u=2)
        lrec = take(2 * NH).rearrange("p (u h) -> p u h", u=2)
        pos[0] = mark
        wk5 = sb("wk5", [P, LV * P])
        wv5 = sb("wv5", [P, LV * P])
        kvw = take(2 * LV * P)
        ephi = take(3 * 512).rearrange("p (u n) -> p u n", u=3)
        KF = [take(2 * LV * P).rearrange("p (a l n) -> p a l n", a=2, l=LV) for _ in range(2)]
        V9 = [take(2 * LV * NH * DE).rearrange("p (c l n) -> p c l n", c=2, l=LV) for _ in range(2)]
        AT = [take(512) for _ in range(4)]
        SB = take(4 * LV * NH * DE).rearrange("p (s l n) -> p s l n", s=4, l=LV)
        den = take(3 * LV * NH).rearrange("p (s l h) -> p s l h", s=3, l=LV)
        quo = take(LV * P).rearrange("p (l n) -> p l n", l=LV)
        hsw = sb("hsw", [P, 4 * LV])
        pos[0] = 0
        dT = [take(512) for _ in range(2)]
        gh = [take(512) for _ in range(2)]
        mix = take(NT * P).rearrange("p (j d) -> p j d", j=NT)
        mixT = [take(512) for _ in range(2)]
        diff = take(NT * P).rearrange("p (j d) -> p j d", j=NT)
        alpha = take(2 * NT)
        pos[0] = 0
        sgu = [take(512) for _ in range(3)]
        act = [take(5 * 512).rearrange("p (q n) -> p q n", q=5) for _ in range(2)]
        pos[0] = 12000
        rt_s, rt_c, rt_ch, rt_sel, rt_w, cw = (take(NT * NE).rearrange("p (j e) -> p j e", j=NT) for _ in range(6))
        rt_g, rt_gr, rt_gm = (take(NT * 4).rearrange("p (j e) -> p j e", j=NT) for _ in range(3))
        rt_p4, rt_q4 = (take(NT * 16).rearrange("p (j a b) -> p j a b", j=NT, a=4) for _ in range(2))
        rt_p8, rt_q8 = (take(NT * 64).rearrange("p (j a b) -> p j a b", j=NT, a=NE) for _ in range(2))
        rt_r8 = take(NT * NE).rearrange("p (j e) -> p j e", j=NT)
        rt_n = take(3 * NT).rearrange("p (k j) -> p k j", k=3)
        pos[0] = 0
        LD = LH * DH
        RC = LH * 2 * DH * DH
        pr = take(CH * PW).rearrange("p (t c) -> p t c", t=CH)
        ovl = take(CH * (3 * LD + LH * 2 * DH))
        kn, qn, kba = (ovl[:, i * CH * LD:(i + 1) * CH * LD].rearrange("p (t c) -> p t c", t=CH) for i in range(3))
        bb = ovl[:, 3 * CH * LD:].rearrange("p (t h c) -> p t h c", t=CH, h=LH)
        oS = [ovl[:, 0:4096], ovl[:, 3 * CH * LD:3 * CH * LD + 4096]]
        oT = ovl[:, 0:CH * LD].rearrange("p (t l) -> p t l", t=CH)
        qeg = take(CH * LD).rearrange("p (t c) -> p t c", t=CH)
        og = take(CH * LD).rearrange("p (t c) -> p t c", t=CH)
        Z_ = take(CH * LH * 2 * DH)
        Zs = Z_.rearrange("p (t c) -> p t c", t=CH)
        Z = Z_.rearrange("p (t h c) -> p t h c", t=CH, h=LH)
        Rs = [take(RC) for _ in range(2)]
        UW = 2 * 64 + 1
        late = take(4 * RC + 16)
        Ra, rk, ro = (late[:, i * RC:(i + 1) * RC] for i in range(3))
        rq = late[:, 3 * RC:4 * RC]
        rq4 = [take(RC // 2).rearrange("p (n d) -> p n d", d=4) for _ in range(2)]
        rq2 = take(RC // 4).rearrange("p (n d) -> p n d", d=2)
        Ui = late[:, 0:NC1 * UW].rearrange("p (n w) -> p n w", n=NC1)
        ry, rx = take(2 * LD), take(2 * LD)
        ss = take(CH * 8).rearrange("p (t h) -> p t h", t=CH)
        rs = take(CH * 8).rearrange("p (t h) -> p t h", t=CH)
        beta, dz, da, dsp, dec, alp, gc, eg, ba, be = (take(CH * LH).rearrange("p (t h) -> p t h", t=CH) for _ in range(10))
        ones = take(CH)
        eA = take(LH)
        Uo = take(LH * (2 * 64 + 1)).rearrange("p (h w) -> p h w", h=LH)
        Hf = H[:, :, :].rearrange("p j d -> p (j d)")
        SH = Hf[:, 0:NC1 * 64].rearrange("p (n w) -> p n w", n=NC1)
        sm, sr_, sv_ = Hf[:, 1024:1536], Hf[:, 1536:1600], Hf[:, 1600:1664]
        SL = Hf[:, 1664:1664 + LH * 64].rearrange("p (h w) -> p h w", h=LH)
        pos[0] = 0
        xr, xk = take(NB * T), take(NB * T)
        rl, ka, sgr, rv = ([take(512) for _ in range(2)] for _ in range(4))
        omu = take(2)

        x_in, w_in, c_in, cb_ready = sem("x_in"), sem("w_in"), sem("c_in"), sem("cb_ready")
        zeroed = sem("zeroed")
        ln_stats, ln_mv, ln_var, ln_sd, ln_rstd = (sem(n) for n in ("ln_stats", "ln_mv", "ln_var", "ln_sd", "ln_rstd"))
        ln_h, ln_T, ln_hT = sem("ln_h"), sem("ln_T"), sem("ln_hT")
        x_upd = sem("x_upd")
        xbo = sem("xbo")
        b_comb, b_w5, b_q, b_qe, b_qT, b_qm, b_qf, b_kl, b_klT, b_vl, b_v9 = (
            sem("b_" + n) for n in ("comb", "w5", "q", "qe", "qT", "qm", "qf", "kl", "klT", "vl", "v9"))
        b_sw, b_klT_pad, v9_zero, v9_ones = sem("b_sw"), sem("b_pads"), sem("v9_zero"), sem("v9_ones")
        c_qbd = [sem(f"c_qbd{i}") for i in range(NQ)]
        d_qbd = [sem(f"d_qbd{i}") for i in range(NQ)]
        c_S, c_max, c_sub, c_P, c_T, c_PT, c_O, c_rec, c_loc = (
            sem("c_" + n) for n in ("S", "max", "sub", "P", "T", "PT", "O", "rec", "loc"))
        d_u, d_kvw, d_e, d_em, d_phi, d_v9 = (sem("d_" + n) for n in ("u", "kvw", "e", "em", "phi", "v9"))
        d_st, d_Sb, d_S, d_A, d_av, d_den, d_rden, d_rw, d_quo, d_glob = (
            sem("d_" + n) for n in ("st", "Sb", "S", "A", "av", "den", "rden", "rw", "quo", "glob"))
        e_diff, e_dT, e_dTs, e_g, e_gh, e_al, e_alpha, e_mix, e_mT, e_mTs, e_out = (
            sem("e_" + n) for n in ("diff", "dT", "dTs", "g", "gh", "al", "alpha", "mix", "mT", "mTs", "out"))
        y_out = sem("y_out")
        f_lg, f_sc, f_rt, f_gu, f_cw, f_sg, f_a1, f_a2, f_out = (
            sem("f_" + n) for n in ("lg", "sc", "rt", "gu", "cw", "sg", "a1", "a2", "out"))
        g_p, g_pr, g_sq, g_ss, g_act, g_dve, g_pool, g_ready = (
            sem("g_" + n) for n in ("p", "pr", "sq", "ss", "act", "dve", "pool", "ready"))
        l_R, l_Ra, l_rk, l_y, l_x, l_o, l_rq, l_r4, l_r2, l_z = (
            sem("l_" + n) for n in ("R", "Ra", "rk", "y", "x", "o", "rq", "r4", "r2", "z"))
        g_Uo, g_Ud, g_Ui, g_chain, g_Sd, g_SL = (sem("g_" + n) for n in ("Uo", "Ud", "Ui", "chain", "Sd", "SL"))
        g_w, g_om, g_os, g_o, g_norm, g_gate, g_oT, g_out = (
            sem("g_" + n) for n in ("w", "om", "os", "o", "norm", "gate", "oT", "out"))
        g_norm0, h_pad = sem("g_norm0"), sem("h_pad")
        h_omu, h_own, h_mix, h_k, h_r, h_rl, h_ka, h_sr, h_v, h_rv, h_x = (
            sem("h_" + n) for n in ("omu", "own", "mix", "k", "r", "rl", "ka", "sr", "v", "rv", "x"))

        block = ctx.enter_context(nc.Block())

        def hslice(q):
            b, o = divmod(q * SEG, T)
            return hT[:, b, PAD + o:PAD + o + SEG]

        hpack = hT[:, :, :].rearrange("p b t -> p (b t)")[:, 0:NB * T]

        def htile(j):
            b, o = divmod(j * P, T)
            return hT[:, b, PAD + o:PAD + o + P]

        def ln_bank(k, q):
            return (6, 2, 2, 4)[k] + q % 2

        def ln_moments(e, k, q):
            if k == 0:
                e.wait_ge(x_in, 64)
            else:
                e.wait_ge(x_upd, 4 * (k - 1) + q + 1)
            for j in range(4 * q, 4 * q + 4):
                e.bn_stats(st[:, j, :], X[:, j, :]).then_inc(ln_stats, 1)
            for j in range(4 * q, 4 * q + 4):
                e.wait_ge(ln_stats, NT * k + j + 1)
                e.bn_aggr(mv[:, j, :], st[:, j, :]).then_inc(ln_mv, 1)
            e.wait_ge(ln_mv, NT * k + 4 * q + 4)
            e.tensor_scalar(sd[:, 0, 4 * q:4 * q + 4], mv[:, 4 * q:4 * q + 4, 1], EPS_LN, None, ALU.add).then_inc(ln_var, 1)

        def ln_root(e, k, q):
            e.wait_ge(ln_var, 4 * k + q + 1)
            e.activation(sd[:, 1, 4 * q:4 * q + 4], sd[:, 0, 4 * q:4 * q + 4], ACT.Sqrt).then_inc(ln_sd, 1)

        def ln_scale(e, k, q):
            e.wait_ge(ln_sd, 4 * k + q + 1)
            e.reciprocal(sd[:, 2, 4 * q:4 * q + 4], sd[:, 1, 4 * q:4 * q + 4]).then_inc(ln_rstd, 1)
            e.wait_ge(ln_rstd, 4 * k + q + 1)
            for j in range(4 * q, 4 * q + 4):
                e.tensor_scalar(H[:, j, :], X[:, j, :], mv[:, j, 0:1], sd[:, 2, j:j + 1],
                                ALU.subtract, ALU.mult).then_inc(ln_h, 1)

        def ln_turn(e, k, q):
            if k == 0 and q == 0:
                e.wait_ge(c_in, 16)
            if q >= 2:
                e.wait_ge(ln_hT, 4 * k + q - 1)
            for j in range(4 * q, 4 * q + 4):
                e.wait_ge(ln_h, NT * k + j + 1)
                m = e.transpose(PS[:, ln_bank(k, q), (j % 4) * P:(j % 4 + 1) * P], H[:, j, :], ident)
            m.then_inc(ln_T, 1)

        def ln_store(e, k, q):
            e.wait_ge(ln_T, 4 * k + q + 1)
            dst = hpack[:, q * SEG:(q + 1) * SEG] if k == 2 else hslice(q)
            e.activation(dst, PS[:, ln_bank(k, q), :], ACT.Copy).then_inc(ln_hT, 1)

        NU = NT * 4

        def local_pe(e):
            def scores(u):
                j, g = divmod(u, 4)
                b, c0 = divmod(2 * j, NC1)
                if u >= 3:
                    e.wait_ge(c_sub, u - 2)
                if u % 16 == 0:
                    e.wait_ge(c_qbd[u // 16], 16 * NH)
                bank = PS[:, u % 3, :]
                e.matmul(bank, identb[:, :], nmaskb[:, 0 if c0 == 0 else 1, :].rearrange("p (o k) -> p o k", o=1)
                         .to_broadcast([P, 4, P]), start=True, stop=False, skip_group_check=True)
                for hh in range(4):
                    for c in range(2):
                        t0 = (j % 4) * P + CH * c
                        m = e.matmul(PS[CH * c:CH * c + CH, u % 3, hh * P:(hh + 1) * P],
                                     qbd[(j // 4) % 2][:, 4 * g + hh, t0:t0 + CH],
                                     klT[:, b, CH * (c0 + c):CH * (c0 + c) + P],
                                     start=False, stop=True, skip_group_check=True)
                m.then_inc(c_S, 1)

            def turn(u):
                e.wait_ge(c_P, u + 1)
                if u >= 2:
                    e.wait_ge(c_PT, u - 1)
                for hh in range(4):
                    m = e.transpose(PS[:, 3 + u % 2, hh * P:(hh + 1) * P], prob[u % 3][:, hh * P:(hh + 1) * P], ident)
                m.then_inc(c_T, 1)

            def values(u):
                j, g = divmod(u, 4)
                e.wait_ge(c_PT, u + 1)
                if g == 0 and j >= 2:
                    e.wait_ge(c_loc, j - 1)
                for hh in range(4):
                    h = 4 * g + hh
                    for c in range(2):
                        o = (8 * c + h // 2) * DE
                        m = e.matmul(PS[CH * (h % 2):CH * (h % 2) + CH, 5 + j % 2, o:o + DE],
                                     probT[u % 2][:, hh * P + CH * c:hh * P + CH * c + CH],
                                     v9l[:, 2 * j + c, h, :], start=True, stop=True, skip_group_check=True)
                m.then_inc(c_O, 1)

            e.wait_ge(cb_ready, 3)
            e.wait_ge(b_klT, NQ)
            e.wait_ge(b_v9, 8)
            scores(0)
            scores(1)
            for u in range(NU):
                if u + 2 < NU:
                    scores(u + 2)
                turn(u)
                if u >= 1:
                    values(u - 1)
            values(NU - 1)

        def local_dve(e):
            def normalise(j):
                e.wait_ge(c_O, 4 * j + 4)
                o = PS[:, 5 + j % 2, 0:NH * DE].rearrange("p (h e) -> p h e", e=DE)
                e.reciprocal(lrec[:, j % 2, :], o[:, :, DH]).then_inc(c_rec, 1)
                e.wait_ge(c_rec, j + 1)
                e.tensor_tensor(loc[:, j, :].rearrange("p (h e) -> p h e", e=DH), o[:, :, 0:DH],
                                lrec[:, j % 2, :].rearrange("p (h o) -> p h o", o=1).to_broadcast([P, NH, DH]),
                                ALU.mult).then_inc(c_loc, 1)

            for u in range(NU):
                e.wait_ge(c_S, u + 1)
                s = PS[:, u % 3, :].rearrange("p (h k) -> p h k", h=4)
                e.tensor_reduce(rowmax[:, u % 2, :], s, AX, ALU.max).then_inc(c_max, 1)
                e.wait_ge(c_max, u + 1)
                if u >= 3:
                    e.wait_ge(c_T, u - 2)
                e.tensor_tensor(prob[u % 3].rearrange("p (h k) -> p h k", h=4), s,
                                rowmax[:, u % 2, :].rearrange("p (h o) -> p h o", o=1).to_broadcast([P, 4, P]),
                                ALU.subtract).then_inc(c_sub, 1)
                if u % 4 == 2 and u >= 4:
                    normalise(u // 4 - 1)
            normalise(NT - 1)

        def local_act(e):
            def copy_back(u):
                e.wait_ge(c_T, u + 1)
                if u >= 2:
                    e.wait_ge(c_O, u - 1)
                e.activation(probT[u % 2], PS[:, 3 + u % 2, :], ACT.Copy).then_inc(c_PT, 1)

            for u in range(NU):
                e.wait_ge(c_sub, u + 1)
                e.activation(prob[u % 3], prob[u % 3], ACT.Exp, scale=float(DH) ** -0.5).then_inc(c_P, 1)
                if u >= 1:
                    copy_back(u - 1)
            copy_back(NU - 1)

        def prep_pe(e, j, i):
            p = 7 * j + i
            bank = PS[:, 6 + p % 2, :]
            h = htile(j)
            if j == 0 and i == 0:
                e.wait_ge(b_w5, 4)
            if i == 0 and j > 0:
                e.wait_ge(d_phi, 3 * j)
            elif i == 1 and j > 0:
                e.wait_ge(d_v9, 4 * j)
            elif i == 2:
                e.wait_ge(d_kvw, 3 * j + 1)
            elif i == 3:
                e.wait_ge(d_kvw, 3 * j + 2)
            elif i == 4:
                e.wait_ge(d_kvw, 3 * j + 3)
            elif i == 5:
                e.wait_ge(d_phi, 3 * j + 1)
            elif i == 6:
                e.wait_ge(d_phi, 3 * j + 2)
                e.wait_ge(d_v9, 4 * j + 2)
            kw = lambda l: kvw[:, l * P:(l + 1) * P] if l < 4 else kvw[:, 512:640]
            vw = lambda l: kvw[:, 768 + l * P:768 + (l + 1) * P] if l < 4 else kvw[:, 640:768]
            mm = lambda c, a, b: e.matmul(bank[:, c * P:(c + 1) * P], a, b, start=True, stop=True, skip_group_check=True)
            if i == 0:
                m = e.matmul(bank, h, wk5[:, 0:512], start=True, stop=True)
            elif i == 1:
                mm(0, h, wk5[:, 512:640])
                m = mm(1, h, wv5[:, 512:640])
            elif i == 2:
                m = e.matmul(bank, h, wv5[:, 0:512], start=True, stop=True)
            elif i == 3:
                for l in range(4):
                    m = mm(l, kw(l), mean[:, l, :])
            elif i == 4:
                mm(0, kw(4), mean[:, 4, :])
                mm(1, mean[:, 4, :], kw(4))
                m = mm(2, mean[:, 4, :], vw(4))
            elif i == 5:
                for l in range(4):
                    m = mm(l, mean[:, l, :], kw(l))
            else:
                for l in range(4):
                    m = mm(l, mean[:, l, :], vw(l))
            m.then_inc(d_u, 1)

        def prep_act(e, j):
            for i in range(7):
                p = 7 * j + i
                bank = PS[:, 6 + p % 2, :]
                e.wait_ge(d_u, p + 1)
                if i in (0, 1, 2):
                    a, n = ((0, 512), (512, 256), (768, 512))[i]
                    e.activation(kvw[:, a:a + n], bank[:, 0:n], ACT.Copy).then_inc(d_kvw, 1)
                if i in (3, 4, 5):
                    n = 256 if i == 4 else 512
                    if j > 0:
                        e.wait_ge(d_phi, 3 * (j - 1) + i - 2)
                    e.activation(ephi[:, i - 3, 0:n], bank[:, 0:n], ACT.Exp).then_inc(d_e, 1)
                if i in (4, 6):
                    if j >= 2:
                        e.wait_ge(d_av, 10 * (j - 1))
                    ls, a = ((4, 5), 256) if i == 4 else ((0, 4), 0)
                    n = (ls[1] - ls[0]) * P
                    for c in range(2):
                        r = slice(CH * c, CH * c + CH)
                        e.activation(V9[j % 2][r, c, ls[0]:ls[1], :].rearrange("p l (h e) -> p (l h) e", e=DE)[:, :, 0:DH],
                                     bank[r, a:a + n].rearrange("p (h e) -> p h e", e=DH), ACT.Copy).then_inc(d_v9, 1)

        def prep_pool(e, j):
            for i in range(3):
                n = 256 if i == 1 else 512
                e.wait_ge(d_e, 3 * j + i + 1)
                e.tensor_scalar(ephi[:, i, 0:n], ephi[:, i, 0:n], 1.0, None, ALU.min).then_inc(d_em, 1)

        def prep_dve(e, j, i):
            p = 7 * j + 3 + i
            bank = PS[:, 6 + p % 2, :]
            e.wait_ge(d_em, 3 * j + i + 1)
            if j >= 2:
                e.wait_ge(d_av, 10 * (j - 1))
            if i == 1:
                e.wait_ge(d_v9, 4 * j + 2)
                out, n, v = KF[j % 2][:, :, 4, :], 256, "p (a n) -> p a n"
                kw_ = dict(a=2)
            else:
                out, n, v = KF[j % 2][:, i // 2, 0:4, :], 512, "p (a n) -> p a n"
                kw_ = dict(a=4)
            e.scalar_tensor_tensor(out, bank[:, 0:n].rearrange(v, **kw_), 1.0, ephi[:, i, 0:n].rearrange(v, **kw_),
                                   ALU.add, ALU.max).then_inc(d_phi, 1)

        STATE = [(4, 0, 3), (5, 3, 5)]
        OUT = [(2, 0, 3), (3, 3, 5)]
        HE = NH * DE

        def bank_of(table, l, rows=slice(0, P)):
            for bk, a, b in table:
                if a <= l < b:
                    return PS[rows, bk, (l - a) * HE:(l - a + 1) * HE]

        def linear_pe(e):
            def state(j, c):
                k = 2 * j + c
                if k > 0:
                    e.wait_ge(d_Sb, 2 * k)
                for l in range(LV):
                    first = j % (NT // NB) == 0 and c == 0 and l in (0, 3)
                    m = e.matmul(bank_of(STATE, l), KF[j % 2][:, 1, l, :], V9[j % 2][:, c, l, :],
                                 start=first, stop=True, skip_group_check=True)
                m.then_inc(d_st, 1)

            def scores(j, s):
                l, hh = divmod(s, 2)
                n = 10 * j + s
                if n >= 2:
                    e.wait_ge(d_A, n - 1)
                if j % 4 == 0 and s == 0:
                    e.wait_ge(d_qbd[j // 4], 16 * NH)
                for c in range(2):
                    t0 = (j % 4) * P + CH * c
                    m = e.matmul(PS[CH * c:CH * c + CH, n % 2, :], KF[j % 2][:, 0, l, CH * c:CH * c + CH],
                                 qbd[(j // 4) % 2][:, 8 * hh:8 * hh + 8, t0:t0 + CH],
                                 start=True, stop=True, skip_group_check=True)
                m.then_inc(d_S, 1)

            def values(j, s):
                l, hh = divmod(s, 2)
                n = 10 * j + s
                if s == 0 and j > 0:
                    e.wait_ge(d_quo, 2 * j)
                if hh == 0:
                    for c in range(2):
                        k = 2 * j + c
                        e.wait_ge(d_Sb, 2 * k)
                        t0 = j * P + CH * c
                        for p in range(2):
                            e.matmul(bank_of(OUT, l, slice(CH * p, CH * p + CH))[:, c * HE // 2:(c + 1) * HE // 2],
                                     qf[:, t0:t0 + CH],
                                     SB[:, k % 4, l, :].rearrange("q (a p e) -> q p a e", p=2, e=DE)[:, p, :, :],
                                     start=(c == 0), stop=False, skip_group_check=True)
                e.wait_ge(d_A, n + 1)
                for h in range(8):
                    hd = 8 * hh + h
                    r = slice(CH * (hd % 2), CH * (hd % 2) + CH)
                    m = e.matmul(bank_of(OUT, l, r).rearrange("p (c a e) -> p c a e", c=2, e=DE)[:, :, hd // 2, :],
                                 AT[n % 4][:, h * CH:(h + 1) * CH], V9[j % 2][:, :, l, hd * DE:(hd + 1) * DE],
                                 start=False, stop=True, skip_group_check=True)
                m.then_inc(d_av, 1)

            e.wait_ge(c_loc, NT)
            e.wait_ge(zeroed, 4)
            e.wait_ge(v9_ones, 2)
            for i in range(7):
                prep_pe(e, 0, i)
            e.wait_ge(d_phi, 3)
            e.wait_ge(d_v9, 4)
            for j in range(NT):
                state(j, 0)
                scores(j, 0)
                scores(j, 1)
                for s in range(10):
                    if s < 7 and j + 1 < NT:
                        prep_pe(e, j + 1, s)
                    if s + 2 < 10:
                        scores(j, s + 2)
                    values(j, s)
                    if s == 4:
                        state(j, 1)
                if j + 1 < NT:
                    e.wait_ge(d_phi, 3 * (j + 2))
                    e.wait_ge(d_v9, 4 * (j + 2))

        tri = cst("tri").rearrange("p (o t) -> p o t", o=1)
        smask = cst("hmask").rearrange("p (h o) -> p h o", o=1)

        def linear_dve(e):
            def state(j, c):
                k = 2 * j + c
                e.wait_ge(d_st, k + 1)
                if k >= 4:
                    e.wait_ge(d_av, 5 * (k - 3) + 5)
                for bk, a, b in STATE:
                    o = SB[:, (k + 1) % 4, a:b, :]
                    if c == 1 and (j + 1) % (NT // NB) == 0:
                        e.memset(o, 0.0).then_inc(d_Sb, 1)
                    else:
                        e.tensor_tensor(o.rearrange("p l (h e) -> p l h e", e=DE),
                                        PS[:, bk, 0:(b - a) * HE].rearrange("p (l h e) -> p l h e", l=b - a, e=DE),
                                        smask.rearrange("p (l h) o -> p l h o", l=1).to_broadcast([P, b - a, NH, DE]),
                                        ALU.mult).then_inc(d_Sb, 1)

            def mask(j, s):
                n = 10 * j + s
                e.wait_ge(d_S, n + 1)
                if n >= 4:
                    e.wait_ge(d_av, n - 3)
                e.tensor_tensor(AT[n % 4].rearrange("p (h t) -> p h t", h=8),
                                PS[:, n % 2, :].rearrange("p (h t) -> p h t", h=8),
                                tri.to_broadcast([P, 8, CH]), ALU.mult).then_inc(d_A, 1)

            def finish(j):
                e.wait_ge(d_av, 10 * (j + 1))
                for bk, a, b in OUT:
                    o = PS[:, bk, 0:(b - a) * HE].rearrange("p (l h e) -> p l h e", l=b - a, e=DE)
                    e.tensor_scalar(den[:, 0, a:b, :], o[:, :, :, DH], EPS_LIN, None, ALU.max).then_inc(d_den, 1)
                e.wait_ge(d_den, 2 * j + 2)
                e.reciprocal(den[:, 1, :, :], den[:, 0, :, :]).then_inc(d_rden, 1)
                e.wait_ge(d_rden, j + 1)
                e.tensor_tensor(den[:, 2, :, :], den[:, 1, :, :],
                                hsw[:, 0:LV].rearrange("p (l o) -> p l o", o=1).to_broadcast([P, LV, NH]),
                                ALU.mult).then_inc(d_rw, 1)
                e.wait_ge(d_rw, j + 1)
                for bk, a, b in OUT:
                    o = PS[:, bk, 0:(b - a) * HE].rearrange("p (l h e) -> p (l h) e", l=b - a, e=DE)
                    e.tensor_tensor(quo[:, a:b, :].rearrange("p l (h e) -> p (l h) e", e=DH), o[:, :, 0:DH],
                                    den[:, 2, a:b, :].rearrange("p l (h o) -> p (l h) o", o=1)
                                    .to_broadcast([P, (b - a) * NH, DH]), ALU.mult).then_inc(d_quo, 1)
                e.wait_ge(d_quo, 2 * j + 2)
                e.tensor_reduce(glob[:, j, :], quo.rearrange("p l n -> p n l"), AX, ALU.add).then_inc(d_glob, 1)

            e.wait_ge(zeroed, 4)
            e.wait_ge(v9_ones, 2)
            for i in range(3):
                prep_dve(e, 0, i)
            for j in range(NT):
                state(j, 0)
                mask(j, 0)
                for s in range(10):
                    if s + 1 < 10:
                        mask(j, s + 1)
                    if s in (5, 6, 7) and j + 1 < NT:
                        prep_dve(e, j + 1, s - 5)
                    if s == 5:
                        state(j, 1)
                finish(j)

        def bc(ap, shape):
            return ap.to_broadcast(shape)

        def moe_pe(e):
            for j in range(NT):
                e.wait_ge(ln_hT, 4 + j // 4 + 1)
                m = e.matmul(PS[:, 0, j * NE:(j + 1) * NE], htile(j), w("gateT"), start=True, stop=True,
                             skip_group_check=True)
            m.then_inc(f_lg, 1)

            def down(tb):
                e.wait_ge(f_a2, 5 * (tb + 1))
                if tb >= 2:
                    e.wait_ge(x_upd, 4 + tb - 1)
                for i in range(4):
                    for q in range(5):
                        k = P if q < 4 else 64
                        wd = w("Ed")[:, q * P:(q + 1) * P] if q < 4 else w("Eds")[0:64, :]
                        m = e.matmul(PS[:, 6 + tb % 2, i * P:(i + 1) * P], act[tb % 2][0:k, q, i * P:(i + 1) * P], wd,
                                     start=(q == 0), stop=(q == 4), skip_group_check=True)
                m.then_inc(f_out, 1)

            for n in range(5 * NQ):
                tb, q = divmod(n, 5)
                rows_ = P if q < 4 else 64
                if n == 0:
                    e.wait_ge(f_sc, 1)
                if n >= 2:
                    e.wait_ge(f_sg, n - 1)
                    e.wait_ge(f_a2, n - 1)
                cols = slice(q * P, q * P + rows_)
                e.matmul(PS[0:rows_, n % 2, :], w("Eg")[:, cols], hslice(tb), start=True, stop=True)
                e.matmul(PS[0:rows_, 2 + n % 2, :], w("Eu")[:, cols], hslice(tb), start=True, stop=True).then_inc(f_gu, 1)
                if q < 4:
                    if n == 0:
                        e.wait_ge(f_rt, RT_STEPS)
                    for i in range(4):
                        for x in range(2):
                            m = e.matmul(PS[64 * x:64 * x + 64, 4 + n % 2, i * P:(i + 1) * P],
                                         bc(cw[:, 4 * tb + i, 2 * q + x:2 * q + x + 1], [P, 64]),
                                         ident, start=True, stop=True, skip_group_check=True)
                    m.then_inc(f_cw, 1)
                if q == 1 and tb > 0:
                    down(tb - 1)
            down(NQ - 1)
            for q in range(NQ):
                ln_turn(e, 2, q)

        RT_STEPS = 17

        def router(e):
            n = [0]

            def step(ins):
                n[0] += 1
                ins.then_inc(f_rt, 1)
                e.wait_ge(f_rt, n[0])

            e.wait_ge(f_sc, 1)
            step(e.tensor_tensor(rt_c, rt_s, bc(w("cbias").rearrange("p (o e) -> p o e", o=1), [P, NT, NE]), ALU.add))
            pair = rt_c.rearrange("p j (g two) -> p j g two", two=2)
            step(e.tensor_tensor(rt_g, pair[:, :, :, 0], pair[:, :, :, 1], ALU.add))

            def rank(v, m, p4, q4, low, r):
                vi = bc(v.rearrange("p j (g o) -> p j g o", o=1), [P, NT, m, m])
                vj = bc(v.rearrange("p j (o g) -> p j o g", o=1), [P, NT, m, m])
                step(e.tensor_tensor(p4, vj, vi, ALU.is_gt))
                step(e.tensor_tensor(q4, vj, vi, ALU.is_equal))
                lw = bc(low.rearrange("p (o n) -> p o n", o=1), [P, NT, m * m])
                step(e.tensor_tensor(q4.rearrange("p j a b -> p j (a b)"), q4.rearrange("p j a b -> p j (a b)"), lw, ALU.mult))
                step(e.tensor_tensor(p4, p4, q4, ALU.add))
                step(e.tensor_reduce(r, p4, AX, ALU.add))

            rank(rt_g, 4, rt_p4, rt_q4, cst("low4"), rt_gr)
            step(e.tensor_scalar(rt_gm, rt_gr, 2.0, None, ALU.is_lt))
            step(e.tensor_tensor(rt_ch.rearrange("p j (g two) -> p j g two", two=2), pair,
                                 bc(rt_gm.rearrange("p j (g o) -> p j g o", o=1), [P, NT, 4, 2]), ALU.mult))
            rank(rt_ch, NE, rt_p8, rt_q8, cst("low8"), rt_r8)
            step(e.scalar_tensor_tensor(rt_w, rt_r8, 4.0, rt_s, ALU.is_lt, ALU.mult))
            step(e.tensor_reduce(rt_n[:, 0, :], rt_w, AX, ALU.add))
            e.tensor_scalar(rt_n[:, 1, :], rt_n[:, 0, :], 1e-20, None, ALU.add).then_inc(g_w, 1)
            e.wait_ge(g_w, 1)
            e.reciprocal(rt_n[:, 2, :], rt_n[:, 1, :]).then_inc(g_w, 1)
            e.wait_ge(g_w, 2)
            e.tensor_tensor(rt_ch, rt_w, bc(rt_n[:, 2, :].rearrange("p (j o) -> p j o", o=1), [P, NT, NE]), ALU.mult)\
                .then_inc(g_w, 1)
            e.wait_ge(g_w, 3)
            step(e.tensor_scalar(cw, rt_ch, 2.5, None, ALU.mult))
            assert n[0] == RT_STEPS, n[0]

        def moe_dve(e):
            router(e)

            def residual(tb):
                e.wait_ge(f_out, tb + 1)
                xs = X[:, 4 * tb:4 * tb + 4, :]
                e.tensor_tensor(xs, PS[:, 6 + tb % 2, :].rearrange("p (j d) -> p j d", j=4), xs, ALU.add).then_inc(x_upd, 1)

            for n in range(5 * NQ):
                tb, q = divmod(n, 5)
                if q == 0 and tb >= 2:
                    e.wait_ge(f_out, tb - 1)
                e.wait_ge(f_sg, n + 1)
                if q < 4:
                    e.tensor_tensor(sgu[n % 3], sgu[n % 3], PS[:, 2 + n % 2, :], ALU.mult).then_inc(f_a1, 1)
                    e.wait_ge(f_a1, 4 * tb + q + 1)
                    e.wait_ge(f_cw, 4 * tb + q + 1)
                    e.tensor_tensor(act[tb % 2][:, q, :], sgu[n % 3], PS[:, 4 + n % 2, :], ALU.mult).then_inc(f_a2, 1)
                else:
                    e.tensor_tensor(act[tb % 2][0:64, q, :], sgu[n % 3][0:64], PS[0:64, 2 + n % 2, :], ALU.mult).then_inc(f_a2, 1)
                if q == 2 and tb > 0:
                    residual(tb - 1)
                    ln_moments(e, 2, tb - 1)
            for q in range(NQ - 1):
                ln_scale(e, 2, q)
            residual(NQ - 1)
            ln_moments(e, 2, NQ - 1)
            ln_scale(e, 2, NQ - 1)

        def moe_act(e):
            e.wait_ge(f_lg, 1)
            e.activation(rt_s.rearrange("p j e -> p (j e)"), PS[:, 0, 0:NT * NE], ACT.Sigmoid).then_inc(f_sc, 1)
            for n in range(5 * NQ):
                rows_ = P if n % 5 < 4 else 64
                e.wait_ge(f_gu, n + 1)
                if n >= 3:
                    e.wait_ge(f_a2, n - 2)
                e.activation(sgu[n % 3][0:rows_], PS[0:rows_, n % 2, :], ACT.Silu).then_inc(f_sg, 1)
            for q in range(NQ - 1):
                ln_root(e, 2, q)
            ln_store(e, 2, 0)
            ln_root(e, 2, NQ - 1)
            for q in range(1, NQ):
                ln_store(e, 2, q)

        tok = hpack.rearrange("p (n c) -> p n c", c=CH)
        NG = (CH + 2) // 3

        def col(ap, o):
            return ap[:, :, o:o + LD].rearrange("p t (h d) -> p t h d", h=LH)

        def per_head(ap, n=DH):
            return bc(ap.rearrange("p t (h o) -> p t h o", o=1), [P, CH, LH, n])

        h4 = lambda ap: ap.rearrange("p t (h d) -> p t h d", h=LH)

        def delta_pe(e):
            e.wait_ge(ln_hT, 12)
            for i in range(NG):
                if i >= 4:
                    e.wait_ge(g_pr, i - 3)
                for s in range(min(3, CH - 3 * i)):
                    t = 3 * i + s
                    for j in range(4):
                        m = e.matmul(PS[32 * j:32 * j + 32, i % 4, s * PW:(s + 1) * PW], tok[:, :, t],
                                     w("L1W")[:, j * PW:(j + 1) * PW], start=True, stop=True, skip_group_check=True)
                m.then_inc(g_p, 1)
            e.wait_ge(g_oT, 1)
            for q in range(NQ):
                if q >= 2:
                    e.wait_ge(x_upd, 8 + q - 1)
                for i in range(4):
                    for c in range(2):
                        m = e.matmul(PS[CH * c:CH * c + CH, 6 + q % 2, i * P:(i + 1) * P], oT[:, :, 2 * (4 * q + i) + c],
                                     w("L1Wo"), start=True, stop=True, skip_group_check=True)
                m.then_inc(g_out, 1)
                if q >= 1:
                    ln_turn(e, 3, q - 1)
            ln_turn(e, 3, NQ - 1)

        def delta_act(e):
            for i in range(NG):
                n = min(3, CH - 3 * i)
                e.wait_ge(g_p, i + 1)
                e.activation(pr[:, 3 * i:3 * i + n, :].rearrange("p t c -> p (t c)"), PS[:, i % 4, 0:n * PW], ACT.Copy)\
                 .then_inc(g_pr, 1)
            e.wait_ge(g_pr, NG)
            e.activation(beta, pr[:, :, 4 * LD:4 * LD + LH], ACT.Sigmoid).then_inc(g_act, 1)
            e.wait_ge(g_dve, 1)
            e.activation(ss, ss, ACT.Sqrt).then_inc(g_act, 1)
            e.wait_ge(g_dve, 2)
            e.activation(da, dz, ACT.Abs).then_inc(g_act, 1)
            e.wait_ge(g_act, 3)
            e.activation(da, da, ACT.Exp, scale=-1.0).then_inc(g_act, 1)
            e.activation(eA, w("Alog"), ACT.Exp).then_inc(g_act, 1)
            e.wait_ge(g_dve, 3)
            e.activation(da, da, ACT.Ln).then_inc(g_act, 1)
            e.wait_ge(g_dve, 6)
            e.activation(alp, dec, ACT.Exp).then_inc(g_act, 1)
            e.activation(eg, gc, ACT.Exp).then_inc(g_act, 1)
            e.activation(pr[:, :, 3 * LD:4 * LD], pr[:, :, 3 * LD:4 * LD], ACT.Silu).then_inc(g_gate, 1)
            e.wait_ge(g_act, 8)
            e.activation(Uo[:, :, 128], eg[:, CH - 1, :], ACT.Copy).then_inc(g_Uo, 1)
            def decay(t, par):
                for h in range(LH):
                    if h % 2 == 0:
                        e.wait_ge(l_R, 2 * t + h // 2 + 1)
                    cols = slice(h * RC // LH, (h + 1) * RC // LH)
                    e.activation(Ra[:, cols], Rs[1 - par][:, cols], ACT.Copy, scale=alp[:, t, h:h + 1]).then_inc(l_Ra, 1)

            e.wait_ge(g_ready, 1)
            for t in range(CH):
                decay(t, t % 2)
            e.wait_ge(l_R, 2 * CH + 2)
            e.activation(Uo[:, :, 0:128], Rs[(CH - 1) % 2].rearrange("p (h w) -> p h w", h=LH), ACT.Copy).then_inc(g_Uo, 1)
            e.wait_ge(g_o, 1)
            e.activation(qeg, og, ACT.Square).then_inc(g_norm, 1)
            e.wait_ge(g_norm, 2)
            e.activation(ss[:, :, 0:LH], ss[:, :, 0:LH], ACT.Sqrt).then_inc(g_norm, 1)
            for q in range(NQ):
                ln_root(e, 3, q)
                if q >= 1:
                    ln_store(e, 3, q - 1)
                    own(e, q - 1)
            ln_store(e, 3, NQ - 1)
            own(e, NQ - 1)

        def delta_pool(e):
            e.memset(ones, 1.0).then_inc(g_pool, 1)
            for c in range(NQ):
                ts = slice(c * CH // NQ, (c + 1) * CH // NQ)
                e.wait_ge(g_pr, ((c + 1) * CH // NQ + 2) // 3)
                e.tensor_tensor(Zs[:, ts, :], pr[:, ts, 0:2 * LD], pr[:, ts, 0:2 * LD], ALU.mult).then_inc(g_sq, 1)
            e.wait_ge(g_p, NG)
            e.memset(hT[:, :, 0:PAD], 0.0).then_inc(h_pad, 1)
            e.wait_ge(g_dve, 5)
            e.tensor_tensor(h4(kn), col(pr, LD), per_head(rs[:, :, 4:8]), ALU.mult).then_inc(g_pool, 1)
            e.wait_ge(g_act, 8)
            e.tensor_tensor(ba, beta, alp, ALU.mult).then_inc(g_pool, 1)
            e.tensor_tensor(be, beta, eg, ALU.mult).then_inc(g_pool, 1)
            e.wait_ge(g_pool, 4)
            e.tensor_tensor(h4(kba), h4(kn), per_head(ba), ALU.mult).then_inc(g_pool, 1)
            e.wait_ge(g_pool, 5)

            def products(t):
                e.wait_ge(l_R, 2 * t + 4)
                if t >= 1:
                    e.wait_ge(l_r4, t)
                e.tensor_tensor(rq.rearrange("p (h c d) -> p h c d", h=LH, d=DH),
                                Rs[t % 2].rearrange("p (h c d) -> p h c d", h=LH, d=DH),
                                bc(qn[:, t, :].rearrange("p (h o d) -> p h o d", h=LH, o=1), [P, LH, 2 * DH, DH]),
                                ALU.mult).then_inc(l_rq, 1)

            def sum4(t):
                e.wait_ge(l_rq, t + 1)
                if t >= 2:
                    e.wait_ge(l_r2, t - 1)
                v = rq.rearrange("p (n d) -> p n d", d=8)
                e.tensor_tensor(rq4[t % 2], v[:, :, 0:4], v[:, :, 4:8], ALU.add).then_inc(l_r4, 1)

            def sum2(t):
                e.wait_ge(l_r4, t + 1)
                if t >= 1:
                    e.wait_ge(l_z, t)
                e.tensor_tensor(rq2, rq4[t % 2][:, :, 0:2], rq4[t % 2][:, :, 2:4], ALU.add).then_inc(l_r2, 1)

            def sum1(t):
                e.wait_ge(l_r2, t + 1)
                e.tensor_tensor(Z[:, t, :, :].rearrange("p h c -> p (h c)"), rq2[:, :, 0], rq2[:, :, 1], ALU.add)\
                 .then_inc(l_z, 1)

            e.wait_ge(g_ready, 1)
            for t in range(CH + 1):
                if t < CH:
                    products(t)
                if t >= 1:
                    sum2(t - 1)
                if t < CH:
                    sum4(t)
                if t >= 1:
                    sum1(t - 1)
            e.wait_ge(l_z, CH)
            e.wait_ge(g_SL, 128)
            e.wait_ge(g_w, 4)
            e.tensor_tensor(oS[1].rearrange("p (t e d) -> p t e d", t=CH, e=DH),
                            bc(qeg[:, :, 3 * DH:4 * DH].rearrange("p t (o d) -> p t o d", o=1), [P, CH, DH, DH]),
                            bc(SL[:, 3, :].rearrange("p (o e d) -> p o e d", o=1, e=DH), [P, CH, DH, DH]),
                            ALU.mult).then_inc(g_os, 1)
            e.wait_ge(g_gate, 1)
            e.tensor_tensor(col(pr, 3 * LD), col(pr, 3 * LD),
                            bc(w("normw").rearrange("p (o q d) -> p o q d", o=1, q=1), [P, CH, LH, DH]), ALU.mult)\
             .then_inc(g_gate, 1)
            e.wait_ge(g_gate, 2)
            e.wait_ge(g_o, 1)
            e.tensor_tensor(pr[:, :, 3 * LD:4 * LD], pr[:, :, 3 * LD:4 * LD], og, ALU.mult).then_inc(g_gate, 1)

        def delta_dve(e):
            for c in range(NQ):
                ts = slice(c * CH // NQ, (c + 1) * CH // NQ)
                e.wait_ge(g_sq, c + 1)
                e.tensor_reduce(ss[:, ts, :], Zs[:, ts, :].rearrange("p t (h d) -> p t h d", d=DH), AX, ALU.add)\
                 .then_inc(g_ss, 1)
            e.wait_ge(g_ss, NQ)
            e.tensor_scalar(ss, ss, EPS_NORM, None, ALU.add).then_inc(g_dve, 1)
            e.tensor_tensor(dz, pr[:, :, 4 * LD + LH:PW], bc(w("dtb").rearrange("p (o h) -> p o h", o=1), [P, CH, LH]),
                            ALU.add).then_inc(g_dve, 1)
            e.wait_ge(g_act, 4)
            e.tensor_scalar(da, da, 1.0, None, ALU.add).then_inc(g_dve, 1)
            e.wait_ge(g_act, 2)
            e.reciprocal(rs, ss).then_inc(g_dve, 1)
            e.wait_ge(g_dve, 4)
            e.tensor_scalar(rs[:, :, 0:LH], rs[:, :, 0:LH], float(DH) ** -0.5, None, ALU.mult).then_inc(g_dve, 1)
            e.wait_ge(g_act, 6)
            e.scalar_tensor_tensor(dsp, dz, 0.0, da, ALU.max, ALU.add).then_inc(g_norm0, 1)
            e.wait_ge(g_norm0, 1)
            e.scalar_tensor_tensor(dec, dsp, -1.0, bc(eA.rearrange("p (o h) -> p o h", o=1), [P, CH, LH]),
                                   ALU.mult, ALU.mult).then_inc(g_norm0, 1)
            e.wait_ge(g_norm0, 2)
            e.wait_ge(g_pool, 1)
            for h in range(LH):
                m = e.tensor_tensor_scan(gc[:, :, h], ones, dec[:, :, h], 0.0, ALU.mult, ALU.add)
            m.then_inc(g_dve, 1)
            e.wait_ge(g_dve, 5)
            e.tensor_tensor(h4(qn), col(pr, 0), per_head(rs[:, :, 0:4]), ALU.mult).then_inc(g_dve, 1)
            e.wait_ge(g_act, 8)
            e.tensor_tensor(bb[:, :, :, 0:DH], col(pr, 2 * LD), per_head(beta), ALU.mult).then_inc(g_dve, 1)
            e.wait_ge(g_pool, 4)
            e.tensor_tensor(bb[:, :, :, DH:2 * DH], h4(kn), per_head(be), ALU.mult).then_inc(g_dve, 1)
            e.wait_ge(g_dve, 7)
            e.tensor_tensor(h4(qeg), h4(qn), per_head(eg), ALU.mult).then_inc(g_dve, 1)
            e.memset(Rs[1], 0.0).then_inc(l_R, 2)
            e.wait_ge(g_pool, 5)
            e.wait_ge(g_dve, 10)
            e.memset(ry, 0.0).then_inc(g_ready, 1)

            def part(ap, g):
                return ap[:, g * RC // 2:(g + 1) * RC // 2].rearrange("p (h c d) -> p h c d", h=2, d=DH)

            def feats(ap, t, g):
                return bc(ap[:, t, g * LD // 2:(g + 1) * LD // 2].rearrange("p (h o d) -> p h o d", h=2, o=1),
                          [P, 2, 2 * DH, DH])

            def step(t, par):
                for g in range(2):
                    e.wait_ge(l_R, 2 * t + g + 1)
                    e.tensor_tensor(part(rk, g), part(Rs[1 - par], g), feats(kba, t, g), ALU.mult).then_inc(l_rk, 1)
                for g in range(2):
                    c = slice(g * LD, (g + 1) * LD)
                    e.wait_ge(l_rk, 2 * t + g + 1)
                    e.tensor_reduce(ry[:, c], part(rk, g), AX, ALU.add).then_inc(l_y, 1)
                for g in range(2):
                    c = slice(g * LD, (g + 1) * LD)
                    e.wait_ge(l_y, 2 * t + g + 1)
                    e.tensor_tensor(rx[:, c], ry[:, c], bb[:, t, 2 * g:2 * g + 2, :].rearrange("p h c -> p (h c)"), ALU.add)\
                     .then_inc(l_x, 1)
                for g in range(2):
                    c = slice(g * LD, (g + 1) * LD)
                    e.wait_ge(l_x, 2 * t + g + 1)
                    e.tensor_tensor(part(ro, g), bc(rx[:, c].rearrange("p (h c o) -> p h c o", h=2, o=1), [P, 2, 2 * DH, DH]),
                                    feats(kn, t, g), ALU.mult).then_inc(l_o, 1)
                if t >= 2:
                    e.wait_ge(l_rq, t - 1)
                for g in range(2):
                    c = slice(g * RC // 2, (g + 1) * RC // 2)
                    e.wait_ge(l_o, 2 * t + g + 1)
                    e.wait_ge(l_Ra, LH * t + 2 * g + 2)
                    e.tensor_tensor(Rs[par][:, c], Ra[:, c], ro[:, c], ALU.add).then_inc(l_R, 1)

            e.wait_ge(g_ready, 1)
            for t in range(CH):
                step(t, t % 2)

            e.memset(SH[0:32, 0, :], 0.0).then_inc(g_chain, 1)
            e.wait_ge(l_z, CH)
            e.tensor_tensor(h4(qeg), h4(qeg), Z[:, :, :, DH:2 * DH], ALU.subtract).then_inc(g_w, 1)
            e.wait_ge(g_Ui, 128)
            k = 1
            for n in range(NC1 - 1):
                S = SH[0:32, n, :]
                e.wait_ge(g_chain, k)
                e.tensor_tensor(sm[0:32].rearrange("p (e d i) -> p e d i", e=DH, d=DH),
                                bc(Ui[0:32, n, 64:128].rearrange("p (o i d) -> p o d i", o=1, i=DH), [32, DH, DH, DH]),
                                bc(S.rearrange("p (e o i) -> p e o i", e=DH, o=1), [32, DH, DH, DH]), ALU.mult)\
                 .then_inc(g_chain, 1)
                e.wait_ge(g_chain, k + 1)
                e.tensor_reduce(sr_[0:32], sm[0:32].rearrange("p (n i) -> p n i", i=DH), AX, ALU.add).then_inc(g_chain, 1)
                e.wait_ge(g_chain, k + 2)
                e.scalar_tensor_tensor(sv_[0:32], S, Ui[0:32, n, 128:129], sr_[0:32], ALU.mult, ALU.subtract)\
                 .then_inc(g_chain, 1)
                e.wait_ge(g_chain, k + 3)
                e.tensor_tensor(SH[0:32, n + 1, :], sv_[0:32], Ui[0:32, n, 0:64], ALU.add).then_inc(g_chain, 1)
                k += 4

            e.wait_ge(g_SL, 128)
            e.wait_ge(g_w, 4)
            for h in range(LH):
                buf = oS[0] if h < 3 else oS[1]
                if h < 3:
                    e.tensor_tensor(buf.rearrange("p (t e d) -> p t e d", t=CH, e=DH),
                                    bc(qeg[:, :, h * DH:(h + 1) * DH].rearrange("p t (o d) -> p t o d", o=1), [P, CH, DH, DH]),
                                    bc(SL[:, h, :].rearrange("p (o e d) -> p o e d", o=1, e=DH), [P, CH, DH, DH]),
                                    ALU.mult).then_inc(g_om, 1)
                    e.wait_ge(g_om, 2 * h + 1)
                else:
                    e.wait_ge(g_os, 1)
                e.tensor_reduce(og[:, :, h * DH:(h + 1) * DH], buf.rearrange("p (t e d) -> p t e d", t=CH, e=DH), AX,
                                ALU.add).then_inc(g_om, 1)
                e.wait_ge(g_om, min(2 * h + 2, 7))
            e.tensor_tensor(h4(og), h4(og), Z[:, :, :, 0:DH], ALU.add).then_inc(g_o, 1)
            e.wait_ge(g_norm, 1)
            e.tensor_reduce(rs[:, :, 0:LH], h4(qeg), AX, ALU.add).then_inc(g_om, 1)
            e.wait_ge(g_om, 8)
            e.tensor_scalar(ss[:, :, 0:LH], rs[:, :, 0:LH], 1.0 / DH, EPS_RMS, ALU.mult, ALU.add).then_inc(g_norm, 1)
            e.wait_ge(g_norm, 3)
            e.reciprocal(rs[:, :, 4:8], ss[:, :, 0:LH]).then_inc(g_om, 1)
            e.wait_ge(g_om, 9)
            e.wait_ge(g_gate, 3)
            e.tensor_tensor(h4(og), col(pr, 3 * LD), per_head(rs[:, :, 4:8]), ALU.mult).then_inc(g_norm, 1)
            e.wait_ge(g_norm, 4)
            e.transpose(oT.rearrange("p t l -> p (t l)"), og.rearrange("p t c -> p (t c)")).then_inc(g_oT, 1)
            for i, (mu, _) in enumerate(LERP):
                e.tensor_scalar(omu[:, i:i + 1], w(mu), -1.0, 1.0, ALU.mult, ALU.add).then_inc(h_omu, 1)
            e.wait_ge(h_omu, 2)
            e.wait_ge(h_pad, 1)
            for q in range(NQ):
                e.wait_ge(g_out, q + 1)
                xs = X[:, 4 * q:4 * q + 4, :]
                e.tensor_tensor(xs, PS[:, 6 + q % 2, :].rearrange("p (j d) -> p j d", j=4), xs, ALU.add).then_inc(x_upd, 1)
                ln_moments(e, 3, q)
                if q >= 1:
                    ln_scale(e, 3, q - 1)
                if q >= 2:
                    shift(e, q - 2)
            ln_scale(e, 3, NQ - 1)
            shift(e, NQ - 2)
            shift(e, NQ - 1)

        LERP = (("mur", xr), ("muk", xk))

        def own(e, q):
            e.wait_ge(ln_hT, 12 + q + 1)
            for mu, dst in LERP:
                e.activation(dst[:, q * SEG:(q + 1) * SEG], hslice(q), ACT.Copy, scale=w(mu)).then_inc(h_own, 1)

        def shift(e, q):
            b, o = divmod(q * SEG, T)
            cols = slice(q * SEG, (q + 1) * SEG)
            for i, (_, dst) in enumerate(LERP):
                e.wait_ge(h_own, 2 * q + i + 1)
                e.scalar_tensor_tensor(dst[:, cols], hT[:, b, PAD + o - 1:PAD + o - 1 + SEG], omu[:, i:i + 1],
                                       dst[:, cols], ALU.mult, ALU.add).then_inc(h_mix, 1)

        def mix_dve(e):
            for q in range(NQ + 1):
                if q < NQ:
                    e.wait_ge(h_rl, q + 1)
                    if q >= 2:
                        e.wait_ge(h_v, q - 1)
                    e.tensor_tensor(ka[q % 2], PS[:, q % 2, :], rl[q % 2], ALU.mult).then_inc(h_ka, 1)
                if q >= 1:
                    p_ = q - 1
                    e.wait_ge(h_v, p_ + 1)
                    e.wait_ge(h_sr, p_ + 1)
                    e.tensor_tensor(rv[p_ % 2], PS[:, 4 + p_ % 2, :], sgr[p_ % 2], ALU.mult).then_inc(h_rv, 1)
                    e.wait_ge(h_rv, p_ + 1)
                    xs = X[:, 4 * p_:4 * p_ + 4, :]
                    e.tensor_tensor(xs, rv[p_ % 2].rearrange("p (j d) -> p j d", j=4), xs, ALU.add).then_inc(h_x, 1)

        def mix_pe(e):
            for q in range(NQ + 1):
                if q < NQ:
                    e.wait_ge(h_mix, 2 * q + 2)
                    if q >= 2:
                        e.wait_ge(h_ka, q - 1)
                        e.wait_ge(h_sr, q - 1)
                    e.matmul(PS[:, q % 2, :], w("WkT2"), xk[:, q * SEG:(q + 1) * SEG], start=True, stop=True).then_inc(h_k, 1)
                    for i in range(4):
                        a = q * SEG + i * P
                        m = e.matmul(PS[:, 2 + q % 2, i * P:(i + 1) * P], xr[:, a:a + P], w("WrT"), start=True, stop=True,
                                     skip_group_check=True)
                    m.then_inc(h_r, 1)
                if q >= 1:
                    p_ = q - 1
                    e.wait_ge(h_ka, p_ + 1)
                    if p_ >= 2:
                        e.wait_ge(h_rv, p_ - 1)
                    for i in range(4):
                        m = e.matmul(PS[:, 4 + p_ % 2, i * P:(i + 1) * P], ka[p_ % 2][:, i * P:(i + 1) * P], w("WvT2"),
                                     start=True, stop=True, skip_group_check=True)
                    m.then_inc(h_v, 1)

        def mix_act(e):
            for q in range(NQ):
                e.wait_ge(h_k, q + 1)
                if q >= 2:
                    e.wait_ge(h_ka, q - 1)
                e.activation(rl[q % 2], PS[:, q % 2, :], ACT.Relu).then_inc(h_rl, 1)
                e.wait_ge(h_r, q + 1)
                if q >= 2:
                    e.wait_ge(h_rv, q - 1)
                e.activation(sgr[q % 2], PS[:, 2 + q % 2, :], ACT.Sigmoid).then_inc(h_sr, 1)

        def turn64(e, bank, src, q):
            for i in range(4):
                for c in range(2):
                    for p in range(2):
                        r = slice(CH * p, CH * p + CH)
                        m = e.matmul(PS[r, bank, i * P + CH * c:i * P + CH * c + CH],
                                     src[r, 4 * q + i, CH * c:CH * c + CH], ident[r, CH * p:CH * p + CH],
                                     start=True, stop=True, skip_group_check=True)
            return m

        @block.sync
        def _(e):
            xv = x_dram.rearrange("b (t p) d -> p (b t) d", p=P)
            for q in range(NQ):
                e.dma_start(X[:, 4 * q:4 * q + 4, :], xv[:, 4 * q:4 * q + 4, :]).then_inc(x_in, 16)
            e.dma_start(C[:, :], c_dram).then_inc(c_in, 16)
            e.dma_start(W[:, :], w_dram).then_inc(w_in, 16)
            e.dma_start(wk5[:, 0:P], wk_dram).then_inc(w_in, 16)
            e.dma_start(wv5[:, 0:P], wv_dram).then_inc(w_in, 16)
            e.wait_ge(zeroed, 2)
            for s in range(NQ):
                e.wait_ge(b_qT, s + 1)
                if s >= 2:
                    e.wait_ge(c_S, 16 * (s - 1))
                for h in range(NH):
                    r = slice(DH * h, DH * h + DH)
                    e.dma_start(qbd[s % 2][r, h, :], qT[r, s * SEG:(s + 1) * SEG]).then_inc(c_qbd[s], 16)
            for s in range(NQ):
                e.wait_ge(b_qf, s + 1)
                if s < 2:
                    e.wait_ge(c_S, 16 * (s + 3))
                else:
                    e.wait_ge(d_S, 40 * (s - 1))
                for h in range(NH):
                    r = slice(DH * h, DH * h + DH)
                    e.dma_start(qbd[s % 2][r, h, :], qf[r, s * SEG:(s + 1) * SEG]).then_inc(d_qbd[s], 16)
            ov = out_dram.rearrange("b (t p) d -> p (b t) d", p=P)
            e.wait_ge(g_Uo, 2)
            e.dma_start(u_dram, Uo).then_inc(g_Ud, 16)
            e.wait_ge(g_Ud, 16)
            e.wait_ge(l_z, CH)
            for jb in range(8):
                e.dma_start(Ui[4 * jb:4 * jb + 4, :, :], u_dram[16 * jb:16 * jb + 16, :, :].rearrange("n h w -> h n w"))\
                 .then_inc(g_Ui, 16)
            e.wait_ge(g_chain, 4 * (NC1 - 1) + 1)
            e.dma_start(s_dram, SH[0:32, :, :]).then_inc(g_Sd, 16)
            e.wait_ge(g_Sd, 16)
            for jb in range(8):
                e.dma_start(SL[16 * jb:16 * jb + 16, :, :], s_dram[4 * jb:4 * jb + 4, :, :].rearrange("h n w -> n h w"))\
                 .then_inc(g_SL, 16)
            for q in range(NQ):
                e.wait_ge(h_x, q + 1)
                e.dma_start(ov[:, 4 * q:4 * q + 4, :], X[:, 4 * q:4 * q + 4, :]).then_inc(y_out, 16)
            e.wait_ge(y_out, 16 * NQ)

        @block.gpsimd
        def _(e):
            e.memset(qbd[0], 0.0).then_inc(zeroed, 1)
            e.memset(qbd[1], 0.0).then_inc(zeroed, 1)
            e.memset(hT[:, :, 0:PAD], 0.0).then_inc(zeroed, 1)
            e.memset(klT[:, :, 0:PAD], 0.0).then_inc(b_klT_pad, 1)
            e.memset(v9l[:, :, :, DH:DE], 1.0).then_inc(b_klT_pad, 1)
            e.wait_ge(c_in, 16)
            e.wait_ge(w_in, 48)
            e.wait_ge(ln_h, NT)
            e.tensor_tensor(X[:, :, :], X[:, :, :], w("bo").rearrange("p (o d) -> p o d", o=1).to_broadcast([P, NT, P]),
                            ALU.add).then_inc(xbo, 1)
            for q in range(NQ):
                e.wait_ge(b_qe, q + 1)
                e.tensor_scalar(qf[:, q * SEG:(q + 1) * SEG], qf[:, q * SEG:(q + 1) * SEG], 1.0, None,
                                ALU.min).then_inc(b_qm, 1)
            e.wait_ge(c_loc, NT)
            for par in range(2):
                e.memset(V9[par], 0.0).then_inc(v9_zero, 1)
            e.memset(SB[:, 0, :, :], 0.0).then_inc(zeroed, 1)
            e.wait_ge(v9_zero, 2)
            for par in range(2):
                e.tensor_copy(V9[par].rearrange("p c l (h e) -> p c (l h) e", e=DE)[:, :, :, DH],
                              cst("half").rearrange("p (c o) -> p c o", o=1).to_broadcast([P, 2, LV * NH]))\
                 .then_inc(v9_ones, 1)
            for j in range(NT):
                prep_pool(e, j)
            for q in range(NQ):
                e.wait_ge(d_glob, 4 * q + 4)
                e.wait_ge(d_av, 10 * NT)
                e.tensor_tensor(diff[:, 4 * q:4 * q + 4, :], loc[:, 4 * q:4 * q + 4, :], glob[:, 4 * q:4 * q + 4, :],
                                ALU.subtract).then_inc(e_diff, 1)
            e.wait_ge(x_upd, 8)
            delta_pool(e)

        @block.scalar
        def _(e):
            e.wait_ge(c_in, 16)
            e.activation(identb[:, :], ident, ACT.Copy).then_inc(cb_ready, 1)
            e.activation(nmaskb[:, 0, :], cst("nmask0"), ACT.Copy).then_inc(cb_ready, 1)
            e.activation(nmaskb[:, 1, :], cst("nmask"), ACT.Copy).then_inc(cb_ready, 1)
            for q in range(NQ):
                ln_root(e, 0, q)
            for q in range(NQ):
                ln_store(e, 0, q)
            for i, t in enumerate((wk5, wv5)):
                e.wait_ge(b_comb, i + 1)
                e.activation(t[:, P:LV * P], PS[:, i, :], ACT.Copy).then_inc(b_w5, 2)
            for q in range(NQ):
                e.wait_ge(b_q, q + 1)
                cols = slice(q * SEG, (q + 1) * SEG)
                e.activation(qT[:, cols], PS[:, 2 + q, :], ACT.Copy).then_inc(b_qT, 1)
                e.activation(qf[:, cols], PS[:, 2 + q, :], ACT.Exp).then_inc(b_qe, 1)
            for q in range(NQ):
                e.wait_ge(b_kl, q + 1)
                b, o = divmod(q * SEG, T)
                e.activation(klT[:, b, PAD + o:PAD + o + SEG], PS[:, 6 + q % 2, :], ACT.Copy).then_inc(b_klT, 1)
            for i in range(8):
                e.wait_ge(b_vl, i + 1)
                if i == 0:
                    e.wait_ge(b_klT_pad, 2)
                e.activation(v9l[:, 4 * i:4 * i + 4, :, 0:DH].rearrange("p w h e -> p (w h) e"),
                             PS[:, i % 2, :].rearrange("p (h e) -> p h e", e=DH), ACT.Copy).then_inc(b_v9, 1)
            e.wait_ge(b_sw, 2)
            e.activation(hsw[:, 8:12], hsw[:, 4:8], ACT.Exp).then_inc(b_sw, 1)
            local_act(e)
            e.wait_ge(zeroed, 4)
            e.wait_ge(v9_ones, 2)
            for j in range(NT):
                prep_act(e, j)
            e.wait_ge(d_glob, NT)
            for q in range(NQ):
                e.wait_ge(e_dT, q + 1)
                e.activation(dT[q % 2], PS[:, q % 2, :], ACT.Copy).then_inc(e_dTs, 1)
                e.wait_ge(e_g, q + 1)
                e.activation(gh[q % 2], PS[:, 2 + q % 2, :], ACT.Silu, bias=w("bg")).then_inc(e_gh, 1)
                e.wait_ge(e_al, q + 1)
                e.activation(alpha[:, 8 * q:8 * q + 8], PS[:, 4 + q % 2, 0:8], ACT.Sigmoid, bias=w("bgo")).then_inc(e_alpha, 1)
            for q in range(NQ + 1):
                if q < NQ:
                    e.wait_ge(e_mT, q + 1)
                    if q >= 2:
                        e.wait_ge(e_out, q - 1)
                    e.activation(mixT[q % 2], PS[:, 6, :], ACT.Copy).then_inc(e_mTs, 1)
                if q >= 1:
                    ln_root(e, 1, q - 1)
                if q >= 2:
                    ln_store(e, 1, q - 2)
            ln_store(e, 1, NQ - 1)
            moe_act(e)
            delta_act(e)
            mix_act(e)

        @block.tensor
        def _(e):
            for q in range(NQ):
                ln_turn(e, 0, q)
            e.wait_ge(w_in, 48)
            e.wait_ge(zeroed, 3)
            for i, (a, b) in enumerate((("Wk", "HBk"), ("Wv", "HBv"))):
                e.matmul(PS[:, i, :], w(a), w(b), start=True, stop=True).then_inc(b_comb, 1)
            e.wait_ge(ln_hT, 4)
            for q in range(NQ):
                e.matmul(PS[:, 2 + q, :], w("WqT"), hslice(q), start=True, stop=True).then_inc(b_q, 1)
            for q in range(NQ):
                if q >= 2:
                    e.wait_ge(b_klT, q - 1)
                e.matmul(PS[:, 6 + q % 2, :], w("WklT"), hslice(q), start=True, stop=True).then_inc(b_kl, 1)
            e.wait_ge(b_w5, 4)
            for i in range(8):
                if i >= 2:
                    e.wait_ge(b_v9, i - 1)
                for k in range(4):
                    b, c = divmod(4 * i + k, NC1)
                    m = e.matmul(PS[:, i % 2, k * P:(k + 1) * P], hT[:, b, CH * c:CH * c + P], w("WvlT"),
                                 start=True, stop=True, skip_group_check=True)
                m.then_inc(b_vl, 1)
            e.wait_ge(b_qf, NQ)
            local_pe(e)
            linear_pe(e)
            e.wait_ge(d_glob, NT)
            for q in range(NQ):
                e.wait_ge(e_diff, q + 1)
                if q >= 2:
                    e.wait_ge(e_dTs, q - 1)
                m = turn64(e, q % 2, diff, q)
                m.then_inc(e_dT, 1)
                e.wait_ge(e_dTs, q + 1)
                if q >= 2:
                    e.wait_ge(e_gh, q - 1)
                e.matmul(PS[:, 2 + q % 2, :], w("WgTa"), hslice(q), start=True, stop=False)
                e.matmul(PS[:, 2 + q % 2, :], w("WgTb"), dT[q % 2], start=False, stop=True).then_inc(e_g, 1)
                e.wait_ge(e_gh, q + 1)
                if q >= 2:
                    e.wait_ge(e_alpha, q - 1)
                for i in range(8):
                    for p in range(2):
                        m = e.matmul(PS[CH * p:CH * p + CH, 4 + q % 2, i:i + 1], gh[q % 2][:, i * CH:(i + 1) * CH], w("WgoT"),
                                     start=True, stop=True, skip_group_check=True)
                m.then_inc(e_al, 1)
            e.wait_ge(e_mix, 8)
            turn64(e, 6, mix, 0).then_inc(e_mT, 1)
            for q in range(NQ):
                e.wait_ge(e_mTs, q + 1)
                if q + 1 < NQ:
                    e.wait_ge(e_mix, 8 * q + 16)
                    turn64(e, 6, mix, q + 1).then_inc(e_mT, 1)
                if q >= 1:
                    e.wait_ge(x_upd, q)
                for i in range(4):
                    m = e.matmul(PS[:, 7, i * P:(i + 1) * P], mixT[q % 2][:, i * P:(i + 1) * P], w("WoT"),
                                 start=True, stop=True, skip_group_check=True)
                m.then_inc(e_out, 1)
                if q >= 1:
                    ln_turn(e, 1, q - 1)
            ln_turn(e, 1, NQ - 1)
            moe_pe(e)
            delta_pe(e)
            mix_pe(e)

        @block.vector
        def _(e):
            ln_moments(e, 0, 0)
            for q in range(NQ):
                if q + 1 < NQ:
                    ln_moments(e, 0, q + 1)
                ln_scale(e, 0, q)
            e.wait_ge(w_in, 48)
            hs = w("hscale")
            e.tensor_reduce(hsw[:, 16:17], hs, AX, ALU.max).then_inc(b_sw, 1)
            e.wait_ge(b_sw, 1)
            e.tensor_scalar(hsw[:, 4:8], hs, hsw[:, 16:17], None, ALU.subtract).then_inc(b_sw, 1)
            for q in range(NQ):
                e.wait_ge(b_qm, q + 1)
                cols = slice(q * SEG, (q + 1) * SEG)
                e.scalar_tensor_tensor(qf[:, cols], PS[:, 2 + q, :], 1.0, qf[:, cols], ALU.add, ALU.max).then_inc(b_qf, 1)
            e.wait_ge(b_sw, 3)
            e.tensor_reduce(hsw[:, 17:18], hsw[:, 8:12], AX, ALU.add).then_inc(b_sw, 1)
            e.wait_ge(b_sw, 4)
            e.reciprocal(hsw[:, 18:19], hsw[:, 17:18]).then_inc(b_sw, 1)
            e.memset(hsw[:, 0:1], 1.0).then_inc(b_sw, 1)
            e.wait_ge(b_sw, 6)
            e.tensor_scalar(hsw[:, 1:5], hsw[:, 8:12], hsw[:, 18:19], None, ALU.mult).then_inc(b_sw, 1)
            e.wait_ge(b_sw, 7)
            local_dve(e)
            linear_dve(e)
            for q in range(NQ):
                e.wait_ge(e_alpha, q + 1)
                for i in range(8):
                    j, cols = 4 * q + i // 2, slice(CH * (i % 2), CH * (i % 2) + CH)
                    e.scalar_tensor_tensor(mix[:, j, cols], diff[:, j, cols], alpha[:, 8 * q + i:8 * q + i + 1],
                                           glob[:, j, cols], ALU.mult, ALU.add).then_inc(e_mix, 1)
            e.wait_ge(xbo, 1)
            for q in range(NQ):
                e.wait_ge(e_out, q + 1)
                xs = X[:, 4 * q:4 * q + 4, :]
                e.tensor_tensor(xs, PS[:, 7, :].rearrange("p (j d) -> p j d", j=4), xs, ALU.add).then_inc(x_upd, 1)
                ln_moments(e, 1, q)
                ln_scale(e, 1, q)
            moe_dve(e)
            delta_dve(e)
            mix_dve(e)


def kernel(**inputs):
    import numpy as np
    import concourse.bacc as _bacc
    from concourse.bass_utils import run_bass_kernel_spmd as _run

    g = {k: np.ascontiguousarray(v) for k, v in inputs.items()}
    f4 = np.float32

    def bd(wl):
        out = np.zeros((NH, DH, 4, NH, DH), f4)
        for h in range(NH):
            out[h, :, :, h, :] = wl.transpose(2, 0, 1)
        return out.reshape(P, 512)

    def rows(v):
        return np.broadcast_to(v.reshape(1, -1), (P, v.size))

    def lanes(v):
        return np.repeat(v.reshape(4, LH), 32, axis=0)

    def split(wt):
        return wt.reshape(NH // 2, 2, DH, P).transpose(1, 0, 2, 3).reshape(P, P)

    a, f = "L0_attn_", "L0_ffn_"
    parts = {
        "WqT": g[a + "Wq"].T, "WklT": g[a + "Wkl"].T, "WvlT": g[a + "Wvl"].T, "Wk": g[a + "Wk"], "Wv": g[a + "Wv"],
        "HBk": bd(g[a + "haar_Wk"]), "HBv": bd(g[a + "haar_Wv"]), "hscale": rows(g[a + "haar_scale"]),
        "bo": rows(g[a + "bo"]), "WgTa": g[a + "Wg"].T[:P], "WgTb": split(g[a + "Wg"].T[P:]), "WgoT": g[a + "Wgo"].T,
        "bg": g[a + "bg"].reshape(P, 1), "bgo": rows(g[a + "bgo"]), "WoT": split(g[a + "Wo"].T),
        "gateT": g[f + "gate_w"].T, "cbias": rows(g[f + "correction_bias"]),
        "Eg": np.concatenate([g[f + "Wg"].transpose(1, 0, 2).reshape(P, 512), g[f + "Wg_s"]], 1),
        "Eu": np.concatenate([g[f + "Wu"].transpose(1, 0, 2).reshape(P, 512), g[f + "Wu_s"]], 1),
        "Ed": g[f + "Wd"].reshape(4, P, P).transpose(1, 0, 2).reshape(P, 512),
        "Eds": np.concatenate([g[f + "Wd_s"], np.zeros((64, P), f4)], 0),
        "dtb": lanes(g["L1_attn_dt_bias"]), "Alog": lanes(g["L1_attn_A_log"]), "normw": rows(g["L1_attn_norm_w"]),
        "L1Wo": g["L1_attn_Wo"],
        "WrT": g["L1_ffn_W_r"].T, "WkT2": g["L1_ffn_W_k"].T, "WvT2": g["L1_ffn_W_v"].T,
        "mur": g["L1_ffn_mu_r"].reshape(P, 1), "muk": g["L1_ffn_mu_k"].reshape(P, 1),
    }
    b = "L1_attn_"
    parts["L1W"] = np.concatenate(
        [np.concatenate([g[b + n][:, 32 * j:32 * j + 32] for n in ("Wq", "Wk", "Wv", "Wg")]
                        + [g[b + n][:, 4 * j:4 * j + 4] for n in ("Wb", "Wa")], 1) for j in range(4)], 1)
    wpack = np.concatenate([parts[n] for n, _ in W_PARTS], 1)

    s, t = np.arange(P)[:, None], np.arange(P)[None, :]
    mean = np.zeros((P, LV, P), f4)
    for i, blk in enumerate((1, 2, 4, 8, 16)):
        mean[:, i, :] = np.where((s // blk == t // blk) & (s <= t), 1.0 / (t % blk + 1), 0.0)
    qq = s % CH
    ok = (t <= qq + CH) & (t > qq)
    consts = {
        "ident": np.eye(P, dtype=f4), "mean": mean.reshape(P, -1),
        "tri": (qq <= np.arange(CH)[None, :]).astype(f4),
        "hmask": (s // DH == np.arange(NH)[None, :]).astype(f4),
        "nmask": np.where(ok, 0.0, -1e30).astype(f4),
        "low4": rows(np.tril(np.ones((4, 4), f4), -1)), "low8": rows(np.tril(np.ones((NE, NE), f4), -1)),
        "half": (s // CH == np.arange(2)[None, :]).astype(f4),
        "nmask0": np.where(ok & ((s >= CH) | (t >= CH)), 0.0, -1e30).astype(f4),
    }
    cpack = np.concatenate([consts[n] for n, _ in C_PARTS], 1).astype(f4)

    nc = _bacc.Bacc("TRN2", target_bir_lowering=False, num_devices=1)
    arrays = {"x": g["L0_attn_x"], "wpack": np.ascontiguousarray(wpack), "wkT": np.ascontiguousarray(g[a + "Wk"].T),
              "wvT": np.ascontiguousarray(g[a + "Wv"].T), "cpack": np.ascontiguousarray(cpack)}
    dram = {n: nc.dram_tensor(n, v.shape, F32, kind="ExternalInput").ap() for n, v in arrays.items()}
    out = nc.dram_tensor("out", (NB, T, P), F32, kind="ExternalOutput").ap()
    u = nc.dram_tensor("carry_out", (P, LH, 2 * DH * DH + 1), F32).ap()
    sd = nc.dram_tensor("carry_in", (32, NC1, DH * DH), F32).ap()
    program(nc, dram["x"], dram["wpack"], dram["wkT"], dram["wvT"], dram["cpack"], out, u, sd)
    return _run(nc, [arrays], core_ids=[0]).results[0]["out"]
```

```python
from contextlib import ExitStack

import concourse.bass as bass
from concourse import mybir

F32 = mybir.dt.float32
BF16 = mybir.dt.bfloat16
ALU = mybir.AluOpType
ACT = mybir.ActivationFunctionType
AX = mybir.AxisListType.X

P = 128
NB, T = 2, 1024
NT = NB * T // P
NH, DH = 16, 8
CH = 64
PAD = 64
LV = 5
SEG = 512
NQ = NB * T // SEG
DE = DH + 1
NE = 8
EPS_LN, EPS_LIN, EPS_NORM, EPS_RMS = 1e-5, 1e-6, 1e-6, 1e-5
NC1 = T // CH
LH = 4
PW = 4 * LH * DH + 2 * LH

W_PARTS = [("WqT", 128), ("WklT", 128), ("WvlT", 128), ("Wk", 128), ("Wv", 128),
           ("HBk", 512), ("HBv", 512), ("hscale", 4), ("bo", 128),
           ("WgTa", 128), ("WgTb", 128), ("WgoT", 1), ("bg", 1), ("bgo", 1), ("WoT", 128),
           ("gateT", NE), ("cbias", NE), ("Eg", 576), ("Eu", 576), ("Ed", 512), ("Eds", 128),
           ("L1W", 4 * PW), ("dtb", LH), ("Alog", LH), ("normw", DH), ("L1Wo", 128),
           ("WrT", 128), ("WkT2", 128), ("WvT2", 128), ("mur", 1), ("muk", 1)]
W_OFF, _o = {}, 0
for _n, _w in W_PARTS:
    W_OFF[_n] = (_o, _o + _w)
    _o += _w
W_COLS = _o
C_PARTS = [("ident", 128), ("mean", (LV - 1) * 128), ("tri", CH), ("hmask", NH), ("nmask", 128), ("nmask0", 128), ("half", 2), ("low4", 16), ("low8", 64)]
C_OFF, _o = {}, 0
for _n, _w in C_PARTS:
    C_OFF[_n] = (_o, _o + _w)
    _o += _w
C_COLS = _o


def program(nc, x_dram, w_dram, wk_dram, wv_dram, c_dram, out_dram, u_dram, s_dram, upto=9):
    with ExitStack() as ctx:
        def sb(name, shape, dt=F32):
            return ctx.enter_context(nc.sbuf_tensor(name, shape, dt))

        def sem(name):
            return ctx.enter_context(nc.semaphore(name))

        PS = ctx.enter_context(nc.psum_tensor("PS", [P, 8, 512], F32))
        W = sb("W", [P, W_COLS])
        C = sb("C", [P, C_COLS])
        X = sb("X", [P, NT, P])
        H = sb("H", [P, NT, P])
        hT = sb("hT", [P, NB, PAD + T])
        identb = sb("identb", [P, P], BF16)
        nmaskb = sb("nmaskb", [P, 2, P], BF16)
        st = sb("st", [P, NT, 6])
        mv = sb("mv", [P, NT, 2])
        sd = sb("sd", [P, 3, NT])
        arena = sb("arena", [P, 36864])
        pos = [0]

        def take(cols):
            a = arena[:, pos[0]:pos[0] + cols]
            pos[0] += cols
            assert pos[0] <= 36864, pos[0]
            return a

        def w(name, rows=P):
            a, b = W_OFF[name]
            return W[0:rows, a:b]

        def cst(name):
            a, b = C_OFF[name]
            return C[:, a:b]

        ident = cst("ident")
        mean = cst("mean").rearrange("p (l t) -> p l t", l=LV - 1)

        qbd = [take(NH * SEG).rearrange("p (h t) -> p h t", h=NH) for _ in range(2)]
        qT = take(NB * T)
        qf = take(NB * T)
        loc_ = take(NT * P)
        loc = loc_.rearrange("p (j d) -> p j d", j=NT)
        glob_ = qT
        glob = glob_.rearrange("p (j d) -> p j d", j=NT)
        mark = pos[0]
        klT = take(NB * (PAD + T)).rearrange("p (b t) -> p b t", b=NB)
        v9l = take(NB * NC1 * NH * DE).rearrange("p (w h e) -> p w h e", w=NB * NC1, h=NH)
        prob = [take(512) for _ in range(3)]
        probT = [take(512) for _ in range(2)]
        rowmax = take(2 * 4).rearrange("p (u h) -> p u h", u=2)
        lrec = take(2 * NH).rearrange("p (u h) -> p u h", u=2)
        pos[0] = mark
        wk5 = sb("wk5", [P, LV * P])
        wv5 = sb("wv5", [P, LV * P])
        kvw = take(2 * LV * P)
        ephi = take(3 * 512).rearrange("p (u n) -> p u n", u=3)
        KF = [take(2 * LV * P).rearrange("p (a l n) -> p a l n", a=2, l=LV) for _ in range(2)]
        V9 = [take(2 * LV * NH * DE).rearrange("p (c l n) -> p c l n", c=2, l=LV) for _ in range(2)]
        AT = [take(512) for _ in range(4)]
        SB = take(4 * LV * NH * DE).rearrange("p (s l n) -> p s l n", s=4, l=LV)
        den = take(3 * LV * NH).rearrange("p (s l h) -> p s l h", s=3, l=LV)
        quo = take(LV * P).rearrange("p (l n) -> p l n", l=LV)
        hsw = sb("hsw", [P, 4 * LV])
        pos[0] = 0
        dT = [take(512) for _ in range(2)]
        gh = [take(512) for _ in range(2)]
        mix = take(NT * P).rearrange("p (j d) -> p j d", j=NT)
        mixT = [take(512) for _ in range(2)]
        diff = take(NT * P).rearrange("p (j d) -> p j d", j=NT)
        alpha = take(2 * NT)
        pos[0] = 0
        sgu = [take(512) for _ in range(3)]
        act = [take(5 * 512).rearrange("p (q n) -> p q n", q=5) for _ in range(2)]
        pos[0] = 12000
        rt_s, rt_c, rt_ch, rt_sel, rt_w, cw = (take(NT * NE).rearrange("p (j e) -> p j e", j=NT) for _ in range(6))
        rt_g, rt_gr, rt_gm = (take(NT * 4).rearrange("p (j e) -> p j e", j=NT) for _ in range(3))
        rt_p4, rt_q4 = (take(NT * 16).rearrange("p (j a b) -> p j a b", j=NT, a=4) for _ in range(2))
        rt_p8, rt_q8 = (take(NT * 64).rearrange("p (j a b) -> p j a b", j=NT, a=NE) for _ in range(2))
        rt_r8 = take(NT * NE).rearrange("p (j e) -> p j e", j=NT)
        rt_n = take(3 * NT).rearrange("p (k j) -> p k j", k=3)
        pos[0] = 0
        LD = LH * DH
        RC = LH * 2 * DH * DH
        pr = take(CH * PW).rearrange("p (t c) -> p t c", t=CH)
        ovl = take(CH * (3 * LD + LH * 2 * DH))
        kn, qn, kba = (ovl[:, i * CH * LD:(i + 1) * CH * LD].rearrange("p (t c) -> p t c", t=CH) for i in range(3))
        bb = ovl[:, 3 * CH * LD:].rearrange("p (t h c) -> p t h c", t=CH, h=LH)
        oS = [ovl[:, 0:4096], ovl[:, 3 * CH * LD:3 * CH * LD + 4096]]
        oT = ovl[:, 0:CH * LD].rearrange("p (t l) -> p t l", t=CH)
        qeg = take(CH * LD).rearrange("p (t c) -> p t c", t=CH)
        og = take(CH * LD).rearrange("p (t c) -> p t c", t=CH)
        Z_ = take(CH * LH * 2 * DH)
        Zs = Z_.rearrange("p (t c) -> p t c", t=CH)
        Z = Z_.rearrange("p (t h c) -> p t h c", t=CH, h=LH)
        Rs = [take(RC) for _ in range(2)]
        UW = 2 * 64 + 1
        late = take(4 * RC + 16)
        Ra, ro = late[:, 0:RC], late[:, RC:2 * RC]
        rkb = [take(2 * LD * DE).rearrange("p (n d) -> p n d", d=DE) for _ in range(2)]
        rq = late[:, 3 * RC:4 * RC]
        rq4 = [take(RC // 2).rearrange("p (n d) -> p n d", d=4) for _ in range(2)]
        rq2 = take(RC // 4).rearrange("p (n d) -> p n d", d=2)
        ER = DH * DH // 4
        Uk = late[:, 0:NC1 * 65].rearrange("p (n w) -> p n w", n=NC1)
        Uv = late[:, NC1 * 65:NC1 * (65 + ER)].rearrange("p (n w) -> p n w", n=NC1)
        rx = take(2 * LD)
        ss = take(CH * 8).rearrange("p (t h) -> p t h", t=CH)
        rs = take(CH * 8).rearrange("p (t h) -> p t h", t=CH)
        beta, dz, da, dsp, dec, alp, gc, eg, ba, be = (take(CH * LH).rearrange("p (t h) -> p t h", t=CH) for _ in range(10))
        ones = take(CH)
        eA = take(LH)
        Uo = take(LH * (2 * 64 + 1)).rearrange("p (h w) -> p h w", h=LH)
        Hf = H[:, :, :].rearrange("p j d -> p (j d)")
        SH = Hf[:, 0:NC1 * ER].rearrange("p (n w) -> p n w", n=NC1)
        sm, sr_, sv_ = Hf[:, 1024:1024 + ER * DH], Hf[:, 1536:1536 + ER], Hf[:, 1600:1600 + ER]
        SL = Hf[:, 1664:1664 + LH * 64].rearrange("p (h w) -> p h w", h=LH)
        pos[0] = 0
        xr, xk = take(NB * T), take(NB * T)
        rl, ka, sgr, rv = ([take(512) for _ in range(2)] for _ in range(4))
        omu = take(2)

        x_in, w_in, c_in, cb_ready = sem("x_in"), sem("w_in"), sem("c_in"), sem("cb_ready")
        zeroed = sem("zeroed")
        ln_stats, ln_mv, ln_var, ln_sd, ln_rstd = (sem(n) for n in ("ln_stats", "ln_mv", "ln_var", "ln_sd", "ln_rstd"))
        ln_h, ln_T, ln_hT = sem("ln_h"), sem("ln_T"), sem("ln_hT")
        x_upd = sem("x_upd")
        xbo = sem("xbo")
        b_comb, b_w5, b_q, b_qe, b_qT, b_qm, b_qf, b_kl, b_klT, b_vl, b_v9 = (
            sem("b_" + n) for n in ("comb", "w5", "q", "qe", "qT", "qm", "qf", "kl", "klT", "vl", "v9"))
        b_sw, b_klT_pad, v9_zero, v9_ones = sem("b_sw"), sem("b_pads"), sem("v9_zero"), sem("v9_ones")
        c_qbd = [sem(f"c_qbd{i}") for i in range(NQ)]
        d_qbd = [sem(f"d_qbd{i}") for i in range(NQ)]
        c_S, c_max, c_sub, c_P, c_T, c_PT, c_O, c_rec, c_loc = (
            sem("c_" + n) for n in ("S", "max", "sub", "P", "T", "PT", "O", "rec", "loc"))
        d_u, d_kvw, d_e, d_phi, d_v9 = (sem("d_" + n) for n in ("u", "kvw", "e", "phi", "v9"))
        d_st, d_Sb, d_S, d_A, d_av, d_den, d_rden, d_rw, d_quo, d_glob = (
            sem("d_" + n) for n in ("st", "Sb", "S", "A", "av", "den", "rden", "rw", "quo", "glob"))
        e_diff, e_dT, e_dTs, e_g, e_gh, e_al, e_alpha, e_mix, e_mT, e_mTs, e_out = (
            sem("e_" + n) for n in ("diff", "dT", "dTs", "g", "gh", "al", "alpha", "mix", "mT", "mTs", "out"))
        y_out = sem("y_out")
        f_lg, f_sc, f_rt, f_gu, f_cw, f_sg, f_a1, f_a2, f_out = (
            sem("f_" + n) for n in ("lg", "sc", "rt", "gu", "cw", "sg", "a1", "a2", "out"))
        g_p, g_pr, g_sq, g_ss, g_eps, g_root, g_rec, g_rs, g_kn, g_qn, g_ready = (
            sem("g_" + n) for n in ("p", "pr", "sq", "ss", "eps", "root", "rec", "rs", "kn", "qn", "ready"))
        g_ones, g_beta, g_dz, g_abs, g_ex, g_eA, g_ex1, g_ln, g_sp, g_dec, g_gc, g_alp, g_eg, g_ba, g_kba, g_bb = (
            sem("g_" + n) for n in ("ones", "beta", "dz", "abs", "ex", "eA", "ex1", "ln", "sp", "dec", "gc", "alp", "eg", "ba", "kba",
                                    "bb"))
        l_R, l_Ra, l_rk, l_b, l_x, l_o, l_rq, l_r4, l_r2, l_z = (
            sem("l_" + n) for n in ("R", "Ra", "rk", "b", "x", "o", "rq", "r4", "r2", "z"))
        g_Uo, g_Ud, g_Ui, g_chain, g_Sd, g_SL = (sem("g_" + n) for n in ("Uo", "Ud", "Ui", "chain", "Sd", "SL"))
        g_w, g_om, g_os, g_o, g_sqo, g_norm, g_gate, g_oT, g_out = (
            sem("g_" + n) for n in ("w", "om", "os", "o", "sqo", "norm", "gate", "oT", "out"))
        h_pad = sem("h_pad")
        h_omu, h_own, h_mix, h_k, h_r, h_rl, h_ka, h_sr, h_v, h_rv, h_x = (
            sem("h_" + n) for n in ("omu", "own", "mix", "k", "r", "rl", "ka", "sr", "v", "rv", "x"))

        block = ctx.enter_context(nc.Block())

        def hslice(q):
            b, o = divmod(q * SEG, T)
            return hT[:, b, PAD + o:PAD + o + SEG]

        hpack = hT[:, :, :].rearrange("p b t -> p (b t)")[:, 0:NB * T]

        def htile(j):
            b, o = divmod(j * P, T)
            return hT[:, b, PAD + o:PAD + o + P]

        def ln_bank(k, q):
            return (6, 2, 2, 4)[k] + q % 2

        def ln_moments(e, k, q):
            if k == 0:
                e.wait_ge(x_in, 64)
            else:
                e.wait_ge(x_upd, 4 * (k - 1) + q + 1)
            for j in range(4 * q, 4 * q + 4):
                e.bn_stats(st[:, j, :], X[:, j, :]).then_inc(ln_stats, 1)
            for j in range(4 * q, 4 * q + 4):
                e.wait_ge(ln_stats, NT * k + j + 1)
                e.bn_aggr(mv[:, j, :], st[:, j, :]).then_inc(ln_mv, 1)
            e.wait_ge(ln_mv, NT * k + 4 * q + 4)
            e.tensor_scalar(sd[:, 0, 4 * q:4 * q + 4], mv[:, 4 * q:4 * q + 4, 1], EPS_LN, None, ALU.add).then_inc(ln_var, 1)

        def ln_root(e, k, q):
            e.wait_ge(ln_var, 4 * k + q + 1)
            e.activation(sd[:, 1, 4 * q:4 * q + 4], sd[:, 0, 4 * q:4 * q + 4], ACT.Sqrt).then_inc(ln_sd, 1)

        def ln_scale(e, k, q):
            e.wait_ge(ln_sd, 4 * k + q + 1)
            e.reciprocal(sd[:, 2, 4 * q:4 * q + 4], sd[:, 1, 4 * q:4 * q + 4]).then_inc(ln_rstd, 1)
            e.wait_ge(ln_rstd, 4 * k + q + 1)
            for j in range(4 * q, 4 * q + 4):
                e.tensor_scalar(H[:, j, :], X[:, j, :], mv[:, j, 0:1], sd[:, 2, j:j + 1],
                                ALU.subtract, ALU.mult).then_inc(ln_h, 1)

        def keep_warm(e, bank, n):
            for _ in range(n):
                e.matmul(PS[:, bank, 0:2 * P], identb[:, :], nmaskb.rearrange("p m k -> p (m k)"), start=True, stop=True)

        def ln_turn(e, k, q):
            if k == 0 and q == 0:
                e.wait_ge(c_in, 16)
            if q >= 2:
                e.wait_ge(ln_hT, 4 * k + q - 1)
            for j in range(4 * q, 4 * q + 4):
                e.wait_ge(ln_h, NT * k + j + 1)
                m = e.transpose(PS[:, ln_bank(k, q), (j % 4) * P:(j % 4 + 1) * P], H[:, j, :], ident)
            m.then_inc(ln_T, 1)

        def ln_store(e, k, q):
            e.wait_ge(ln_T, 4 * k + q + 1)
            dst = hpack[:, q * SEG:(q + 1) * SEG] if k == 2 else hslice(q)
            e.activation(dst, PS[:, ln_bank(k, q), :], ACT.Copy).then_inc(ln_hT, 1)

        NU = NT * 4

        def local_pe(e):
            def scores(u):
                j, g = divmod(u, 4)
                b, c0 = divmod(2 * j, NC1)
                if u >= 3:
                    e.wait_ge(c_sub, u - 2)
                if u % 16 == 0:
                    e.wait_ge(c_qbd[u // 16], 16 * NH)
                bank = PS[:, u % 3, :]
                e.matmul(bank, identb[:, :], nmaskb[:, 0 if c0 == 0 else 1, :].rearrange("p (o k) -> p o k", o=1)
                         .to_broadcast([P, 4, P]), start=True, stop=False, skip_group_check=True)
                for hh in range(4):
                    for c in range(2):
                        t0 = (j % 4) * P + CH * c
                        m = e.matmul(PS[CH * c:CH * c + CH, u % 3, hh * P:(hh + 1) * P],
                                     qbd[(j // 4) % 2][:, 4 * g + hh, t0:t0 + CH],
                                     klT[:, b, CH * (c0 + c):CH * (c0 + c) + P],
                                     start=False, stop=True, skip_group_check=True)
                m.then_inc(c_S, 1)

            def turn(u):
                e.wait_ge(c_P, u + 1)
                if u >= 2:
                    e.wait_ge(c_PT, u - 1)
                for hh in range(4):
                    m = e.transpose(PS[:, 3 + u % 2, hh * P:(hh + 1) * P], prob[u % 3][:, hh * P:(hh + 1) * P], ident)
                m.then_inc(c_T, 1)

            def values(u):
                j, g = divmod(u, 4)
                e.wait_ge(c_PT, u + 1)
                if g == 0 and j >= 2:
                    e.wait_ge(c_loc, j - 1)
                for hh in range(4):
                    h = 4 * g + hh
                    for c in range(2):
                        o = (8 * c + h // 2) * DE
                        m = e.matmul(PS[CH * (h % 2):CH * (h % 2) + CH, 5 + j % 2, o:o + DE],
                                     probT[u % 2][:, hh * P + CH * c:hh * P + CH * c + CH],
                                     v9l[:, 2 * j + c, h, :], start=True, stop=True, skip_group_check=True)
                m.then_inc(c_O, 1)

            e.wait_ge(cb_ready, 3)
            e.wait_ge(b_klT, NQ)
            e.wait_ge(b_v9, 8)
            scores(0)
            scores(1)
            for u in range(NU):
                if u + 2 < NU:
                    scores(u + 2)
                turn(u)
                if u >= 1:
                    values(u - 1)
            values(NU - 1)

        def local_dve(e):
            def normalise(j):
                e.wait_ge(c_O, 4 * j + 4)
                o = PS[:, 5 + j % 2, 0:NH * DE].rearrange("p (h e) -> p h e", e=DE)
                e.reciprocal(lrec[:, j % 2, :], o[:, :, DH]).then_inc(c_rec, 1)
                e.wait_ge(c_rec, j + 1)
                e.tensor_tensor(loc[:, j, :].rearrange("p (h e) -> p h e", e=DH), o[:, :, 0:DH],
                                lrec[:, j % 2, :].rearrange("p (h o) -> p h o", o=1).to_broadcast([P, NH, DH]),
                                ALU.mult).then_inc(c_loc, 1)

            for u in range(NU):
                e.wait_ge(c_S, u + 1)
                s = PS[:, u % 3, :].rearrange("p (h k) -> p h k", h=4)
                e.tensor_reduce(rowmax[:, u % 2, :], s, AX, ALU.max).then_inc(c_max, 1)
                e.wait_ge(c_max, u + 1)
                if u >= 3:
                    e.wait_ge(c_T, u - 2)
                e.tensor_tensor(prob[u % 3].rearrange("p (h k) -> p h k", h=4), s,
                                rowmax[:, u % 2, :].rearrange("p (h o) -> p h o", o=1).to_broadcast([P, 4, P]),
                                ALU.subtract).then_inc(c_sub, 1)
                if u % 4 == 2 and u >= 4:
                    normalise(u // 4 - 1)
            normalise(NT - 1)

        def local_act(e):
            def copy_back(u):
                e.wait_ge(c_T, u + 1)
                if u >= 2:
                    e.wait_ge(c_O, u - 1)
                e.activation(probT[u % 2], PS[:, 3 + u % 2, :], ACT.Copy).then_inc(c_PT, 1)

            for u in range(NU):
                e.wait_ge(c_sub, u + 1)
                e.activation(prob[u % 3], prob[u % 3], ACT.Exp, scale=float(DH) ** -0.5).then_inc(c_P, 1)
                if u >= 1:
                    copy_back(u - 1)
            copy_back(NU - 1)

        def prep_pe(e, j, i):
            p = 7 * j + i
            bank = PS[:, 6 + p % 2, :]
            h = htile(j)
            if j == 0 and i == 0:
                e.wait_ge(b_w5, 2)
            if i == 0 and j > 0:
                e.wait_ge(d_e, 3 * j)
            elif i == 1 and j > 0:
                e.wait_ge(d_v9, 4 * j)
            elif i == 2:
                e.wait_ge(d_kvw, 3 * j + 1)
            elif i == 3:
                e.wait_ge(d_kvw, 3 * j + 2)
            elif i == 4:
                e.wait_ge(d_kvw, 3 * j + 3)
            elif i == 5:
                e.wait_ge(d_e, 3 * j + 1)
            elif i == 6:
                e.wait_ge(d_e, 3 * j + 2)
                e.wait_ge(d_v9, 4 * j + 2)
            kw = lambda l: kvw[:, l * P:(l + 1) * P] if l < 4 else kvw[:, 512:640]
            vw = lambda l: kvw[:, 768 + l * P:768 + (l + 1) * P] if l < 4 else kvw[:, 640:768]
            mm = lambda c, a, b: e.matmul(bank[:, c * P:(c + 1) * P], a, b, start=True, stop=True, skip_group_check=True)
            if i == 0:
                m = e.matmul(bank, h, wk5[:, 0:512], start=True, stop=True)
            elif i == 1:
                mm(0, h, wk5[:, 512:640])
                m = mm(1, h, wv5[:, 512:640])
            elif i == 2:
                m = e.matmul(bank, h, wv5[:, 0:512], start=True, stop=True)
            elif i == 3:
                e.transpose(bank[:, 0:P], kw(0), ident)
                for l in range(1, 4):
                    m = mm(l, kw(l), mean[:, l - 1, :])
            elif i == 4:
                mm(0, kw(4), mean[:, 3, :])
                mm(1, mean[:, 3, :], kw(4))
                m = mm(2, mean[:, 3, :], vw(4))
            elif i == 5:
                for l in range(1, 4):
                    m = mm(l, mean[:, l - 1, :], kw(l))
            else:
                for l in range(1, 4):
                    m = mm(l, mean[:, l - 1, :], vw(l))
            m.then_inc(d_u, 1)

        def prep_act(e, j):
            for i in range(7):
                p = 7 * j + i
                bank = PS[:, 6 + p % 2, :]
                e.wait_ge(d_u, p + 1)
                if i in (0, 1, 2):
                    a, n = ((0, 512), (512, 256), (768, 512))[i]
                    e.activation(kvw[:, a:a + n], bank[:, 0:n], ACT.Copy).then_inc(d_kvw, 1)
                if i in (3, 4, 5):
                    n, first = (512, 256, 512)[i - 3], int(i == 5)
                    a = first * P
                    kf = keys_of(j, i - 3)
                    if j > 0:
                        e.wait_ge(d_phi, 3 * (j - 1) + i - 2)
                    if j >= 2:
                        e.wait_ge(d_av, 10 * (j - 1))
                    if first:
                        e.activation(ephi[:, 2, 0:P], kvw[:, 0:P], ACT.Exp)
                        e.activation(kf[:, 0, :], kvw[:, 0:P], ACT.Relu)
                    e.activation(ephi[:, i - 3, a:n], bank[:, a:n], ACT.Exp)
                    e.activation(kf[:, first:, :], bank[:, a:n].rearrange("p (l n) -> p l n", n=P), ACT.Relu).then_inc(d_e, 1)
                if i in (4, 6):
                    if j >= 2:
                        e.wait_ge(d_av, 10 * (j - 1))
                    ls, a = ((4, 5), 256) if i == 4 else ((1, 4), P)
                    n = (ls[1] - ls[0]) * P
                    for c in range(2):
                        r = slice(CH * c, CH * c + CH)
                        if i == 6:
                            e.activation(V9[j % 2][r, c, 0, :].rearrange("p (h e) -> p h e", e=DE)[:, :, 0:DH],
                                         kvw[r, 768:768 + P].rearrange("p (h e) -> p h e", e=DH), ACT.Copy)
                        e.activation(V9[j % 2][r, c, ls[0]:ls[1], :].rearrange("p l (h e) -> p (l h) e", e=DE)[:, :, 0:DH],
                                     bank[r, a:a + n].rearrange("p (h e) -> p h e", e=DH), ACT.Copy).then_inc(d_v9, 1)

        def keys_of(j, i):
            return KF[j % 2][:, :, 4, :] if i == 1 else KF[j % 2][:, i // 2, 0:4, :]

        def prep_dve(e, j, i):
            n = 256 if i == 1 else 512
            kf = keys_of(j, i)
            e.wait_ge(d_e, 3 * j + i + 1)
            e.scalar_tensor_tensor(kf, ephi[:, i, 0:n].rearrange("p (l n) -> p l n", n=P), 1.0, kf,
                                   ALU.min, ALU.add).then_inc(d_phi, 1)

        STATE = [(4, 0, 3), (5, 3, 5)]
        OUT = [(2, 0, 3), (3, 3, 5)]
        HE = NH * DE

        def bank_of(table, l, rows=slice(0, P)):
            for bk, a, b in table:
                if a <= l < b:
                    return PS[rows, bk, (l - a) * HE:(l - a + 1) * HE]

        def linear_pe(e):
            def state(j, c):
                k = 2 * j + c
                if k > 0:
                    e.wait_ge(d_Sb, 2 * k)
                for l in range(LV):
                    first = j % (NT // NB) == 0 and c == 0 and l in (0, 3)
                    m = e.matmul(bank_of(STATE, l), KF[j % 2][:, 1, l, :], V9[j % 2][:, c, l, :],
                                 start=first, stop=True, skip_group_check=True)
                m.then_inc(d_st, 1)

            def scores(j, s):
                l, hh = divmod(s, 2)
                n = 10 * j + s
                if n >= 2:
                    e.wait_ge(d_A, n - 1)
                if j % 4 == 0 and s == 0:
                    e.wait_ge(d_qbd[j // 4], 16 * NH)
                for c in range(2):
                    t0 = (j % 4) * P + CH * c
                    m = e.matmul(PS[CH * c:CH * c + CH, n % 2, :], KF[j % 2][:, 0, l, CH * c:CH * c + CH],
                                 qbd[(j // 4) % 2][:, 8 * hh:8 * hh + 8, t0:t0 + CH],
                                 start=True, stop=True, skip_group_check=True)
                m.then_inc(d_S, 1)

            def values(j, s):
                l, hh = divmod(s, 2)
                n = 10 * j + s
                if s == 0 and j > 0:
                    e.wait_ge(d_quo, 2 * j)
                if hh == 0:
                    for c in range(2):
                        k = 2 * j + c
                        e.wait_ge(d_Sb, 2 * k)
                        t0 = j * P + CH * c
                        for p in range(2):
                            e.matmul(bank_of(OUT, l, slice(CH * p, CH * p + CH))[:, c * HE // 2:(c + 1) * HE // 2],
                                     qf[:, t0:t0 + CH],
                                     SB[:, k % 4, l, :].rearrange("q (a p e) -> q p a e", p=2, e=DE)[:, p, :, :],
                                     start=(c == 0), stop=False, skip_group_check=True)
                e.wait_ge(d_A, n + 1)
                for h in range(8):
                    hd = 8 * hh + h
                    r = slice(CH * (hd % 2), CH * (hd % 2) + CH)
                    m = e.matmul(bank_of(OUT, l, r).rearrange("p (c a e) -> p c a e", c=2, e=DE)[:, :, hd // 2, :],
                                 AT[n % 4][:, h * CH:(h + 1) * CH], V9[j % 2][:, :, l, hd * DE:(hd + 1) * DE],
                                 start=False, stop=True, skip_group_check=True)
                m.then_inc(d_av, 1)

            e.matmul(PS[:, 7, :], w("Wk"), w("HBk"), start=True, stop=True).then_inc(b_comb, 1)
            e.wait_ge(c_loc, NT)
            e.matmul(PS[:, 0, :], w("Wv"), w("HBv"), start=True, stop=True).then_inc(b_comb, 1)
            for i in range(7):
                prep_pe(e, 0, i)
            e.wait_ge(zeroed, 4)
            e.wait_ge(v9_ones, 2)
            e.wait_ge(d_phi, 3)
            e.wait_ge(d_v9, 4)
            for j in range(NT):
                state(j, 0)
                scores(j, 0)
                scores(j, 1)
                for s in range(10):
                    if s < 7 and j + 1 < NT:
                        prep_pe(e, j + 1, s)
                    if s + 2 < 10:
                        scores(j, s + 2)
                    values(j, s)
                    if s == 4:
                        state(j, 1)
                if j + 1 < NT:
                    e.wait_ge(d_phi, 3 * (j + 2))
                    e.wait_ge(d_v9, 4 * (j + 2))

        tri = cst("tri").rearrange("p (o t) -> p o t", o=1)
        smask = cst("hmask").rearrange("p (h o) -> p h o", o=1)

        def linear_dve(e):
            def state(j, c):
                k = 2 * j + c
                e.wait_ge(d_st, k + 1)
                if k >= 4:
                    e.wait_ge(d_av, 5 * (k - 3) + 5)
                for bk, a, b in STATE:
                    o = SB[:, (k + 1) % 4, a:b, :]
                    if c == 1 and (j + 1) % (NT // NB) == 0:
                        e.memset(o, 0.0).then_inc(d_Sb, 1)
                    else:
                        e.tensor_tensor(o.rearrange("p l (h e) -> p l h e", e=DE),
                                        PS[:, bk, 0:(b - a) * HE].rearrange("p (l h e) -> p l h e", l=b - a, e=DE),
                                        smask.rearrange("p (l h) o -> p l h o", l=1).to_broadcast([P, b - a, NH, DE]),
                                        ALU.mult).then_inc(d_Sb, 1)

            def mask(j, s):
                n = 10 * j + s
                e.wait_ge(d_S, n + 1)
                if n >= 4:
                    e.wait_ge(d_av, n - 3)
                e.tensor_tensor(AT[n % 4].rearrange("p (h t) -> p h t", h=8),
                                PS[:, n % 2, :].rearrange("p (h t) -> p h t", h=8),
                                tri.to_broadcast([P, 8, CH]), ALU.mult).then_inc(d_A, 1)

            def finish(j):
                e.wait_ge(d_av, 10 * (j + 1))
                for bk, a, b in OUT:
                    o = PS[:, bk, 0:(b - a) * HE].rearrange("p (l h e) -> p l h e", l=b - a, e=DE)
                    e.tensor_scalar(den[:, 0, a:b, :], o[:, :, :, DH], EPS_LIN, None, ALU.max).then_inc(d_den, 1)
                e.wait_ge(d_den, 2 * j + 2)
                e.reciprocal(den[:, 1, :, :], den[:, 0, :, :]).then_inc(d_rden, 1)
                e.wait_ge(d_rden, j + 1)
                e.tensor_tensor(den[:, 2, :, :], den[:, 1, :, :],
                                hsw[:, 0:LV].rearrange("p (l o) -> p l o", o=1).to_broadcast([P, LV, NH]),
                                ALU.mult).then_inc(d_rw, 1)
                e.wait_ge(d_rw, j + 1)
                for bk, a, b in OUT:
                    o = PS[:, bk, 0:(b - a) * HE].rearrange("p (l h e) -> p (l h) e", l=b - a, e=DE)
                    e.tensor_tensor(quo[:, a:b, :].rearrange("p l (h e) -> p (l h) e", e=DH), o[:, :, 0:DH],
                                    den[:, 2, a:b, :].rearrange("p l (h o) -> p (l h) o", o=1)
                                    .to_broadcast([P, (b - a) * NH, DH]), ALU.mult).then_inc(d_quo, 1)

            def collect(j):
                e.wait_ge(d_quo, 2 * j + 2)
                e.tensor_reduce(glob[:, j, :], quo.rearrange("p l n -> p n l"), AX, ALU.add).then_inc(d_glob, 1)

            e.wait_ge(zeroed, 4)
            e.wait_ge(v9_ones, 2)
            for i in range(3):
                prep_dve(e, 0, i)
            for j in range(NT):
                state(j, 0)
                mask(j, 0)
                for s in range(10):
                    if s + 1 < 10:
                        mask(j, s + 1)
                    if s == 0 and j > 0:
                        collect(j - 1)
                    if s in (5, 6, 7) and j + 1 < NT:
                        prep_dve(e, j + 1, s - 5)
                    if s == 5:
                        state(j, 1)
                finish(j)
            collect(NT - 1)

        def bc(ap, shape):
            return ap.to_broadcast(shape)

        def moe_pe(e):
            for j in range(NT):
                e.wait_ge(ln_hT, 4 + j // 4 + 1)
                m = e.matmul(PS[:, 0, j * NE:(j + 1) * NE], htile(j), w("gateT"), start=True, stop=True,
                             skip_group_check=True)
            m.then_inc(f_lg, 1)

            def down(tb):
                e.wait_ge(f_a2, 5 * (tb + 1))
                if tb >= 2:
                    e.wait_ge(x_upd, 4 + tb - 1)
                for i in range(4):
                    for q in range(5):
                        k = P if q < 4 else 64
                        wd = w("Ed")[:, q * P:(q + 1) * P] if q < 4 else w("Eds")[0:64, :]
                        m = e.matmul(PS[:, 6 + tb % 2, i * P:(i + 1) * P], act[tb % 2][0:k, q, i * P:(i + 1) * P], wd,
                                     start=(q == 0), stop=(q == 4), skip_group_check=True)
                m.then_inc(f_out, 1)

            for n in range(5 * NQ):
                tb, q = divmod(n, 5)
                rows_ = P if q < 4 else 64
                if n == 0:
                    e.wait_ge(f_sc, 1)
                if n >= 2:
                    e.wait_ge(f_sg, n - 1)
                    e.wait_ge(f_a2, n - 1)
                cols = slice(q * P, q * P + rows_)
                e.matmul(PS[0:rows_, n % 2, :], w("Eg")[:, cols], hslice(tb), start=True, stop=True)
                e.matmul(PS[0:rows_, 2 + n % 2, :], w("Eu")[:, cols], hslice(tb), start=True, stop=True).then_inc(f_gu, 1)
                if q < 4:
                    if q == 0:
                        e.wait_ge(f_rt, RT_STEPS * (tb + 1))
                    for i in range(4):
                        for x in range(2):
                            m = e.matmul(PS[64 * x:64 * x + 64, 4 + n % 2, i * P:(i + 1) * P],
                                         bc(cw[:, 4 * tb + i, 2 * q + x:2 * q + x + 1], [P, 64]),
                                         ident, start=True, stop=True, skip_group_check=True)
                    m.then_inc(f_cw, 1)
                if q == 1 and tb > 0:
                    down(tb - 1)
            down(NQ - 1)
            for q in range(NQ):
                ln_turn(e, 2, q)
                keep_warm(e, 4, 8)

        RT_GROUPS, RT_RANKS, RT_STEPS = 9, 15, 20

        def rt_step(e, tb, n, ins):
            ins.then_inc(f_rt, 1)
            e.wait_ge(f_rt, RT_STEPS * tb + n)

        def rank(e, tb, n, v, m, pq, qq, low, r):
            vi = bc(v.rearrange("p j (g o) -> p j g o", o=1), [P, 4, m, m])
            vj = bc(v.rearrange("p j (o g) -> p j o g", o=1), [P, 4, m, m])
            lw = bc(low.rearrange("p (o n) -> p o n", o=1), [P, 4, m * m])
            flat = qq.rearrange("p j a b -> p j (a b)")
            rt_step(e, tb, n + 1, e.tensor_tensor(pq, vj, vi, ALU.is_gt))
            rt_step(e, tb, n + 2, e.tensor_tensor(qq, vj, vi, ALU.is_equal))
            rt_step(e, tb, n + 3, e.tensor_tensor(flat, flat, lw, ALU.mult))
            rt_step(e, tb, n + 4, e.tensor_tensor(pq, pq, qq, ALU.add))
            rt_step(e, tb, n + 5, e.tensor_reduce(r, pq, AX, ALU.add))

        def quarter_of(tb, *arrays):
            return (a[:, 4 * tb:4 * tb + 4] for a in arrays)

        def router_groups(e, tb):
            sc, c, ch, g, gr, gm, p4, q4 = quarter_of(tb, rt_s, rt_c, rt_ch, rt_g, rt_gr, rt_gm, rt_p4, rt_q4)
            if tb == 0:
                e.wait_ge(f_sc, 1)
            pair = c.rearrange("p j (g two) -> p j g two", two=2)
            rt_step(e, tb, 1, e.tensor_tensor(c, sc, bc(w("cbias").rearrange("p (o e) -> p o e", o=1), [P, 4, NE]), ALU.add))
            rt_step(e, tb, 2, e.tensor_tensor(g, pair[:, :, :, 0], pair[:, :, :, 1], ALU.add))
            rank(e, tb, 2, g, 4, p4, q4, cst("low4"), gr)
            rt_step(e, tb, 8, e.tensor_scalar(gm, gr, 2.0, None, ALU.is_lt))
            rt_step(e, tb, RT_GROUPS, e.tensor_tensor(ch.rearrange("p j (g two) -> p j g two", two=2), pair,
                                                      bc(gm.rearrange("p j (g o) -> p j g o", o=1), [P, 4, 4, 2]), ALU.mult))

        def router_experts(e, tb):
            sc, ch, wt, r8, p8, q8 = quarter_of(tb, rt_s, rt_ch, rt_w, rt_r8, rt_p8, rt_q8)
            rank(e, tb, RT_GROUPS, ch, NE, p8, q8, cst("low8"), r8)
            rt_step(e, tb, RT_RANKS, e.scalar_tensor_tensor(wt, r8, 4.0, sc, ALU.is_lt, ALU.mult))

        def router_weights(e, tb):
            wt, ch, out = quarter_of(tb, rt_w, rt_ch, cw)
            total, safe, inv = (rt_n[:, k, 4 * tb:4 * tb + 4] for k in range(3))
            rt_step(e, tb, 16, e.tensor_reduce(total, wt, AX, ALU.add))
            rt_step(e, tb, 17, e.tensor_scalar(safe, total, 1e-20, None, ALU.add))
            rt_step(e, tb, 18, e.reciprocal(inv, safe))
            rt_step(e, tb, 19, e.tensor_tensor(ch, wt, bc(inv.rearrange("p (j o) -> p j o", o=1), [P, 4, NE]), ALU.mult))
            rt_step(e, tb, RT_STEPS, e.tensor_scalar(out, ch, 2.5, None, ALU.mult))

        def moe_dve(e):
            router_groups(e, 0)
            router_experts(e, 0)
            router_weights(e, 0)

            def residual(tb):
                e.wait_ge(f_out, tb + 1)
                xs = X[:, 4 * tb:4 * tb + 4, :]
                e.tensor_tensor(xs, PS[:, 6 + tb % 2, :].rearrange("p (j d) -> p j d", j=4), xs, ALU.add).then_inc(x_upd, 1)

            for n in range(5 * NQ):
                tb, q = divmod(n, 5)
                if q == 0 and tb >= 2:
                    e.wait_ge(f_out, tb - 1)
                e.wait_ge(f_sg, n + 1)
                if q < 4:
                    e.tensor_tensor(sgu[n % 3], sgu[n % 3], PS[:, 2 + n % 2, :], ALU.mult).then_inc(f_a1, 1)
                    e.wait_ge(f_a1, 4 * tb + q + 1)
                    e.wait_ge(f_cw, 4 * tb + q + 1)
                    e.tensor_tensor(act[tb % 2][:, q, :], sgu[n % 3], PS[:, 4 + n % 2, :], ALU.mult).then_inc(f_a2, 1)
                else:
                    e.tensor_tensor(act[tb % 2][0:64, q, :], sgu[n % 3][0:64], PS[0:64, 2 + n % 2, :], ALU.mult).then_inc(f_a2, 1)
                if tb + 1 < NQ:
                    if q == 0:
                        router_groups(e, tb + 1)
                    elif q == 1:
                        router_experts(e, tb + 1)
                    elif q == 3:
                        router_weights(e, tb + 1)
                if q == 2 and tb > 0:
                    residual(tb - 1)
                    ln_moments(e, 2, tb - 1)
            for q in range(NQ - 1):
                ln_scale(e, 2, q)
            residual(NQ - 1)
            ln_moments(e, 2, NQ - 1)
            ln_scale(e, 2, NQ - 1)

        def moe_act(e):
            e.wait_ge(f_lg, 1)
            e.activation(rt_s.rearrange("p j e -> p (j e)"), PS[:, 0, 0:NT * NE], ACT.Sigmoid).then_inc(f_sc, 1)
            for n in range(5 * NQ):
                rows_ = P if n % 5 < 4 else 64
                e.wait_ge(f_gu, n + 1)
                if n >= 3:
                    e.wait_ge(f_a2, n - 2)
                e.activation(sgu[n % 3][0:rows_], PS[0:rows_, n % 2, :], ACT.Silu).then_inc(f_sg, 1)
            for q in range(NQ - 1):
                ln_root(e, 2, q)
            ln_store(e, 2, 0)
            ln_root(e, 2, NQ - 1)
            for q in range(1, NQ):
                ln_store(e, 2, q)

        tok = hpack.rearrange("p (n c) -> p n c", c=CH)
        NG = (CH + 2) // 3
        quarter = lambda c: slice(c * CH // NQ, (c + 1) * CH // NQ)
        quarter_in = lambda c: ((c + 1) * CH // NQ + 2) // 3

        def col(ap, o):
            return ap[:, :, o:o + LD].rearrange("p t (h d) -> p t h d", h=LH)

        def per_head(ap, n=DH, t=CH):
            return bc(ap.rearrange("p t (h o) -> p t h o", o=1), [P, t, LH, n])

        h4 = lambda ap: ap.rearrange("p t (h d) -> p t h d", h=LH)

        def delta_pe(e):
            e.wait_ge(ln_hT, 12)
            for i in range(NG):
                if i >= 4:
                    e.wait_ge(g_pr, i - 3)
                for s in range(min(3, CH - 3 * i)):
                    t = 3 * i + s
                    for j in range(4):
                        m = e.matmul(PS[32 * j:32 * j + 32, i % 4, s * PW:(s + 1) * PW], tok[:, :, t],
                                     w("L1W")[:, j * PW:(j + 1) * PW], start=True, stop=True, skip_group_check=True)
                m.then_inc(g_p, 1)
            e.wait_ge(g_oT, 1)
            for q in range(NQ):
                if q >= 2:
                    e.wait_ge(x_upd, 8 + q - 1)
                for i in range(4):
                    for c in range(2):
                        m = e.matmul(PS[CH * c:CH * c + CH, 6 + q % 2, i * P:(i + 1) * P], oT[:, :, 2 * (4 * q + i) + c],
                                     w("L1Wo"), start=True, stop=True, skip_group_check=True)
                m.then_inc(g_out, 1)
            for q in range(NQ):
                ln_turn(e, 3, q)

        def delta_act(e):
            def root(c):
                e.wait_ge(g_eps, c + 1)
                e.activation(ss[:, quarter(c), :], ss[:, quarter(c), :], ACT.Sqrt).then_inc(g_root, 1)

            for i in range(NG):
                n = min(3, CH - 3 * i)
                e.wait_ge(g_p, i + 1)
                e.activation(pr[:, 3 * i:3 * i + n, :].rearrange("p t c -> p (t c)"), PS[:, i % 4, 0:n * PW], ACT.Copy)\
                 .then_inc(g_pr, 1)
                for c in range(NQ - 1):
                    if i == quarter_in(c) + 5:
                        root(c)
            e.wait_ge(g_pr, NG)
            e.activation(beta, pr[:, :, 4 * LD:4 * LD + LH], ACT.Sigmoid).then_inc(g_beta, 1)
            e.activation(eA, w("Alog"), ACT.Exp).then_inc(g_eA, 1)
            e.wait_ge(g_dz, 1)
            e.activation(da, dz, ACT.Abs).then_inc(g_abs, 1)
            e.wait_ge(g_abs, 1)
            e.activation(da, da, ACT.Exp, scale=-1.0).then_inc(g_ex, 1)
            e.wait_ge(g_ex1, 1)
            e.activation(da, da, ACT.Ln).then_inc(g_ln, 1)
            e.wait_ge(g_dec, 1)
            e.activation(alp, dec, ACT.Exp).then_inc(g_alp, 1)
            e.wait_ge(g_gc, 1)
            e.activation(eg, gc, ACT.Exp).then_inc(g_eg, 1)
            root(NQ - 1)
            e.wait_ge(g_eg, 1)
            e.activation(Uo[:, :, 128], eg[:, CH - 1, :], ACT.Copy).then_inc(g_Uo, 1)
            def ninth(t):
                if t >= 2:
                    e.wait_ge(l_x, 2 * (t - 1))
                e.activation(rkb[t % 2][:, :, DH], bb[:, t, :, :].rearrange("p h c -> p (h c)"), ACT.Copy).then_inc(l_b, 1)

            def decay(t, par):
                for h in range(LH):
                    if h % 2 == 0:
                        e.wait_ge(l_R, 2 * t + h // 2 + 1)
                    cols = slice(h * RC // LH, (h + 1) * RC // LH)
                    e.activation(Ra[:, cols], Rs[1 - par][:, cols], ACT.Copy, scale=alp[:, t, h:h + 1]).then_inc(l_Ra, 1)

            e.wait_ge(g_ready, 1)
            ninth(0)
            for t in range(CH):
                decay(t, t % 2)
                if t + 1 < CH:
                    ninth(t + 1)
            e.wait_ge(l_R, 2 * CH + 2)
            e.activation(Uo[:, :, 0:128], Rs[(CH - 1) % 2].rearrange("p (h w) -> p h w", h=LH), ACT.Copy).then_inc(g_Uo, 1)
            e.activation(pr[:, :, 3 * LD:4 * LD], pr[:, :, 3 * LD:4 * LD], ACT.Silu).then_inc(g_gate, 1)
            for c in range(2):
                ts = slice(c * CH // 2, (c + 1) * CH // 2)
                e.wait_ge(g_o, c + 1)
                e.activation(qeg[:, ts, :], og[:, ts, :], ACT.Square).then_inc(g_sqo, 1)
            e.wait_ge(g_norm, 1)
            e.activation(ss[:, :, 0:LH], ss[:, :, 0:LH], ACT.Sqrt).then_inc(g_norm, 1)
            for q in range(NQ):
                ln_root(e, 3, q)
                if q >= 1:
                    ln_store(e, 3, q - 1)
                    own(e, q - 1)
            ln_store(e, 3, NQ - 1)
            own(e, NQ - 1)

        def delta_pool(e):
            e.memset(ones, 1.0).then_inc(g_ones, 1)

            def keys(c):
                e.wait_ge(g_rec, c + 1)
                e.tensor_tensor(h4(kn)[:, quarter(c)], col(pr, LD)[:, quarter(c)], per_head(rs[:, quarter(c), 4:8], n=DH, t=CH // NQ),
                                ALU.mult).then_inc(g_kn, 1)

            def rows_of_keys(c):
                e.wait_ge(g_kn, c + 1)
                e.tensor_tensor(h4(kba)[:, quarter(c)], h4(kn)[:, quarter(c)], per_head(ba[:, quarter(c), :], n=DH, t=CH // NQ),
                                ALU.mult).then_inc(g_kba, 1)

            for c in range(NQ):
                e.wait_ge(g_pr, quarter_in(c))
                e.tensor_tensor(Zs[:, quarter(c), :], pr[:, quarter(c), 0:2 * LD], pr[:, quarter(c), 0:2 * LD], ALU.mult)\
                 .then_inc(g_sq, 1)
                if c >= 2:
                    keys(c - 2)
            keys(NQ - 2)
            e.wait_ge(g_p, NG)
            e.memset(hT[:, :, 0:PAD], 0.0).then_inc(h_pad, 1)
            e.wait_ge(g_ba, 1)
            for c in range(NQ - 1):
                rows_of_keys(c)
            keys(NQ - 1)
            rows_of_keys(NQ - 1)

            def products(t):
                e.wait_ge(l_R, 2 * t + 4)
                if t >= 1:
                    e.wait_ge(l_r4, t)
                e.tensor_tensor(rq.rearrange("p (h c d) -> p h c d", h=LH, d=DH),
                                Rs[t % 2].rearrange("p (h c d) -> p h c d", h=LH, d=DH),
                                bc(qn[:, t, :].rearrange("p (h o d) -> p h o d", h=LH, o=1), [P, LH, 2 * DH, DH]),
                                ALU.mult).then_inc(l_rq, 1)

            def sum4(t):
                e.wait_ge(l_rq, t + 1)
                if t >= 2:
                    e.wait_ge(l_r2, t - 1)
                v = rq.rearrange("p (n d) -> p n d", d=8)
                e.tensor_tensor(rq4[t % 2], v[:, :, 0:4], v[:, :, 4:8], ALU.add).then_inc(l_r4, 1)

            def sum2(t):
                e.wait_ge(l_r4, t + 1)
                if t >= 1:
                    e.wait_ge(l_z, t)
                e.tensor_tensor(rq2, rq4[t % 2][:, :, 0:2], rq4[t % 2][:, :, 2:4], ALU.add).then_inc(l_r2, 1)

            def sum1(t):
                e.wait_ge(l_r2, t + 1)
                e.tensor_tensor(Z[:, t, :, :].rearrange("p h c -> p (h c)"), rq2[:, :, 0], rq2[:, :, 1], ALU.add)\
                 .then_inc(l_z, 1)

            e.wait_ge(g_ready, 1)
            for t in range(CH + 1):
                if t < CH:
                    products(t)
                if t >= 1:
                    sum2(t - 1)
                if t < CH:
                    sum4(t)
                if t >= 1:
                    sum1(t - 1)
            e.wait_ge(l_z, CH)
            e.wait_ge(g_SL, 16 * LH)
            e.wait_ge(g_w, 1)
            e.tensor_tensor(oS[1].rearrange("p (t e d) -> p t e d", t=CH, e=DH),
                            bc(qeg[:, :, 3 * DH:4 * DH].rearrange("p t (o d) -> p t o d", o=1), [P, CH, DH, DH]),
                            bc(SL[:, 3, :].rearrange("p (o e d) -> p o e d", o=1, e=DH), [P, CH, DH, DH]),
                            ALU.mult).then_inc(g_os, 1)
            v8 = oS[1].rearrange("p (n d) -> p n d", d=8)
            for n, half in enumerate((4, 2, 1)):
                e.wait_ge(g_os, n + 1)
                dst = v8[:, :, 0:half] if half > 1 else og.rearrange("p t (h e) -> p t h e", e=DH)[:, :, 3, :]
                a_, b_ = v8[:, :, 0:half], v8[:, :, half:2 * half]
                if half == 1:
                    a_, b_ = (z.rearrange("p (t e) o -> p t (e o)", e=DH) for z in (a_, b_))
                e.tensor_tensor(dst, a_, b_, ALU.add).then_inc(g_os, 1)
            e.wait_ge(g_gate, 1)
            e.tensor_tensor(col(pr, 3 * LD), col(pr, 3 * LD),
                            bc(w("normw").rearrange("p (o q d) -> p o q d", o=1, q=1), [P, CH, LH, DH]), ALU.mult)\
             .then_inc(g_gate, 1)
            e.wait_ge(g_gate, 2)
            e.wait_ge(g_o, 2)
            e.tensor_tensor(pr[:, :, 3 * LD:4 * LD], pr[:, :, 3 * LD:4 * LD], og, ALU.mult).then_inc(g_gate, 1)

        def delta_dve(e):
            def norms(c):
                e.wait_ge(g_sq, c + 1)
                e.tensor_reduce(ss[:, quarter(c), :], Zs[:, quarter(c), :].rearrange("p t (h d) -> p t h d", d=DH), AX, ALU.add)\
                 .then_inc(g_ss, 1)
                e.wait_ge(g_ss, c + 1)
                e.tensor_scalar(ss[:, quarter(c), :], ss[:, quarter(c), :], EPS_NORM, None, ALU.add).then_inc(g_eps, 1)

            def queries(c):
                e.wait_ge(g_root, c + 1)
                e.reciprocal(rs[:, quarter(c), :], ss[:, quarter(c), :]).then_inc(g_rec, 1)
                e.wait_ge(g_rec, c + 1)
                e.tensor_scalar(rs[:, quarter(c), 0:LH], rs[:, quarter(c), 0:LH], float(DH) ** -0.5, None, ALU.mult).then_inc(g_rs, 1)
                e.wait_ge(g_rs, c + 1)
                e.tensor_tensor(h4(qn)[:, quarter(c)], col(pr, 0)[:, quarter(c)], per_head(rs[:, quarter(c), 0:4], t=CH // NQ),
                                ALU.mult).then_inc(g_qn, 1)

            norms(0)
            norms(1)
            queries(0)
            norms(2)
            queries(1)
            e.wait_ge(g_pr, NG)
            e.tensor_tensor(dz, pr[:, :, 4 * LD + LH:PW], bc(w("dtb").rearrange("p (o h) -> p o h", o=1), [P, CH, LH]),
                            ALU.add).then_inc(g_dz, 1)
            queries(2)
            e.wait_ge(g_ex, 1)
            e.tensor_scalar(da, da, 1.0, None, ALU.add).then_inc(g_ex1, 1)
            norms(3)
            e.wait_ge(g_ln, 1)
            e.scalar_tensor_tensor(dsp, dz, 0.0, da, ALU.max, ALU.add).then_inc(g_sp, 1)
            e.wait_ge(g_sp, 1)
            e.wait_ge(g_eA, 1)
            e.scalar_tensor_tensor(dec, dsp, -1.0, bc(eA.rearrange("p (o h) -> p o h", o=1), [P, CH, LH]),
                                   ALU.mult, ALU.mult).then_inc(g_dec, 1)
            e.wait_ge(g_dec, 1)
            e.wait_ge(g_ones, 1)
            for h in range(LH):
                m = e.tensor_tensor_scan(gc[:, :, h], ones, dec[:, :, h], 0.0, ALU.mult, ALU.add)
            m.then_inc(g_gc, 1)
            e.wait_ge(g_beta, 1)
            e.wait_ge(g_alp, 1)
            e.tensor_tensor(ba, beta, alp, ALU.mult).then_inc(g_ba, 1)
            e.wait_ge(g_eg, 1)
            e.tensor_tensor(be, beta, eg, ALU.mult).then_inc(g_ba, 1)
            e.tensor_tensor(bb[:, :, :, 0:DH], col(pr, 2 * LD), per_head(beta), ALU.mult).then_inc(g_bb, 1)
            queries(3)
            e.wait_ge(g_ba, 2)
            for c in range(2):
                ts = (slice(0, 3 * CH // 4), slice(3 * CH // 4, CH))[c]
                e.wait_ge(g_kn, (NQ - 1, NQ)[c])
                e.tensor_tensor(bb[:, ts, :, DH:2 * DH], h4(kn)[:, ts], per_head(be[:, ts, :], t=ts.stop - ts.start), ALU.mult)\
                 .then_inc(g_bb, 1)
                if c == 0:
                    e.wait_ge(g_qn, NQ)
                    e.tensor_tensor(h4(qeg), h4(qn), per_head(eg), ALU.mult).then_inc(g_bb, 1)
            e.memset(Rs[1], 0.0).then_inc(l_R, 2)
            e.wait_ge(g_kba, NQ)
            e.wait_ge(g_bb, 4)
            e.memset(rx, 0.0).then_inc(g_ready, 1)

            def part(ap, g):
                return ap[:, g * RC // 2:(g + 1) * RC // 2].rearrange("p (h c d) -> p h c d", h=2, d=DH)

            def feats(ap, t, g):
                return bc(ap[:, t, g * LD // 2:(g + 1) * LD // 2].rearrange("p (h o d) -> p h o d", h=2, o=1),
                          [P, 2, 2 * DH, DH])

            def step(t, par):
                for g in range(2):
                    c = slice(g * LD, (g + 1) * LD)
                    e.wait_ge(l_R, 2 * t + g + 1)
                    e.tensor_tensor(rkb[par][:, c, 0:DH].rearrange("p (h c) d -> p h c d", h=2), part(Rs[1 - par], g),
                                    feats(kba, t, g), ALU.mult).then_inc(l_rk, 1)
                e.wait_ge(l_b, t + 1)
                for g in range(2):
                    c = slice(g * LD, (g + 1) * LD)
                    e.wait_ge(l_rk, 2 * t + g + 1)
                    e.tensor_reduce(rx[:, c], rkb[par][:, c, :], AX, ALU.add).then_inc(l_x, 1)
                for g in range(2):
                    c = slice(g * LD, (g + 1) * LD)
                    e.wait_ge(l_x, 2 * t + g + 1)
                    e.tensor_tensor(part(ro, g), bc(rx[:, c].rearrange("p (h c o) -> p h c o", h=2, o=1), [P, 2, 2 * DH, DH]),
                                    feats(kn, t, g), ALU.mult).then_inc(l_o, 1)
                if t >= 2:
                    e.wait_ge(l_rq, t - 1)
                for g in range(2):
                    c = slice(g * RC // 2, (g + 1) * RC // 2)
                    e.wait_ge(l_o, 2 * t + g + 1)
                    e.wait_ge(l_Ra, LH * t + 2 * g + 2)
                    e.tensor_tensor(Rs[par][:, c], Ra[:, c], ro[:, c], ALU.add).then_inc(l_R, 1)

            e.wait_ge(g_ready, 1)
            for t in range(CH):
                step(t, t % 2)

            e.memset(SH[:, 0, :], 0.0).then_inc(g_chain, 1)
            e.wait_ge(l_z, CH)
            e.tensor_tensor(h4(qeg), h4(qeg), Z[:, :, :, DH:2 * DH], ALU.subtract).then_inc(g_w, 1)
            e.wait_ge(g_Ui, 128)
            k = 1
            for n in range(NC1 - 1):
                S = SH[:, n, :]
                e.wait_ge(g_chain, k)
                e.tensor_tensor(sm.rearrange("p (e d i) -> p e d i", e=2, d=DH),
                                bc(Uk[:, n, 0:64].rearrange("p (o i d) -> p o d i", o=1, i=DH), [P, 2, DH, DH]),
                                bc(S.rearrange("p (e o i) -> p e o i", e=2, o=1), [P, 2, DH, DH]), ALU.mult)\
                 .then_inc(g_chain, 1)
                e.wait_ge(g_chain, k + 1)
                e.tensor_reduce(sr_, sm.rearrange("p (n i) -> p n i", i=DH), AX, ALU.add).then_inc(g_chain, 1)
                e.wait_ge(g_chain, k + 2)
                e.scalar_tensor_tensor(sv_, S, Uk[:, n, 64:65], sr_, ALU.mult, ALU.subtract).then_inc(g_chain, 1)
                e.wait_ge(g_chain, k + 3)
                e.tensor_tensor(SH[:, n + 1, :], sv_, Uv[:, n, :], ALU.add).then_inc(g_chain, 1)
                k += 4

            e.wait_ge(g_SL, 16 * LH)
            e.wait_ge(g_w, 1)
            for h in range(LH - 1):
                buf = oS[0].rearrange("p (t e d) -> p t e d", t=CH, e=DH)
                if h > 0:
                    e.wait_ge(g_om, 2 * h)
                e.tensor_tensor(buf, bc(qeg[:, :, h * DH:(h + 1) * DH].rearrange("p t (o d) -> p t o d", o=1), [P, CH, DH, DH]),
                                bc(SL[:, h, :].rearrange("p (o e d) -> p o e d", o=1, e=DH), [P, CH, DH, DH]),
                                ALU.mult).then_inc(g_om, 1)
                e.wait_ge(g_om, 2 * h + 1)
                e.tensor_reduce(og[:, :, h * DH:(h + 1) * DH], buf, AX, ALU.add).then_inc(g_om, 1)
            e.wait_ge(g_om, 2 * (LH - 1))
            e.wait_ge(g_os, 4)
            half = lambda c: slice(c * CH // 2, (c + 1) * CH // 2)
            for c in range(2):
                e.tensor_tensor(h4(og)[:, half(c)], h4(og)[:, half(c)], Z[:, half(c), :, 0:DH], ALU.add).then_inc(g_o, 1)
            for c in range(2):
                e.wait_ge(g_sqo, c + 1)
                e.tensor_reduce(rs[:, half(c), 0:LH], h4(qeg)[:, half(c)], AX, ALU.add).then_inc(g_om, 1)
            e.wait_ge(g_om, 8)
            e.tensor_scalar(ss[:, :, 0:LH], rs[:, :, 0:LH], 1.0 / DH, EPS_RMS, ALU.mult, ALU.add).then_inc(g_norm, 1)
            e.wait_ge(g_norm, 2)
            e.reciprocal(rs[:, :, 4:8], ss[:, :, 0:LH]).then_inc(g_om, 1)
            e.wait_ge(g_om, 9)
            e.wait_ge(g_gate, 3)
            e.tensor_tensor(h4(og), col(pr, 3 * LD), per_head(rs[:, :, 4:8]), ALU.mult).then_inc(g_norm, 1)
            e.wait_ge(g_norm, 3)
            e.transpose(oT.rearrange("p t l -> p (t l)"), og.rearrange("p t c -> p (t c)")).then_inc(g_oT, 1)
            for i, (mu, _) in enumerate(LERP):
                e.tensor_scalar(omu[:, i:i + 1], w(mu), -1.0, 1.0, ALU.mult, ALU.add).then_inc(h_omu, 1)
            e.wait_ge(h_omu, 2)
            e.wait_ge(h_pad, 1)
            for q in range(NQ):
                e.wait_ge(g_out, q + 1)
                xs = X[:, 4 * q:4 * q + 4, :]
                e.tensor_tensor(xs, PS[:, 6 + q % 2, :].rearrange("p (j d) -> p j d", j=4), xs, ALU.add).then_inc(x_upd, 1)
                ln_moments(e, 3, q)
                if q >= 1:
                    ln_scale(e, 3, q - 1)
                if q >= 2:
                    shift(e, q - 2)
            ln_scale(e, 3, NQ - 1)
            shift(e, NQ - 2)
            shift(e, NQ - 1)

        LERP = (("mur", xr), ("muk", xk))

        def own(e, q):
            e.wait_ge(ln_hT, 12 + q + 1)
            for mu, dst in LERP:
                e.activation(dst[:, q * SEG:(q + 1) * SEG], hslice(q), ACT.Copy, scale=w(mu)).then_inc(h_own, 1)

        def shift(e, q):
            b, o = divmod(q * SEG, T)
            cols = slice(q * SEG, (q + 1) * SEG)
            for i, (_, dst) in enumerate(LERP):
                e.wait_ge(h_own, 2 * q + i + 1)
                e.scalar_tensor_tensor(dst[:, cols], hT[:, b, PAD + o - 1:PAD + o - 1 + SEG], omu[:, i:i + 1],
                                       dst[:, cols], ALU.mult, ALU.add).then_inc(h_mix, 1)

        def mix_dve(e):
            for q in range(NQ + 1):
                if q < NQ:
                    e.wait_ge(h_rl, q + 1)
                    if q >= 2:
                        e.wait_ge(h_v, q - 1)
                    e.tensor_tensor(ka[q % 2], PS[:, q % 2, :], rl[q % 2], ALU.mult).then_inc(h_ka, 1)
                if q >= 1:
                    p_ = q - 1
                    e.wait_ge(h_v, p_ + 1)
                    e.wait_ge(h_sr, p_ + 1)
                    e.tensor_tensor(rv[p_ % 2], PS[:, 4 + p_ % 2, :], sgr[p_ % 2], ALU.mult).then_inc(h_rv, 1)
                    e.wait_ge(h_rv, p_ + 1)
                    xs = X[:, 4 * p_:4 * p_ + 4, :]
                    e.tensor_tensor(xs, rv[p_ % 2].rearrange("p (j d) -> p j d", j=4), xs, ALU.add).then_inc(h_x, 1)

        def mix_pe(e):
            for q in range(NQ + 1):
                if q < NQ:
                    e.wait_ge(h_mix, 2 * q + 2)
                    if q >= 2:
                        e.wait_ge(h_ka, q - 1)
                        e.wait_ge(h_sr, q - 1)
                    e.matmul(PS[:, q % 2, :], w("WkT2"), xk[:, q * SEG:(q + 1) * SEG], start=True, stop=True).then_inc(h_k, 1)
                    for i in range(4):
                        a = q * SEG + i * P
                        m = e.matmul(PS[:, 2 + q % 2, i * P:(i + 1) * P], xr[:, a:a + P], w("WrT"), start=True, stop=True,
                                     skip_group_check=True)
                    m.then_inc(h_r, 1)
                if q >= 1:
                    p_ = q - 1
                    e.wait_ge(h_ka, p_ + 1)
                    if p_ >= 2:
                        e.wait_ge(h_rv, p_ - 1)
                    for i in range(4):
                        m = e.matmul(PS[:, 4 + p_ % 2, i * P:(i + 1) * P], ka[p_ % 2][:, i * P:(i + 1) * P], w("WvT2"),
                                     start=True, stop=True, skip_group_check=True)
                    m.then_inc(h_v, 1)

        def mix_act(e):
            for q in range(NQ):
                e.wait_ge(h_k, q + 1)
                if q >= 2:
                    e.wait_ge(h_ka, q - 1)
                e.activation(rl[q % 2], PS[:, q % 2, :], ACT.Relu).then_inc(h_rl, 1)
                e.wait_ge(h_r, q + 1)
                if q >= 2:
                    e.wait_ge(h_rv, q - 1)
                e.activation(sgr[q % 2], PS[:, 2 + q % 2, :], ACT.Sigmoid).then_inc(h_sr, 1)

        TURN, PROJ = (6, 0), (7, 5)

        def turn64(e, bank, src, q):
            for i in range(4):
                for c in range(2):
                    for p in range(2):
                        r = slice(CH * p, CH * p + CH)
                        m = e.matmul(PS[r, bank, i * P + CH * c:i * P + CH * c + CH],
                                     src[r, 4 * q + i, CH * c:CH * c + CH], ident[r, CH * p:CH * p + CH],
                                     start=True, stop=True, skip_group_check=True)
            return m

        @block.sync
        def _(e):
            xv = x_dram.rearrange("b (t p) d -> p (b t) d", p=P)
            for q in range(NQ):
                e.dma_start(X[:, 4 * q:4 * q + 4, :], xv[:, 4 * q:4 * q + 4, :]).then_inc(x_in, 16)
            e.dma_start(C[:, :], c_dram).then_inc(c_in, 16)
            e.dma_start(W[:, :], w_dram).then_inc(w_in, 16)
            e.dma_start(wk5[:, 0:P], wk_dram).then_inc(w_in, 16)
            e.dma_start(wv5[:, 0:P], wv_dram).then_inc(w_in, 16)
            e.wait_ge(zeroed, 2)
            for s in range(NQ):
                e.wait_ge(b_qT, s + 1)
                if s >= 2:
                    e.wait_ge(c_S, 16 * (s - 1))
                for h in range(NH):
                    r = slice(DH * h, DH * h + DH)
                    e.dma_start(qbd[s % 2][r, h, :], qT[r, s * SEG:(s + 1) * SEG]).then_inc(c_qbd[s], 16)
            for s in range(NQ):
                e.wait_ge(b_qf, s + 1)
                if s < 2:
                    e.wait_ge(c_S, 16 * (s + 3))
                else:
                    e.wait_ge(d_S, 40 * (s - 1))
                for h in range(NH):
                    r = slice(DH * h, DH * h + DH)
                    e.dma_start(qbd[s % 2][r, h, :], qf[r, s * SEG:(s + 1) * SEG]).then_inc(d_qbd[s], 16)
            ov = out_dram.rearrange("b (t p) d -> p (b t) d", p=P)
            e.wait_ge(g_Uo, 2)
            uh, sh = (d.rearrange("(g h) n w -> h g n w", h=LH) for d in (u_dram, s_dram))
            for h in range(LH):
                e.dma_start(uh[h], Uo[:, h, :]).then_inc(g_Ud, 16)
            e.wait_ge(g_Ud, 16 * LH)
            e.wait_ge(l_z, CH)
            for r in range(4):
                rows_ = slice(32 * r, 32 * r + 32)
                e.dma_start(Uv[rows_, :, :], u_dram[:, :, ER * r:ER * r + ER]).then_inc(g_Ui, 16)
                e.dma_start(Uk[rows_, :, :], u_dram[:, :, 64:UW]).then_inc(g_Ui, 16)
            e.wait_ge(g_chain, 4 * (NC1 - 1) + 1)
            for r in range(4):
                e.dma_start(s_dram[:, :, ER * r:ER * r + ER], SH[32 * r:32 * r + 32, :, :]).then_inc(g_Sd, 16)
            e.wait_ge(g_Sd, 64)
            for h in range(LH):
                e.dma_start(SL[:, h, :], sh[h]).then_inc(g_SL, 16)
            for q in range(NQ):
                e.wait_ge(h_x, q + 1)
                e.dma_start(ov[:, 4 * q:4 * q + 4, :], X[:, 4 * q:4 * q + 4, :]).then_inc(y_out, 16)
            e.wait_ge(y_out, 16 * NQ)

        @block.gpsimd
        def _(e):
            e.memset(qbd[0], 0.0).then_inc(zeroed, 1)
            e.memset(qbd[1], 0.0).then_inc(zeroed, 1)
            e.memset(hT[:, :, 0:PAD], 0.0).then_inc(zeroed, 1)
            e.memset(klT[:, :, 0:PAD], 0.0).then_inc(b_klT_pad, 1)
            e.memset(v9l[:, :, :, DH:DE], 1.0).then_inc(b_klT_pad, 1)
            e.wait_ge(c_in, 16)
            e.wait_ge(w_in, 48)
            e.wait_ge(ln_h, NT)
            e.tensor_tensor(X[:, :, :], X[:, :, :], w("bo").rearrange("p (o d) -> p o d", o=1).to_broadcast([P, NT, P]),
                            ALU.add).then_inc(xbo, 1)
            for q in range(NQ):
                e.wait_ge(b_qe, q + 1)
                e.tensor_scalar(qf[:, q * SEG:(q + 1) * SEG], qf[:, q * SEG:(q + 1) * SEG], 1.0, None,
                                ALU.min).then_inc(b_qm, 1)
            e.wait_ge(c_loc, NT)
            for par in range(2):
                e.memset(V9[par], 0.0).then_inc(v9_zero, 1)
                if par == 0:
                    e.memset(SB[:, 0, :, :], 0.0).then_inc(zeroed, 1)
                e.wait_ge(v9_zero, par + 1)
                e.tensor_copy(V9[par].rearrange("p c l (h e) -> p c (l h) e", e=DE)[:, :, :, DH],
                              cst("half").rearrange("p (c o) -> p c o", o=1).to_broadcast([P, 2, LV * NH]))\
                 .then_inc(v9_ones, 1)
            for q in range(NQ):
                e.wait_ge(d_glob, 4 * q + 4)
                e.wait_ge(d_av, 10 * NT)
                e.tensor_tensor(diff[:, 4 * q:4 * q + 4, :], loc[:, 4 * q:4 * q + 4, :], glob[:, 4 * q:4 * q + 4, :],
                                ALU.subtract).then_inc(e_diff, 1)
            e.wait_ge(x_upd, 8)
            delta_pool(e)

        @block.scalar
        def _(e):
            e.wait_ge(c_in, 16)
            e.activation(identb[:, :], ident, ACT.Copy).then_inc(cb_ready, 1)
            e.activation(nmaskb[:, 0, :], cst("nmask0"), ACT.Copy).then_inc(cb_ready, 1)
            e.activation(nmaskb[:, 1, :], cst("nmask"), ACT.Copy).then_inc(cb_ready, 1)
            for q in range(NQ):
                ln_root(e, 0, q)
            for q in range(NQ):
                ln_store(e, 0, q)
            for q in range(NQ):
                e.wait_ge(b_q, q + 1)
                cols = slice(q * SEG, (q + 1) * SEG)
                e.activation(qT[:, cols], PS[:, 2 + q, :], ACT.Copy).then_inc(b_qT, 1)
                e.activation(qf[:, cols], PS[:, 2 + q, :], ACT.Exp).then_inc(b_qe, 1)
            for q in range(NQ):
                e.wait_ge(b_kl, q + 1)
                b, o = divmod(q * SEG, T)
                e.activation(klT[:, b, PAD + o:PAD + o + SEG], PS[:, 6 + q % 2, :], ACT.Copy).then_inc(b_klT, 1)
            for i in range(8):
                e.wait_ge(b_vl, i + 1)
                if i == 0:
                    e.wait_ge(b_klT_pad, 2)
                e.activation(v9l[:, 4 * i:4 * i + 4, :, 0:DH].rearrange("p w h e -> p (w h) e"),
                             PS[:, i % 2, :].rearrange("p (h e) -> p h e", e=DH), ACT.Copy).then_inc(b_v9, 1)
            e.wait_ge(b_sw, 2)
            e.activation(hsw[:, 8:12], hsw[:, 4:8], ACT.Exp).then_inc(b_sw, 1)
            local_act(e)
            for i, t in enumerate((wk5, wv5)):
                e.wait_ge(b_comb, i + 1)
                e.activation(t[:, P:LV * P], PS[:, (7, 0)[i], :], ACT.Copy).then_inc(b_w5, 1)
            e.wait_ge(c_loc, NT)
            for j in range(NT):
                if j < 2:
                    e.wait_ge(v9_ones, j + 1)
                prep_act(e, j)
            e.wait_ge(d_glob, NT)
            for q in range(NQ + 1):
                if q < NQ:
                    e.wait_ge(e_dT, q + 1)
                    if q >= 2:
                        e.wait_ge(e_g, q - 1)
                    e.activation(dT[q % 2], PS[:, q % 2, :], ACT.Copy).then_inc(e_dTs, 1)
                if q >= 1:
                    e.wait_ge(e_g, q)
                    if q >= 3:
                        e.wait_ge(e_al, q - 2)
                    e.activation(gh[(q - 1) % 2], PS[:, 2 + (q - 1) % 2, :], ACT.Silu, bias=w("bg")).then_inc(e_gh, 1)
            e.wait_ge(e_al, NQ)
            e.activation(alpha, PS[:, 4, 0:2 * NT], ACT.Sigmoid, bias=w("bgo")).then_inc(e_alpha, 1)
            for q in range(NQ + 1):
                if q < NQ:
                    e.wait_ge(e_mT, q + 1)
                    if q >= 2:
                        e.wait_ge(e_out, q - 1)
                    e.activation(mixT[q % 2], PS[:, TURN[q % 2], :], ACT.Copy).then_inc(e_mTs, 1)
                if q >= 1:
                    ln_root(e, 1, q - 1)
                if q >= 2:
                    ln_store(e, 1, q - 2)
            ln_store(e, 1, NQ - 1)
            moe_act(e)
            delta_act(e)
            mix_act(e)

        @block.tensor
        def _(e):
            e.wait_ge(cb_ready, 3)
            keep_warm(e, 4, 6)
            for q in range(NQ):
                ln_turn(e, 0, q)
                keep_warm(e, 4, 5)
            e.wait_ge(w_in, 48)
            e.wait_ge(zeroed, 3)
            e.wait_ge(ln_hT, 4)
            for q in range(NQ):
                e.matmul(PS[:, 2 + q, :], w("WqT"), hslice(q), start=True, stop=True).then_inc(b_q, 1)
            for q in range(NQ):
                if q >= 2:
                    e.wait_ge(b_klT, q - 1)
                e.matmul(PS[:, 6 + q % 2, :], w("WklT"), hslice(q), start=True, stop=True).then_inc(b_kl, 1)
            for i in range(8):
                if i >= 2:
                    e.wait_ge(b_v9, i - 1)
                for k in range(4):
                    b, c = divmod(4 * i + k, NC1)
                    m = e.matmul(PS[:, i % 2, k * P:(k + 1) * P], hT[:, b, CH * c:CH * c + P], w("WvlT"),
                                 start=True, stop=True, skip_group_check=True)
                m.then_inc(b_vl, 1)
            e.wait_ge(b_qf, NQ)
            local_pe(e)
            linear_pe(e)
            keep_warm(e, 0, 20)
            e.wait_ge(d_glob, NT)
            for q in range(NQ + 2):
                if q < NQ:
                    e.wait_ge(e_diff, q + 1)
                    if q >= 2:
                        e.wait_ge(e_dTs, q - 1)
                    turn64(e, q % 2, diff, q).then_inc(e_dT, 1)
                if 1 <= q <= NQ:
                    g = q - 1
                    e.wait_ge(e_dTs, g + 1)
                    if g >= 2:
                        e.wait_ge(e_gh, g - 1)
                    e.matmul(PS[:, 2 + g % 2, :], w("WgTa"), hslice(g), start=True, stop=False)
                    e.matmul(PS[:, 2 + g % 2, :], w("WgTb"), dT[g % 2], start=False, stop=True).then_inc(e_g, 1)
                if q >= 2:
                    g = q - 2
                    e.wait_ge(e_gh, g + 1)
                    for i in range(8):
                        for p in range(2):
                            m = e.matmul(PS[CH * p:CH * p + CH, 4, 8 * g + i:8 * g + i + 1],
                                         gh[g % 2][:, i * CH:(i + 1) * CH], w("WgoT"),
                                         start=True, stop=True, skip_group_check=True)
                    m.then_inc(e_al, 1)
            e.wait_ge(e_mix, 8)
            turn64(e, TURN[0], mix, 0).then_inc(e_mT, 1)
            for q in range(NQ):
                if q + 1 < NQ:
                    e.wait_ge(e_mix, 8 * q + 16)
                    if q >= 1:
                        e.wait_ge(e_mTs, q)
                    turn64(e, TURN[(q + 1) % 2], mix, q + 1).then_inc(e_mT, 1)
                e.wait_ge(e_mTs, q + 1)
                if q >= 2:
                    e.wait_ge(x_upd, q - 1)
                for i in range(4):
                    m = e.matmul(PS[:, PROJ[q % 2], i * P:(i + 1) * P], mixT[q % 2][:, i * P:(i + 1) * P], w("WoT"),
                                 start=True, stop=True, skip_group_check=True)
                m.then_inc(e_out, 1)
                if q >= 1:
                    ln_turn(e, 1, q - 1)
            ln_turn(e, 1, NQ - 1)
            moe_pe(e)
            delta_pe(e)
            mix_pe(e)

        @block.vector
        def _(e):
            ln_moments(e, 0, 0)
            for q in range(NQ):
                if q + 1 < NQ:
                    ln_moments(e, 0, q + 1)
                ln_scale(e, 0, q)
            e.wait_ge(w_in, 48)
            hs = w("hscale")
            e.tensor_reduce(hsw[:, 16:17], hs, AX, ALU.max).then_inc(b_sw, 1)
            e.wait_ge(b_sw, 1)
            e.tensor_scalar(hsw[:, 4:8], hs, hsw[:, 16:17], None, ALU.subtract).then_inc(b_sw, 1)
            for q in range(NQ):
                e.wait_ge(b_qm, q + 1)
                cols = slice(q * SEG, (q + 1) * SEG)
                e.scalar_tensor_tensor(qf[:, cols], PS[:, 2 + q, :], 1.0, qf[:, cols], ALU.add, ALU.max).then_inc(b_qf, 1)
            e.wait_ge(b_sw, 3)
            e.tensor_reduce(hsw[:, 17:18], hsw[:, 8:12], AX, ALU.add).then_inc(b_sw, 1)
            e.wait_ge(b_sw, 4)
            e.reciprocal(hsw[:, 18:19], hsw[:, 17:18]).then_inc(b_sw, 1)
            e.memset(hsw[:, 0:1], 1.0).then_inc(b_sw, 1)
            e.wait_ge(b_sw, 6)
            e.tensor_scalar(hsw[:, 1:5], hsw[:, 8:12], hsw[:, 18:19], None, ALU.mult).then_inc(b_sw, 1)
            e.wait_ge(b_sw, 7)
            local_dve(e)
            linear_dve(e)
            e.wait_ge(e_alpha, 1)
            for q in range(NQ):
                for i in range(8):
                    j, cols = 4 * q + i // 2, slice(CH * (i % 2), CH * (i % 2) + CH)
                    e.scalar_tensor_tensor(mix[:, j, cols], diff[:, j, cols], alpha[:, 8 * q + i:8 * q + i + 1],
                                           glob[:, j, cols], ALU.mult, ALU.add).then_inc(e_mix, 1)
            e.wait_ge(xbo, 1)
            for q in range(NQ):
                e.wait_ge(e_out, q + 1)
                xs = X[:, 4 * q:4 * q + 4, :]
                e.tensor_tensor(xs, PS[:, PROJ[q % 2], :].rearrange("p (j d) -> p j d", j=4), xs, ALU.add).then_inc(x_upd, 1)
                ln_moments(e, 1, q)
                ln_scale(e, 1, q)
            moe_dve(e)
            delta_dve(e)
            mix_dve(e)


def kernel(**inputs):
    import numpy as np
    import concourse.bacc as _bacc
    from concourse.bass_utils import run_bass_kernel_spmd as _run

    g = {k: np.ascontiguousarray(v) for k, v in inputs.items()}
    f4 = np.float32

    def bd(wl):
        out = np.zeros((NH, DH, 4, NH, DH), f4)
        for h in range(NH):
            out[h, :, :, h, :] = wl.transpose(2, 0, 1)
        return out.reshape(P, 512)

    def rows(v):
        return np.broadcast_to(v.reshape(1, -1), (P, v.size))

    def lanes(v):
        return np.repeat(v.reshape(4, LH), 32, axis=0)

    def split(wt):
        return wt.reshape(NH // 2, 2, DH, P).transpose(1, 0, 2, 3).reshape(P, P)

    a, f = "L0_attn_", "L0_ffn_"
    parts = {
        "WqT": g[a + "Wq"].T, "WklT": g[a + "Wkl"].T, "WvlT": g[a + "Wvl"].T, "Wk": g[a + "Wk"], "Wv": g[a + "Wv"],
        "HBk": bd(g[a + "haar_Wk"]), "HBv": bd(g[a + "haar_Wv"]), "hscale": rows(g[a + "haar_scale"]),
        "bo": rows(g[a + "bo"]), "WgTa": g[a + "Wg"].T[:P], "WgTb": split(g[a + "Wg"].T[P:]), "WgoT": g[a + "Wgo"].T,
        "bg": g[a + "bg"].reshape(P, 1), "bgo": rows(g[a + "bgo"]), "WoT": split(g[a + "Wo"].T),
        "gateT": g[f + "gate_w"].T, "cbias": rows(g[f + "correction_bias"]),
        "Eg": np.concatenate([g[f + "Wg"].transpose(1, 0, 2).reshape(P, 512), g[f + "Wg_s"]], 1),
        "Eu": np.concatenate([g[f + "Wu"].transpose(1, 0, 2).reshape(P, 512), g[f + "Wu_s"]], 1),
        "Ed": g[f + "Wd"].reshape(4, P, P).transpose(1, 0, 2).reshape(P, 512),
        "Eds": np.concatenate([g[f + "Wd_s"], np.zeros((64, P), f4)], 0),
        "dtb": lanes(g["L1_attn_dt_bias"]), "Alog": lanes(g["L1_attn_A_log"]), "normw": rows(g["L1_attn_norm_w"]),
        "L1Wo": g["L1_attn_Wo"],
        "WrT": g["L1_ffn_W_r"].T, "WkT2": g["L1_ffn_W_k"].T, "WvT2": g["L1_ffn_W_v"].T,
        "mur": g["L1_ffn_mu_r"].reshape(P, 1), "muk": g["L1_ffn_mu_k"].reshape(P, 1),
    }
    b = "L1_attn_"
    parts["L1W"] = np.concatenate(
        [np.concatenate([g[b + n][:, 32 * j:32 * j + 32] for n in ("Wq", "Wk", "Wv", "Wg")]
                        + [g[b + n][:, 4 * j:4 * j + 4] for n in ("Wb", "Wa")], 1) for j in range(4)], 1)
    wpack = np.concatenate([parts[n] for n, _ in W_PARTS], 1)

    s, t = np.arange(P)[:, None], np.arange(P)[None, :]
    mean = np.zeros((P, LV - 1, P), f4)
    for i, blk in enumerate((2, 4, 8, 16)):
        mean[:, i, :] = np.where((s // blk == t // blk) & (s <= t), 1.0 / (t % blk + 1), 0.0)
    qq = s % CH
    ok = (t <= qq + CH) & (t > qq)
    consts = {
        "ident": np.eye(P, dtype=f4), "mean": mean.reshape(P, -1),
        "tri": (qq <= np.arange(CH)[None, :]).astype(f4),
        "hmask": (s // DH == np.arange(NH)[None, :]).astype(f4),
        "nmask": np.where(ok, 0.0, -1e30).astype(f4),
        "low4": rows(np.tril(np.ones((4, 4), f4), -1)), "low8": rows(np.tril(np.ones((NE, NE), f4), -1)),
        "half": (s // CH == np.arange(2)[None, :]).astype(f4),
        "nmask0": np.where(ok & ((s >= CH) | (t >= CH)), 0.0, -1e30).astype(f4),
    }
    cpack = np.concatenate([consts[n] for n, _ in C_PARTS], 1).astype(f4)

    nc = _bacc.Bacc("TRN2", target_bir_lowering=False, num_devices=1)
    arrays = {"x": g["L0_attn_x"], "wpack": np.ascontiguousarray(wpack), "wkT": np.ascontiguousarray(g[a + "Wk"].T),
              "wvT": np.ascontiguousarray(g[a + "Wv"].T), "cpack": np.ascontiguousarray(cpack)}
    dram = {n: nc.dram_tensor(n, v.shape, F32, kind="ExternalInput").ap() for n, v in arrays.items()}
    out = nc.dram_tensor("out", (NB, T, P), F32, kind="ExternalOutput").ap()
    u = nc.dram_tensor("carry_out", (32, NC1, 2 * DH * DH + 1), F32).ap()
    sd = nc.dram_tensor("carry_in", (32, NC1, DH * DH), F32).ap()
    program(nc, dram["x"], dram["wpack"], dram["wkT"], dram["wvT"], dram["cpack"], out, u, sd)
    return _run(nc, [arrays], core_ids=[0]).results[0]["out"]
```
